# Optimizing a Trainium2 kernel written in Bass

```python
import numpy as np
import jax
import jax.numpy as jnp

def _softmax(x, axis=-1):
    return jax.nn.softmax(x, axis=axis)

def _gelu(x):
    return jax.nn.gelu(x, approximate=True)

def _silu(x):
    return jax.nn.silu(x)

def _sigmoid(x):
    return jax.nn.sigmoid(x)

def _layernorm(x, axis=-1, eps=1e-05):
    m = jnp.mean(x, axis=axis, keepdims=True)
    v = jnp.var(x, axis=axis, keepdims=True)
    return (x - m) / jnp.sqrt(v + eps)

def _scatter_add(tgt, idx, src, axis=0):
    return tgt.at[idx].add(src)

def _segment_sum(src, seg, n):
    return jax.ops.segment_sum(src, seg, n)
kernel_name = 'mk_seq_postln_d2_jaxref_r8_7fea7b'

def setup_inputs(seed: int=0):
    np.random.seed(seed)
    _w = jnp.asarray

    def _L0_attn_setup():
        import jax, jax.numpy as jnp
        import numpy as np
        import math
        B = 2
        D_MODEL = 256
        L_MAX = 512
        FILTER_ORDER = 64
        EMB_DIM = 3
        SHORT_K = 3

        def _pos_emb(L):
            t = jnp.linspace(0.0, 1.0, L)[:, None]
            t_resc = jnp.linspace(0.0, L - 1.0, L)
            w = 2.0 * math.pi * t_resc / L
            bands = (EMB_DIM - 1) // 2
            f = jnp.linspace(0.0001, bands - 1.0, bands)
            ang = f[None, :] * w[:, None]
            z = jnp.concatenate([t, jnp.cos(ang), -jnp.sin(ang)], axis=-1)
            return (z, t)

        def _filter_k(L, w0, b0, freq, w1, b1, w2, b2, w3):
            z, t = _pos_emb(L)
            h = jnp.sin(freq * (z @ w0.T + b0))
            h = jnp.sin(freq * (h @ w1.T + b1))
            h = jnp.sin(freq * (h @ w2.T + b2))
            h = h @ w3.T
            max_decay = math.log(0.01) / 0.3
            min_decay = math.log(0.01) / 1.5
            deltas = jnp.linspace(min_decay, max_decay, h.shape[-1])
            decay = jnp.exp(-t * jnp.abs(deltas)[None, :])
            return (h * decay).T

        def _fftconv(u, k, bias):
            L = u.shape[-1]
            n = 2 * L
            k_f = jnp.fft.rfft(k, n=n) / n
            u_f = jnp.fft.rfft(u, n=n)
            y = jnp.fft.irfft(u_f * k_f, n=n, norm='forward')[..., :L]
            return y + u * bias[:, None]
        key = jax.random.key(seed)
        ks = jax.random.split(key, 16)
        D = D_MODEL

        def n(k, shape, scale=0.02):
            return jax.random.normal(k, shape, dtype=jnp.float32) * scale
        return {'x': jax.random.normal(ks[0], (B, L_MAX, D), dtype=jnp.float32), 'in_proj_w': n(ks[1], (3 * D, D)), 'in_proj_b': n(ks[2], (3 * D,)), 'short_w': n(ks[3], (3 * D, 1, SHORT_K), 0.3), 'short_b': n(ks[4], (3 * D,), 0.1), 'mlp_w0': n(ks[5], (FILTER_ORDER, EMB_DIM), 0.5), 'mlp_b0': n(ks[6], (FILTER_ORDER,), 0.5), 'sin_freq': jnp.ones((1, FILTER_ORDER), dtype=jnp.float32), 'mlp_w1': n(ks[7], (FILTER_ORDER, FILTER_ORDER), 0.1), 'mlp_b1': n(ks[8], (FILTER_ORDER,), 0.1), 'mlp_w2': n(ks[9], (FILTER_ORDER, FILTER_ORDER), 0.1), 'mlp_b2': n(ks[10], (FILTER_ORDER,), 0.1), 'mlp_w3': n(ks[11], (D, FILTER_ORDER), 0.1), 'filter_bias': jax.random.normal(ks[12], (D,), dtype=jnp.float32), 'out_proj_w': n(ks[13], (D, D)), 'out_proj_b': n(ks[14], (D,))}
    _L0_attn_in = _L0_attn_setup()

    def _L0_ffn_setup():
        import jax, jax.numpy as jnp
        import numpy as np
        B, S, D, H = (4, 256, 256, 1024)

        def fwht(x):
            orig_shape = x.shape
            n = orig_shape[-1]
            x = x.reshape(-1, n)
            h = 1
            while h < n:
                xb = x.reshape(-1, n // (2 * h), 2, h)
                a = xb[:, :, 0, :]
                b = xb[:, :, 1, :]
                x = jnp.stack([a + b, a - b], axis=2).reshape(-1, n)
                h *= 2
            scale = jnp.asarray(1.0 / np.sqrt(n), dtype=x.dtype)
            return (x * scale).reshape(orig_shape)
        key = jax.random.key(seed)
        kx, k1, k2, k3 = jax.random.split(key, 4)
        x = jax.random.normal(kx, (B, S, D), dtype=jnp.float32)
        W1 = jax.random.normal(k1, (H, D), dtype=jnp.float32) * (1.0 / np.sqrt(D))
        W2 = jax.random.normal(k2, (D, H), dtype=jnp.float32) * (1.0 / np.sqrt(H))
        W3 = jax.random.normal(k3, (H, D), dtype=jnp.float32) * (1.0 / np.sqrt(D))
        return {'x': x, 'W1': W1, 'W2': W2, 'W3': W3}
    _L0_ffn_in = _L0_ffn_setup()

    def _L1_attn_setup():
        import jax, jax.numpy as jnp
        import numpy as np
        EPS = 1.1920929e-07
        HQ, HKV = (16, 4)
        WIN = 32

        def rmsnorm(x):
            return x * jax.lax.rsqrt(jnp.mean(x * x, axis=-1, keepdims=True) + EPS)
        key = jax.random.key(seed)
        ks = jax.random.split(key, 5)
        B, T, C = (2, 256, 256)
        Dh = C // HQ
        s = 0.02
        x = jax.random.normal(ks[0], (B, T, C), jnp.float32)
        Wq = jax.random.normal(ks[1], (C, HQ * Dh), jnp.float32) * s
        Wk = jax.random.normal(ks[2], (C, HKV * Dh), jnp.float32) * s
        Wv = jax.random.normal(ks[3], (C, HKV * Dh), jnp.float32) * s
        Wo = jax.random.normal(ks[4], (C, C), jnp.float32) * s
        return {'x': x, 'Wq': Wq, 'Wk': Wk, 'Wv': Wv, 'Wo': Wo}
    _L1_attn_in = _L1_attn_setup()

    def _L1_ffn_setup():
        import jax, jax.numpy as jnp
        import numpy as np
        TOPK = 6
        CAP = 128
        ROUTE_SCALE = 1.0
        key = jax.random.key(seed)
        k = jax.random.split(key, 6)
        B, T, C = (2, 256, 256)
        E, H, HS = (64, 32, 64)
        std = 0.01
        return {'x': jax.random.normal(k[0], (B, T, C), jnp.float32), 'w_gate': jax.random.normal(k[1], (C, E), jnp.float32) * std, 'w_shared_up': jax.random.normal(k[2], (C, 2 * HS), jnp.float32) * std, 'w_shared_down': jax.random.normal(k[3], (HS, C), jnp.float32) * std, 'w_up': jax.random.normal(k[4], (E, C, 2 * H), jnp.float32) * std, 'w_down': jax.random.normal(k[5], (E, H, C), jnp.float32) * std}
    _L1_ffn_in = _L1_ffn_setup()
    _d = {'L0_attn_x': _L0_attn_in['x'], 'L0_attn_in_proj_w': _L0_attn_in['in_proj_w'], 'L0_attn_in_proj_b': _L0_attn_in['in_proj_b'], 'L0_attn_short_w': _L0_attn_in['short_w'], 'L0_attn_short_b': _L0_attn_in['short_b'], 'L0_attn_mlp_w0': _L0_attn_in['mlp_w0'], 'L0_attn_mlp_b0': _L0_attn_in['mlp_b0'], 'L0_attn_sin_freq': _L0_attn_in['sin_freq'], 'L0_attn_mlp_w1': _L0_attn_in['mlp_w1'], 'L0_attn_mlp_b1': _L0_attn_in['mlp_b1'], 'L0_attn_mlp_w2': _L0_attn_in['mlp_w2'], 'L0_attn_mlp_b2': _L0_attn_in['mlp_b2'], 'L0_attn_mlp_w3': _L0_attn_in['mlp_w3'], 'L0_attn_filter_bias': _L0_attn_in['filter_bias'], 'L0_attn_out_proj_w': _L0_attn_in['out_proj_w'], 'L0_attn_out_proj_b': _L0_attn_in['out_proj_b'], 'L0_ffn_W1': _L0_ffn_in['W1'], 'L0_ffn_W2': _L0_ffn_in['W2'], 'L0_ffn_W3': _L0_ffn_in['W3'], 'L1_attn_Wq': _L1_attn_in['Wq'], 'L1_attn_Wk': _L1_attn_in['Wk'], 'L1_attn_Wv': _L1_attn_in['Wv'], 'L1_attn_Wo': _L1_attn_in['Wo'], 'L1_ffn_w_gate': _L1_ffn_in['w_gate'], 'L1_ffn_w_shared_up': _L1_ffn_in['w_shared_up'], 'L1_ffn_w_shared_down': _L1_ffn_in['w_shared_down'], 'L1_ffn_w_up': _L1_ffn_in['w_up'], 'L1_ffn_w_down': _L1_ffn_in['w_down']}
    _x0 = _d['L0_attn_x']
    _d['L0_attn_x'] = jax.random.normal(jax.random.fold_in(jax.random.key(seed), 1), (8, 256, 256), dtype=_x0.dtype)
    del _x0
    return _d

def reference(L0_attn_x, L0_attn_in_proj_w, L0_attn_in_proj_b, L0_attn_short_w, L0_attn_short_b, L0_attn_mlp_w0, L0_attn_mlp_b0, L0_attn_sin_freq, L0_attn_mlp_w1, L0_attn_mlp_b1, L0_attn_mlp_w2, L0_attn_mlp_b2, L0_attn_mlp_w3, L0_attn_filter_bias, L0_attn_out_proj_w, L0_attn_out_proj_b, L0_ffn_W1, L0_ffn_W2, L0_ffn_W3, L1_attn_Wq, L1_attn_Wk, L1_attn_Wv, L1_attn_Wo, L1_ffn_w_gate, L1_ffn_w_shared_up, L1_ffn_w_shared_down, L1_ffn_w_up, L1_ffn_w_down):

    def _L0_attn_ref(x, in_proj_w, in_proj_b, short_w, short_b, mlp_w0, mlp_b0, sin_freq, mlp_w1, mlp_b1, mlp_w2, mlp_b2, mlp_w3, filter_bias, out_proj_w, out_proj_b):
        import jax, jax.numpy as jnp
        import numpy as np
        import math
        B = 2
        D_MODEL = 256
        L_MAX = 512
        FILTER_ORDER = 64
        EMB_DIM = 3
        SHORT_K = 3

        def _pos_emb(L):
            t = jnp.linspace(0.0, 1.0, L)[:, None]
            t_resc = jnp.linspace(0.0, L - 1.0, L)
            w = 2.0 * math.pi * t_resc / L
            bands = (EMB_DIM - 1) // 2
            f = jnp.linspace(0.0001, bands - 1.0, bands)
            ang = f[None, :] * w[:, None]
            z = jnp.concatenate([t, jnp.cos(ang), -jnp.sin(ang)], axis=-1)
            return (z, t)

        def _filter_k(L, w0, b0, freq, w1, b1, w2, b2, w3):
            z, t = _pos_emb(L)
            h = jnp.sin(freq * (z @ w0.T + b0))
            h = jnp.sin(freq * (h @ w1.T + b1))
            h = jnp.sin(freq * (h @ w2.T + b2))
            h = h @ w3.T
            max_decay = math.log(0.01) / 0.3
            min_decay = math.log(0.01) / 1.5
            deltas = jnp.linspace(min_decay, max_decay, h.shape[-1])
            decay = jnp.exp(-t * jnp.abs(deltas)[None, :])
            return (h * decay).T

        def _fftconv(u, k, bias):
            L = u.shape[-1]
            n = 2 * L
            k_f = jnp.fft.rfft(k, n=n) / n
            u_f = jnp.fft.rfft(u, n=n)
            y = jnp.fft.irfft(u_f * k_f, n=n, norm='forward')[..., :L]
            return y + u * bias[:, None]
        Bn, L, D = x.shape
        u = x @ in_proj_w.T + in_proj_b
        u = jnp.transpose(u, (0, 2, 1))
        uc = jax.lax.conv_general_dilated(u, short_w, window_strides=(1,), padding=[(SHORT_K - 1, SHORT_K - 1)], feature_group_count=3 * D, dimension_numbers=('NCH', 'OIH', 'NCH'))
        uc = uc[..., :L] + short_b[None, :, None]
        x0, x1, v = jnp.split(uc, 3, axis=1)
        k = _filter_k(L, mlp_w0, mlp_b0, sin_freq, mlp_w1, mlp_b1, mlp_w2, mlp_b2, mlp_w3)
        v = v * x1
        v = _fftconv(v, k, filter_bias)
        y = v * x0
        y = jnp.transpose(y, (0, 2, 1))
        return y @ out_proj_w.T + out_proj_b

    def _L0_ffn_ref(x, W1, W2, W3):
        import jax, jax.numpy as jnp
        import numpy as np
        B, S, D, H = (4, 256, 256, 1024)

        def fwht(x):
            orig_shape = x.shape
            n = orig_shape[-1]
            x = x.reshape(-1, n)
            h = 1
            while h < n:
                xb = x.reshape(-1, n // (2 * h), 2, h)
                a = xb[:, :, 0, :]
                b = xb[:, :, 1, :]
                x = jnp.stack([a + b, a - b], axis=2).reshape(-1, n)
                h *= 2
            scale = jnp.asarray(1.0 / np.sqrt(n), dtype=x.dtype)
            return (x * scale).reshape(orig_shape)
        up_gate = jnp.einsum('bsd,hd->bsh', x, W1)
        up_lin = jnp.einsum('bsd,hd->bsh', x, W3)
        hidden = jax.nn.silu(up_gate) * up_lin
        hidden = fwht(hidden)
        out = jnp.einsum('bsh,dh->bsd', hidden, W2)
        return out

    def _L1_attn_ref(x, Wq, Wk, Wv, Wo):
        import jax, jax.numpy as jnp
        import numpy as np
        EPS = 1.1920929e-07
        HQ, HKV = (16, 4)
        WIN = 32

        def rmsnorm(x):
            return x * jax.lax.rsqrt(jnp.mean(x * x, axis=-1, keepdims=True) + EPS)
        B, T, C = x.shape
        Dh = C // HQ
        g = HQ // HKV
        Q = (x @ Wq).reshape(B, T, HQ, Dh).transpose(0, 2, 1, 3)
        V = (x @ Wv).reshape(B, T, HKV, Dh).transpose(0, 2, 1, 3)
        _K_unused = x @ Wk
        Q = rmsnorm(Q)
        K = rmsnorm(V)
        Q = Q.reshape(B, HKV, g, T, Dh)
        scores = jnp.einsum('bhgtd,bhsd->bhgts', Q, K)
        i = jnp.arange(T)[:, None]
        j = jnp.arange(T)[None, :]
        mask = (j > i) & (j <= i - WIN)
        scores = jnp.where(mask, -jnp.inf, scores)
        p = jax.nn.softmax(scores, axis=-1)
        y = jnp.einsum('bhgts,bhsd->bhgtd', p, V)
        y = y.reshape(B, HQ, T, Dh).transpose(0, 2, 1, 3).reshape(B, T, C)
        return rmsnorm(y @ Wo)

    def _L1_ffn_ref(x, w_gate, w_shared_up, w_shared_down, w_up, w_down):
        import jax, jax.numpy as jnp
        import numpy as np
        TOPK = 6
        CAP = 128
        ROUTE_SCALE = 1.0
        B, T, C = x.shape
        E = w_gate.shape[1]
        x_flat = x.reshape(-1, C)
        N = x_flat.shape[0]
        su = x_flat @ w_shared_up
        y_s, g_s = jnp.split(su, 2, axis=-1)
        shared = jax.nn.silu(g_s) * y_s @ w_shared_down
        scores = jax.nn.sigmoid(x_flat @ w_gate)
        _, topk_idx = jax.lax.top_k(scores, TOPK)
        w = jnp.take_along_axis(scores, topk_idx, axis=-1)
        w = w / w.sum(-1, keepdims=True) * ROUTE_SCALE
        flat_e = topk_idx.reshape(-1)
        oh = jax.nn.one_hot(flat_e, E, dtype=jnp.int32)
        pos = jnp.take_along_axis(jnp.cumsum(oh, axis=0), flat_e[:, None], axis=1)[:, 0] - 1
        valid = pos < CAP
        pos_c = jnp.where(valid, pos, CAP - 1)
        token_ids = jnp.repeat(jnp.arange(N), TOPK)
        x_disp = jnp.zeros((E, CAP, C), x.dtype).at[flat_e, pos].set(x_flat[token_ids], mode='drop')
        up = jnp.einsum('ecd,edh->ech', x_disp, w_up)
        g_r, v_r = jnp.split(up, 2, axis=-1)
        h_r = jax.nn.silu(g_r) * v_r
        out_r = jnp.einsum('ech,ehd->ecd', h_r, w_down)
        y_ts = out_r[flat_e, pos_c]
        y_ts = jnp.where(valid[:, None], y_ts, 0.0)
        routed = (y_ts.reshape(N, TOPK, C) * w[:, :, None]).sum(axis=1)
        return (shared + routed).reshape(B, T, C)
    x = L0_attn_x
    x = _layernorm(x + _L0_attn_ref(x, L0_attn_in_proj_w, L0_attn_in_proj_b, L0_attn_short_w, L0_attn_short_b, L0_attn_mlp_w0, L0_attn_mlp_b0, L0_attn_sin_freq, L0_attn_mlp_w1, L0_attn_mlp_b1, L0_attn_mlp_w2, L0_attn_mlp_b2, L0_attn_mlp_w3, L0_attn_filter_bias, L0_attn_out_proj_w, L0_attn_out_proj_b), axis=-1)
    x = _layernorm(x + _L0_ffn_ref(x, L0_ffn_W1, L0_ffn_W2, L0_ffn_W3), axis=-1)
    x = _layernorm(x + _L1_attn_ref(x, L1_attn_Wq, L1_attn_Wk, L1_attn_Wv, L1_attn_Wo), axis=-1)
    x = _layernorm(x + _L1_ffn_ref(x, L1_ffn_w_gate, L1_ffn_w_shared_up, L1_ffn_w_shared_down, L1_ffn_w_up, L1_ffn_w_down), axis=-1)
    return x

_drawn_inputs = setup_inputs


def setup_inputs(seed=0):
    import zlib

    import numpy as np

    out = dict(_drawn_inputs(seed))
    spreads = {'L0_attn_sin_freq': (1.0, 0.6)}
    factors = {'L0_attn_in_proj_w': 4.815,
     'L0_attn_in_proj_b': 8.0,
     'L0_attn_short_w': 4.417,
     'L0_attn_short_b': 4.351,
     'L0_attn_mlp_w0': 6.656,
     'L0_attn_mlp_b0': 6.757,
     'L0_attn_mlp_w1': 5.22,
     'L0_attn_mlp_b1': 8.0,
     'L0_attn_mlp_w2': 4.98,
     'L0_attn_mlp_b2': 8.0,
     'L0_attn_mlp_w3': 4.051,
     'L0_attn_filter_bias': 8.0,
     'L0_attn_out_proj_w': 4.072,
     'L1_ffn_w_gate': 8.0,
     'L1_ffn_w_shared_up': 8.0,
     'L1_ffn_w_shared_down': 8.0,
     'L1_ffn_w_up': 8.0,
     'L1_ffn_w_down': 8.0}
    for name, (base, spread) in spreads.items():
        noise = np.random.default_rng([zlib.crc32(name.encode()), seed]).standard_normal(out[name].shape)
        drawn = base * np.exp(spread * noise) if base else spread * noise
        out[name] = jnp.asarray(drawn.astype(out[name].dtype))
    for name, factor in factors.items():
        out[name] = (out[name] * factor).astype(out[name].dtype)
    return out
```

```python
from contextlib import ExitStack

import concourse.bass as bass
from concourse import mybir

F32 = mybir.dt.float32
BF16 = mybir.dt.bfloat16
ALU = mybir.AluOpType
ACT = mybir.ActivationFunctionType
AX_X = mybir.AxisListType.X

P = 128
NB, L, D = 8, 256, 256
TOK = NB * L
LT = L // P
DT = D // P
CH = 3 * D // P
FO = 64
HID = 1024
HT = HID // P
HQ, HKV, DH = 16, 4, 16
G = HQ // HKV
QV = HQ * DH + HKV * DH
E, EH, HS = 64, 32, 64
TOPK, CAP = 6, 128
EPT = P // EH
ET = E // EPT
LN_EPS = 1e-5
RMS_EPS = 1.1920929e-07
TWO_PI = 6.283185307179586
TWO_PI_HI = 6.28125
TWO_PI_LO = TWO_PI - TWO_PI_HI
PI_SAFE = 3.1415925
ROUND = 12582912.0

MATS = ["ident", "cos_t", "msin_t", "cos_w", "msin_w", "icos", "imsin", "sumsel", "tri", "ones", "had"]


def mixed_kernel(nc, x, xT, w_in, b_in, short_w, short_b, mlp_w0, mlp_b0, freq, mlp_w1, mlp_b1, mlp_w2, mlp_b2,
                 mlp_w3, filter_bias, w_out, b_out, w1, w3, w2, wqv, wo, wgate, ws_up, ws_down,
                 we_gate, we_val, we_down, mats, decay, pos_emb, expert_sel, out):
    with ExitStack() as ctx:
        def sb(name, shape, dt=F32):
            return ctx.enter_context(nc.sbuf_tensor(name, shape, dt))

        def sem(name):
            return ctx.enter_context(nc.semaphore(name))

        mat = {n: sb("m_" + n, [P, P]) for n in MATS}
        pos_sb = sb("pos_sb", [3, L])
        bin_sb = sb("bin_sb", [P, CH])
        sw = sb("sw", [P, 3, CH])
        sbias = sb("sbias", [P, CH])
        bias2 = sb("bias2", [P, CH])
        m0 = sb("m0", [3, FO])
        m1 = sb("m1", [FO, FO])
        m2 = sb("m2", [FO, FO])
        m3 = sb("m3", [FO, D])
        mb = sb("mb", [FO, 4])
        fb = sb("fb", [1, D])
        wout = sb("wout", [P, DT, D])
        bout = sb("bout", [P, D])
        wqv_sb = sb("wqv_sb", [P, DT, QV])
        wo_sb = sb("wo_sb", [P, G, D])
        wg_sb = sb("wg_sb", [P, DT, E])
        wsu = sb("wsu", [P, DT, 2 * HS])
        wsd = sb("wsd", [HS, D])
        rms_eps = sb("rms_eps", [P, HQ + HKV])
        mhalf = sb("mhalf", [P, HQ + HKV])
        ln_eps = sb("ln_eps", [P, LT])
        scratch = sb("scratch", [P, 1])


        def views(store, *shapes):
            got, at_word = [], 0
            for shape in shapes:
                n = 1
                for d in shape:
                    n *= d
                piece = store[:, at_word:at_word + n]
                dims = " ".join("abc"[:len(shape)])
                if len(shape) > 1:
                    piece = piece.rearrange(f"p ({dims}) -> p {dims}", **dict(zip("abc", shape)))
                got.append(piece)
                at_word += n
            return got

        store_a = sb("store_a", [P, 2 * DT * E * EH])
        weg, wev = views(store_a, (DT, E * EH), (DT, E * EH))
        win, u, uc, vT, vtok, Vr, Vi, Yr, pr0 = views(
            store_a, (DT, 3 * D), (CH, L + 2), (CH, L), (DT, L), (LT, D), (LT, D), (LT, D), (LT, D), (LT, D))
        store_b = sb("store_b", [P, 2 * DT * HID + HT * D])
        w1_sb, w3_sb, w2_sb = views(store_b, (DT, HID), (DT, HID), (HT, D))
        wed, esel_all = views(store_b, (ET, D), (ET, P))
        esel = esel_all[0:E]
        store_c = sb("store_c", [P, ET * L])
        w2_tmp, _ = views(store_c, (HT, D), (HT, D))
        prob = views(store_c, (HKV, 2 * L), (HKV, 2 * L))
        hT2, = views(store_c, (ET, L))

        xtok = sb("xtok", [P, NB * LT, D])
        xT0 = sb("xT0", [P, DT, TOK])
        x3T = xT0
        gateT = sb("gateT", [E, TOK])
        arg = sb("arg", [FO, L])
        turns = sb("turns", [FO, L])
        hf = sb("hf", [FO, L])
        Kr = sb("Kr", [P, 2, D])
        Ki = sb("Ki", [P, 2, D])

        Yi = sb("Yi", [P, LT, D])
        pr = [pr0] + [sb(f"pr{n}", [P, LT, D]) for n in (1, 2, 3)]
        yx = sb("yx", [P, DT, L])
        lnA, lnA_in = sb("lnA", [P, LT, D]), sb("lnA_in", [P, LT, D])
        x1T = sb("x1T", [P, DT, L])

        th = sb("th", [P, 2, L])
        hT = sb("hT", [P, HT, L])
        lnB, lnB_in = sb("lnB", [P, LT, D]), sb("lnB_in", [P, LT, D])
        decay_sb, taps = lnB, lnB_in
        x2T = sb("x2T", [P, DT, L])

        sq = sb("sq", [P, LT, QV])
        ms = sb("ms", [P, LT, HQ + HKV])
        rs = sb("rs", [P, LT, HQ + HKV])
        qpad = sb("qpad", [P, LT, G, HKV, 32])
        kpad = sb("kpad", [P, LT, HKV, 32])
        vaug = sb("vaug", [P, LT, HKV, 32])
        QT = sb("QT", [P, G, L])
        KT = sb("KT", [P, L])
        yT = sb("yT", [P, G, L])
        rsum = sb("rsum", [P, G, L])
        lnC, lnC_in = sb("lnC", [P, LT, D]), sb("lnC_in", [P, LT, D])
        ssq = sb("ssq", [P, LT])
        rms = sb("rms", [P, LT])
        x3s = sb("x3s", [P, DT, L])
        sc = sb("sc", [P, LT, E])
        rep = sb("rep", [P, LT, E])
        top = sb("top", [P, LT, 8])
        tsum = sb("tsum", [P, LT])
        picked = sb("picked", [P, LT, E], BF16)
        before = sb("before", [P, E], BF16)
        onesb = sb("onesb", [P, P], BF16)
        trib = sb("trib", [P, P], BF16)
        wtok = sb("wtok", [P, LT, P])

        stat = {k: sb("stat" + k, [P, LT, 6]) for k in "ABCD"}
        mv = {k: sb("mv" + k, [P, LT, 2]) for k in "ABCD"}
        rstd = {k: sb("rstd" + k, [P, LT]) for k in "ABCD"}
        lnD = sb("lnD", [P, LT, D])
        hs = sb("hs", [HS, L])

        ps = ctx.enter_context(nc.psum_tensor("ps", [P, 8, 512], F32))
        bank = [ps[:, n, :] for n in range(8)]

        s_mat, s_filt, s_wa, s_x, s_xT, s_wb, s_w2l, s_wc, s_wd = (sem("s_" + n) for n in (
            "mat", "filt", "wa", "x", "xT", "wb", "w2l", "wc", "wd"))
        s_out = sem("s_out")
        i_dve, i_pool, i_pe, i_act = (sem("i_" + n) for n in ("dve", "pool", "pe", "act"))
        i_w2 = sem("i_w2")
        i_w2pe = sem("i_w2pe")
        i_w2done = sem("i_w2done")
        i_ready = sem("i_ready")
        i_bias2 = sem("i_bias2")
        i_pads = sem("i_pads")
        i_bout = sem("i_bout")
        names = """a_full a_free a_u a_conv a_vT a_vtok a_Vr a_Yr a_Yi a_yx a_ln a_x1T a_dve a_pool a_var a_rstd a_kept a_Vi a_pool2
                   b_full b_free b_th b_g b_h b_ln b_x2T b_dve b_pool b_var b_rstd b_kept
                   c_qv c_sq c_ms c_rs c_q c_v c_qt c_qtc c_s c_p c_pv c_y c_den c_ssum c_yn c_wo c_ss c_rms c_wod c_ln c_tr c_x3
                   c_dve c_pool c_var c_rstd c_kept c_lg c_sc c_pick c_pos c_posd c_w c_wtr c_gateT c_before c_cnt
                   d_full d_free d_th d_h d_hs d_acc d_accd d_dve d_pool d_var d_rstd d_ln d_act d_g""".split()
        S = {n: sem(n) for n in names}

        class Chain:

            def __init__(self, eng, s, per=None):
                self.eng, self.s, self.per, self.n = eng, s, per, 0

            def begin(self, b):
                if self.n and self.per is None:
                    self.per = self.n
                self.b, self.n = b, 0

            def link(self, ins):
                self.n += 1
                ins.then_inc(self.s, 1)

            def settle(self):
                self.eng.wait_ge(self.s, self.n if self.per is None else self.b * self.per + self.n)

        def at(eng, name, b, k, per):
            eng.wait_ge(S[name], b * per + k)

        def ago(eng, name, b, k, per):
            if not (isinstance(b, int) and b == 0):
                eng.wait_ge(S[name], (b - 1) * per + k)

        def hold():
            nc.vector.memset(scratch[:, :], 0.0)

        def tiles(b):
            return bass.ds(b * LT, LT)

        def toks(b):
            return bass.ds(b * L, L)

        def halves(t):
            return t.rearrange("p (a n) -> p a n", a=2)

        ORDER = [("C", 0), ("B", 0), ("A", 0), ("B", 1), ("C", 1), ("B", 2), ("A", 1), ("C", 2), ("B", 3), ("C", 3),
                 ("A", 2), ("B", 4), ("C", 4), ("A", 3), ("B", 5), ("C", 5), ("A", 4), ("B", 6), ("C", 6), ("A", 5),
                 ("B", 7), ("C", 7), ("A", 6), ("B", 8), ("C", 8), ("A", 7), ("B", 9), ("C", 9),
                 ("C", 10), ("C", 11), ("A", 8), ("C", 12)]

        def layers(eng, steps):
            def turn(a, b, c):
                for piece, k in ORDER:
                    n = {"A": a, "B": b, "C": c}[piece]
                    if n is not None and k < len(steps[piece]) and steps[piece][k] is not None:
                        steps[piece][k](n)

            turn(0, None, None)
            turn(1, 0, None)
            turn(2, 1, 0)
            with eng.Fori(3, NB) as i:
                turn(i, i - 1, i - 2)
            turn(None, NB - 1, NB - 2)
            turn(None, None, NB - 1)

        def used(eng, name, b, j):
            if j >= 2:
                at(eng, name, b, j - 1, ET + 1)
            else:
                ago(eng, name, b, ET + j, ET + 1)

        def each_batch(eng, step):
            step(0)
            with eng.Fori(1, NB) as b:
                step(b)

        block = ctx.enter_context(nc.Block())

        @block.sync
        def _(sp):
            for n, name in enumerate(MATS):
                sp.dma_start(mat[name][:, :], mats[n]).then_inc(s_mat, 16)
            for dst, src in ((pos_sb[:, :], pos_emb), (m0[:, :], mlp_w0), (m1[:, :], mlp_w1), (m2[:, :], mlp_w2),
                             (m3[:, :], mlp_w3), (mb[:, 0:1], mlp_b0), (mb[:, 1:2], mlp_b1), (mb[:, 2:3], mlp_b2),
                             (mb[:, 3:4], freq), (fb[:, :], filter_bias), (decay_sb[:, :, :], decay)):
                sp.dma_start(dst, src).then_inc(s_filt, 16)
            sp.dma_start(w2_sb[:, :, :], w2).then_inc(s_w2l, 16)
            for dst, src in ((w1_sb, w1), (w3_sb, w3)):
                sp.dma_start(dst[:, :, :], src).then_inc(s_wb, 16)
            for dst, src in ((wqv_sb[:, :, :], wqv), (wo_sb[:, :, :], wo), (wg_sb[:, :, :], wgate)):
                sp.dma_start(dst, src).then_inc(s_wc, 16)
            for dst, src in ((wsu[:, :, :], ws_up), (wsd[:, :], ws_down)):
                sp.dma_start(dst, src).then_inc(s_wd, 16)
            at(sp, "a_full", NB - 1, 9, 9)
            for dst, src in ((weg, we_gate), (wev, we_val)):
                sp.dma_start(dst, src).then_inc(s_wd, 16)
            at(sp, "b_full", NB - 1, 9, 10)
            for dst, src in ((esel, expert_sel), (wed, we_down)):
                sp.dma_start(dst, src).then_inc(s_wd, 16)
            with sp.Fori(0, NB) as b:
                at(sp, "d_ln", b, 2, 2)
                sp.dma_start(out[:, tiles(b), :], lnD[:, :, :]).then_inc(s_out, 16)
            sp.wait_ge(s_out, 16 * NB)

        @block.scalar
        def _(act):
            act.dma_start(xT0[:, :, :], xT).then_inc(s_xT, 16)
            for dst, src in ((win[:, :, :], w_in), (bin_sb[:, :], b_in), (sw[:, :, :], short_w),
                             (sbias[:, :], short_b), (wout[:, :, :], w_out), (bout[:, :], b_out)):
                act.dma_start(dst, src).then_inc(s_wa, 16)
            act.dma_start(xtok[:, :, :], x).then_inc(s_x, 16)
            for k in range(3):
                act.wait_ge(i_dve, 6 * (k + 1))
                nc.scalar.activation(hf[:, :], arg[:, :], ACT.Sin).then_inc(i_act, 1)
            act.wait_ge(i_bias2, 2)

            def a_u(b, part):
                at(act, "a_full", b, part + 1, 9)
                ago(act, "a_yx" if part == 2 else "a_vT", b, 1, 1)
                for q in range(2):
                    m = 4 - 2 * part + q
                    nc.scalar.activation(u[:, m, 2:L + 2], halves(bank[0])[:, q, :], ACT.Identity,
                                         bias=bin_sb[:, m:m + 1])
                    last = nc.scalar.activation(uc[:, m, :], halves(bank[0])[:, q, :], ACT.Identity,
                                                bias=bias2[:, m:m + 1], scale=sw[:, 2, m:m + 1])
                last.then_inc(S["a_u"], 1)

            def a_vtok(b):
                at(act, "a_full", b, 4, 9)
                nc.scalar.activation(vtok[:, :, :], halves(bank[0]), ACT.Copy).then_inc(S["a_vtok"], 1)

            def a_spec(b, k):
                at(act, "a_full", b, 5 + k, 9)
                ago(act, "a_Yr", b, 1, 1)
                ago(act, "a_Yi", b, 1, 1)
                nc.scalar.activation((Vr, Vi)[k][:, :, :], halves(bank[0]), ACT.Copy)\
                    .then_inc(S[("a_Vr", "a_Vi")[k]], 1)

            def a_x1T(b):
                at(act, "a_full", b, 9, 9)
                ago(act, "b_full", b, 8, 10)
                nc.scalar.activation(x1T[:, :, :], halves(bank[0]), ACT.Copy).then_inc(S["a_x1T"], 1)

            def b_th(b, h):
                at(act, "b_full", b, h + 1, 10)
                if h >= 2:
                    at(act, "b_g", b, h - 1, 8)
                else:
                    ago(act, "b_g", b, h + 7, 8)
                nc.scalar.activation(th[:, h % 2, :], bank[1 + h % 2][:, 0:L], ACT.Tanh, scale=0.5)\
                    .then_inc(S["b_th"], 1)

            def b_x2T(b):
                at(act, "b_full", b, 10, 10)
                ago(act, "c_qv", b, 1, 1)
                nc.scalar.activation(x2T[:, :, :], halves(bank[2]), ACT.Copy).then_inc(S["b_x2T"], 1)

            def c_sq(b):
                at(act, "c_qv", b, 1, 1)
                ago(act, "c_ssum", b, 1, 1)
                for t in range(LT):
                    last = nc.scalar.activation(sq[:, t, :], bank[3 + t][:, 0:QV], ACT.Square, scale=DH ** -0.5)
                last.then_inc(S["c_sq"], 1)
                ago(act, "c_pv", b, 4, 4)
                act.wait_ge(i_pads, 1)
                for t in range(LT):
                    last = nc.scalar.activation(vaug[:, t, :, 0:DH],
                                                bank[3 + t][:, HQ * DH:QV].rearrange("p (h d) -> p h d", h=HKV),
                                                ACT.Copy)
                last.then_inc(S["c_v"], 1)

            def c_qtc(b):
                at(act, "c_qt", b, 1, 1)
                ago(act, "c_s", b, 4, 4)
                for p in range(2):
                    nc.scalar.activation(QT[:, 2 * p:2 * p + 2, :], halves(bank[5 + p]), ACT.Copy)
                nc.scalar.activation(KT[:, :], bank[3][:, 0:L], ACT.Copy).then_inc(S["c_qtc"], 1)

            def c_exp(b, n):
                at(act, "c_s", b, n + 1, 4)
                if n >= 2:
                    at(act, "c_pv", b, n - 1, 4)
                else:
                    ago(act, "c_pv", b, n + 3, 4)
                for h in range(0, HKV, 2):
                    last = nc.scalar.activation(prob[n % 2][:, h:h + 2, :], ps[:, 3 + h:5 + h, :], ACT.Exp)
                last.then_inc(S["c_p"], 1)

            def c_ss(b):
                at(act, "c_wo", b, 1, 1)
                at(act, "c_ms", b, 1, 1)
                for t in range(LT):
                    last = nc.scalar.activation(sq[:, t, 0:D], halves(bank[5])[:, t, :], ACT.Square,
                                                scale=D ** -0.5)
                last.then_inc(S["c_ss"], 1)

            def c_x3(b):
                at(act, "c_tr", b, 1, 1)
                nc.scalar.activation(x3s[:, :, :], halves(bank[3]), ACT.Copy)
                nc.scalar.activation(x3T[:, :, toks(b)], halves(bank[3]), ACT.Copy).then_inc(S["c_x3"], 1)

            def c_sc(b):
                at(act, "c_lg", b, 1, 1)
                ago(act, "c_pick", b, 1, 1)
                nc.scalar.activation(rep[:, :, :], bank[4][:, 0:LT * E].rearrange("p (t e) -> p t e", t=LT),
                                     ACT.Tanh, scale=0.5).then_inc(S["c_sc"], 1)

            def c_gateT(b):
                at(act, "c_wtr", b, 1, 1)
                nc.scalar.activation(gateT[:, toks(b)], bank[4][0:E, 0:L], ACT.Copy).then_inc(S["c_gateT"], 1)

            layers(act, {
                "A": [lambda b: a_u(b, 0), lambda b: a_u(b, 1), lambda b: a_u(b, 2), a_vtok,
                      lambda b: a_spec(b, 0), lambda b: a_spec(b, 1), None, None, a_x1T],
                "B": [lambda b, h=h: b_th(b, h) for h in range(HT)] + [None, b_x2T],
                "C": [c_sq, c_qtc] + [lambda b, n=n: c_exp(b, n) for n in range(4)]
                + [None, None, c_ss, c_x3, c_sc, None, c_gateT]})

            at(act, "b_g", NB - 1, 8, 8)
            def d_gates(b):
                for j in range(ET + 1):
                    at(act, "d_full", b, j + 1, ET + 1)
                    used(act, "d_g", b, j)
                    n = P if j < ET else HS
                    nc.scalar.activation(th[0:n, j % 2, :], bank[2 * (j % 2)][0:n, 0:L], ACT.Tanh, scale=0.5)\
                        .then_inc(S["d_th"], 1)

            each_batch(act, d_gates)

        @block.tensor
        def _(pe):
            mm, tr = nc.tensor.matmul, nc.tensor.transpose
            ident = mat["ident"]
            pe.wait_ge(s_mat, 16 * len(MATS))
            pe.wait_ge(s_filt, 16 * 11)
            mm(bank[0][0:FO, 0:L], m0[:, :], pos_sb[:, :], start=True, stop=True).then_inc(i_pe, 1)
            pe.wait_ge(i_act, 1)
            mm(bank[0][0:FO, 0:L], m1[:, :], hf[:, :], start=True, stop=True).then_inc(i_pe, 1)
            pe.wait_ge(i_act, 2)
            mm(bank[0][0:FO, 0:L], m2[:, :], hf[:, :], start=True, stop=True).then_inc(i_pe, 1)
            pe.wait_ge(i_act, 3)
            for t in range(LT):
                last = mm(halves(bank[0])[:, t, :], hf[:, t * P:(t + 1) * P], m3[:, :], start=True, stop=True)
            last.then_inc(i_pe, 1)
            pe.wait_ge(i_dve, 20)
            for k, (first, wide) in enumerate((("cos_t", "cos_w"), ("msin_t", "msin_w"))):
                view = halves(bank[1 + k])
                mm(view[:, 0, :], mat[first][:, :], taps[:, 0, :], start=True, stop=True)
                mm(view[:, 1, :], mat[first][:, :], taps[:, 1, :], start=True, stop=False)
                last = mm(view[:, 1, :], mat[wide][:, :], taps[:, 0, :], start=False, stop=True)
            last.then_inc(i_pe, 1)
            pe.wait_ge(i_w2, 6)
            for q in range(HT // 2):
                mm(bank[4 + q][:, :], mat["had"][:, :], w2_tmp[:, 2 * q:2 * q + 2, :].rearrange("p a d -> p (a d)"),
                   start=True, stop=True).then_inc(i_w2pe, 1)
            pe.wait_ge(s_xT, 16)
            pe.wait_ge(s_wa, 16 * 6)
            pe.wait_ge(i_ready, 1)

            def a_u(b, part):
                a_wait(b, part)
                for q in range(2):
                    m = 4 - 2 * part + q
                    for c in range(DT):
                        last = mm(halves(bank[0])[:, q, :], win[:, c, m * P:(m + 1) * P], xT0[:, c, toks(b)],
                                  start=c == 0, stop=c == DT - 1)
                last.then_inc(S["a_full"], 1)

            def a_wait(b, k):
                name, n, per = (("a_x1T", 1, 1), ("a_u", 1, 3), ("a_u", 2, 3), ("a_u", 3, 3), ("a_vtok", 1, 1),
                                ("a_Vr", 1, 1), ("a_Vi", 1, 1), ("a_yx", 1, 1), ("a_free", 1, 1))[k]
                (ago if k == 0 else at)(pe, name, b, n, per)

            def a_vT(b):
                a_wait(b, 3)
                at(pe, "a_vT", b, 1, 1)
                for t in range(LT):
                    for m in range(DT):
                        last = tr(halves(bank[0])[:, t, m * P:(m + 1) * P], vT[:, m, t * P:(t + 1) * P], ident[:, :])
                last.then_inc(S["a_full"], 1)

            def a_dft(b, k):
                a_wait(b, 4 + k)
                at(pe, "a_vtok", b, 1, 1)
                last = mm(bank[0][:, :], mat[("cos_t", "msin_t")[k]][:, :],
                          vtok[:, :, :].rearrange("p t d -> p (t d)"), start=True, stop=True)
                last.then_inc(S["a_full"], 1)

            def a_idft(b):
                a_wait(b, 6)
                at(pe, "a_Yr", b, 1, 1)
                at(pe, "a_Yi", b, 1, 1)
                for m in range(DT):
                    for t in range(LT):
                        o = halves(bank[0])[:, m, t * P:(t + 1) * P]
                        mm(o, Yr[:, t, m * P:(m + 1) * P], mat["icos"][:, :], start=True, stop=False)
                        last = mm(o, Yi[:, t, m * P:(m + 1) * P], mat["imsin"][:, :], start=False, stop=True)
                last.then_inc(S["a_full"], 1)

            def a_out(b):
                a_wait(b, 7)
                at(pe, "a_yx", b, 1, 1)
                for t in range(LT):
                    for m in range(DT):
                        last = mm(halves(bank[0])[:, t, :], yx[:, m, t * P:(t + 1) * P], wout[:, m, :],
                                  start=m == 0, stop=m == DT - 1)
                last.then_inc(S["a_full"], 1)

            def turn_rows(dst, src):
                for m in range(DT):
                    for t in range(LT):
                        last = tr(halves(dst)[:, m, t * P:(t + 1) * P], src[:, t, m * P:(m + 1) * P], ident[:, :])
                return last

            def a_tr(b):
                a_wait(b, 8)
                at(pe, "a_ln", b, 2, 2)
                turn_rows(bank[0], lnA).then_inc(S["a_full"], 1)

            def b_up(b, h):
                if h == 0:
                    at(pe, "a_x1T", b, 1, 1)
                if h >= 2:
                    at(pe, "b_h", b, h - 1, 8)
                elif h == 0:
                    ago(pe, "b_free", b, 1, 1)
                else:
                    ago(pe, "b_x2T", b, 1, 1)
                for q, w in enumerate((w1_sb, w3_sb)):
                    for c in range(DT):
                        last = mm(halves(bank[1 + h % 2])[:, q, :], w[:, c, h * P:(h + 1) * P], x1T[:, c, :],
                                  start=c == 0, stop=c == DT - 1)
                last.then_inc(S["b_full"], 1)

            def b_down(b):
                at(pe, "b_h", b, HT, 8)
                if isinstance(b, int) and b == 0:
                    pe.wait_ge(i_w2done, 1)
                for t in range(LT):
                    for h in range(HT):
                        last = mm(halves(bank[1])[:, t, :], hT[:, h, t * P:(t + 1) * P], w2_sb[:, h, :],
                                  start=h == 0, stop=h == HT - 1)
                last.then_inc(S["b_full"], 1)

            def b_tr(b):
                at(pe, "b_h", b, HT, 8)
                at(pe, "b_ln", b, 2, 2)
                turn_rows(bank[2], lnB).then_inc(S["b_full"], 1)

            def c_qv(b):
                at(pe, "b_x2T", b, 1, 1)
                ago(pe, "c_x3", b, 1, 1)
                ago(pe, "c_gateT", b, 1, 1)
                for t in range(LT):
                    for c in range(DT):
                        last = mm(bank[3 + t][:, 0:QV], x2T[:, c, t * P:(t + 1) * P], wqv_sb[:, c, :],
                                  start=c == 0, stop=c == DT - 1)
                last.then_inc(S["c_qv"], 1)

            def c_qt(b):
                at(pe, "c_q", b, 1, 1)
                at(pe, "c_v", b, 1, 1)
                ago(pe, "c_wod", b, 1, 1)
                for g in range(G):
                    for t in range(LT):
                        tr(halves(bank[5 + g // 2])[:, g % 2, t * P:(t + 1) * P],
                           qpad[:, t, g, :, :].rearrange("p h d -> p (h d)"), ident[:, :])
                for t in range(LT):
                    last = tr(bank[3][:, t * P:(t + 1) * P], kpad[:, t, :, :].rearrange("p h d -> p (h d)"),
                              ident[:, :])
                last.then_inc(S["c_qt"], 1)

            def c_s(b, n):
                if n == 0:
                    at(pe, "c_qtc", b, 1, 1)
                else:
                    at(pe, "c_p", b, n, 4)
                pair, t = n // 2, n % 2
                for h in range(HKV):
                    last = mm(bank[3 + h][:, :], KT[32 * h:32 * h + 32, t * P:(t + 1) * P],
                              QT[32 * h:32 * h + 32, 2 * pair:2 * pair + 2, :].rearrange("p g n -> p (g n)"),
                              start=True, stop=True)
                last.then_inc(S["c_s"], 1)

            def c_pv(b, n):
                at(pe, "c_p", b, n + 1, 4)
                if n == 0:
                    ago(pe, "c_y", b, 2, 2)
                if n == 2:
                    at(pe, "c_y", b, 1, 2)
                for h in range(HKV):
                    last = mm(bank[7][32 * h:32 * h + 32, :], vaug[:, n % 2, h, :], prob[n % 2][:, h, :],
                              start=n % 2 == 0, stop=n % 2 == 1, skip_group_check=True)
                last.then_inc(S["c_pv"], 1)

            def c_den(b):
                at(pe, "c_y", b, 2, 2)
                for p in range(2):
                    last = mm(bank[3 + p][:, :], mat["sumsel"][:, :],
                              yT[:, 2 * p:2 * p + 2, :].rearrange("p g n -> p (g n)"), start=True, stop=True)
                last.then_inc(S["c_den"], 1)

            def c_wo(b):
                at(pe, "c_yn", b, 1, 1)
                at(pe, "c_p", b, 4, 4)
                for t in range(LT):
                    for g in range(G):
                        last = mm(halves(bank[5])[:, t, :], yT[:, g, t * P:(t + 1) * P], wo_sb[:, g, :],
                                  start=g == 0, stop=g == G - 1)
                last.then_inc(S["c_wo"], 1)

            def c_tr(b):
                at(pe, "c_ln", b, 2, 2)
                turn_rows(bank[3], lnC).then_inc(S["c_tr"], 1)

            def c_lg(b):
                at(pe, "c_x3", b, 1, 1)
                for t in range(LT):
                    for c in range(DT):
                        last = mm(bank[4][:, t * E:(t + 1) * E], x3s[:, c, t * P:(t + 1) * P], wg_sb[:, c, :],
                                  start=c == 0, stop=c == DT - 1)
                last.then_inc(S["c_lg"], 1)

            def c_pos(b):
                at(pe, "c_pick", b, 1, 1)
                ago(pe, "c_before", b, 1, 1)
                if isinstance(b, int) and b == 0:
                    pe.wait_ge(i_pads, 1)
                mm(bank[4][:, 0:E], trib[:, :], picked[:, 0, :], start=True, stop=False)
                mm(bank[4][:, 0:E], onesb[:, :], before[:, :], start=False, stop=True)
                mm(bank[4][:, E:2 * E], trib[:, :], picked[:, 1, :], start=True, stop=False)
                mm(bank[4][:, E:2 * E], onesb[:, :], picked[:, 0, :], start=False, stop=False)
                mm(bank[4][:, E:2 * E], onesb[:, :], before[:, :], start=False, stop=True).then_inc(S["c_pos"], 1)

            def c_wtr(b):
                at(pe, "c_w", b, 1, 1)
                for t in range(LT):
                    last = tr(bank[4][:, t * P:(t + 1) * P], wtok[:, t, :], ident[:, :])
                last.then_inc(S["c_wtr"], 1)

            pe.wait_ge(s_wb, 32)
            pe.wait_ge(s_wc, 48)

            def s_then_pv(n):
                def step(b):
                    if n < 4:
                        c_s(b, n)
                    if n:
                        c_pv(b, n - 1)
                return step

            layers(pe, {
                "A": [lambda b: a_u(b, 0), lambda b: a_u(b, 1), lambda b: a_u(b, 2), a_vT,
                      lambda b: a_dft(b, 0), lambda b: a_dft(b, 1), a_idft, a_out, a_tr],
                "B": [lambda b, h=h: b_up(b, h) for h in range(HT)] + [b_down, b_tr],
                "C": [c_qv, c_qt] + [s_then_pv(n) for n in range(5)] + [c_den, c_wo, c_tr, c_lg, c_pos, c_wtr]})

            pe.wait_ge(s_wd, 16 * 6)
            at(pe, "c_gateT", NB - 1, 1, 1)
            at(pe, "c_wod", NB - 1, 1, 1)

            def down(b, j):
                at(pe, "d_h", b, j + 1, ET + 1)
                if j == 0:
                    ago(pe, "d_accd", b, 1, 1)
                for t in range(LT):
                    h = hT2[:, j, t * P:(t + 1) * P] if j < ET else hs[:, t * P:(t + 1) * P]
                    w = wed[:, j, :] if j < ET else wsd[:, :]
                    last = mm(bank[4 + t][:, 0:D], h, w, start=j == 0, stop=j == ET)
                if j == ET:
                    last.then_inc(S["d_acc"], 1)

            def d_experts(b):
                for j in range(ET + 1):
                    if j >= 2:
                        down(b, j - 2)
                    else:
                        used(pe, "d_h", b, j)
                    o = halves(bank[2 * (j % 2)])
                    if j < ET:
                        for q, w in enumerate((weg, wev)):
                            for c in range(DT):
                                mm(o[:, q, :], w[:, c, j * P:(j + 1) * P], x3T[:, c, toks(b)],
                                   start=c == 0, stop=c == DT - 1)
                        last = mm(bank[1 + 2 * (j % 2)][:, 0:L], esel[:, j, :], gateT[:, toks(b)],
                                  start=True, stop=True)
                    else:
                        for q in range(2):
                            for c in range(DT):
                                last = mm(o[0:HS, q, :], wsu[:, c, (1 - q) * HS:(2 - q) * HS], x3T[:, c, toks(b)],
                                          start=c == 0, stop=c == DT - 1)
                    last.then_inc(S["d_full"], 1)
                down(b, ET - 1)
                down(b, ET)

            each_batch(pe, d_experts)

        @block.vector
        def _(dve):
            V = nc.vector
            setup = Chain(dve, i_dve)
            setup.begin(0)
            dve.wait_ge(s_filt, 16 * 11)
            for k in range(3):
                dve.wait_ge(i_pe, k + 1)
                setup.link(V.tensor_scalar(arg[:, :], bank[0][0:FO, 0:L], mb[:, k:k + 1], mb[:, 3:4],
                                           ALU.add, ALU.mult))
                setup.settle()
                setup.link(V.tensor_scalar(turns[:, :], arg[:, :], 1.0 / TWO_PI, ROUND, ALU.mult, ALU.add))
                setup.settle()
                setup.link(V.tensor_scalar(turns[:, :], turns[:, :], ROUND, None, ALU.subtract))
                setup.settle()
                for part in (TWO_PI_HI, TWO_PI_LO):
                    setup.link(V.scalar_tensor_tensor(out=arg[:, :], in0=turns[:, :], scalar=-part,
                                                      in1=arg[:, :], op0=ALU.mult, op1=ALU.add))
                    setup.settle()
                setup.link(V.tensor_scalar(arg[:, :], arg[:, :], PI_SAFE, -PI_SAFE, ALU.min, ALU.max))
            dve.wait_ge(i_pe, 4)
            setup.link(V.tensor_tensor(taps[:, :, :], halves(bank[0]), decay_sb[:, :, :], ALU.mult))
            setup.settle()
            setup.link(V.tensor_tensor(taps[0:1, 0, :], taps[0:1, 0, :], fb[:, :], ALU.add))
            dve.wait_ge(i_pe, 5)
            setup.link(V.tensor_copy(Kr[:, :, :], halves(bank[1])))
            setup.link(V.tensor_copy(Ki[:, :, :], halves(bank[2])))
            setup.settle()
            dve.wait_ge(s_wa, 16 * 6)
            setup.link(V.tensor_tensor(bias2[:, :], bin_sb[:, :], sw[:, 2, :], ALU.mult))
            setup.settle()
            V.tensor_tensor(bias2[:, :], bias2[:, :], sbias[:, :], ALU.add).then_inc(i_bias2, 1)
            V.memset(u[:, :, 0:2], 0.0).then_inc(i_bias2, 1)
            dve.wait_ge(i_bias2, 2)
            for q in range(HT // 2):
                dve.wait_ge(i_w2pe, q + 1)
                last = V.tensor_copy(w2_sb[:, 2 * q:2 * q + 2, :], halves(bank[4 + q]))
            last.then_inc(i_w2done, 1)
            dve.wait_ge(i_w2done, 1)
            V.memset(scratch[:, :], 0.0).then_inc(i_ready, 1)
            dve.wait_ge(s_x, 16)
            dve.wait_ge(i_pads, 1)
            dve.wait_ge(i_bout, NB * LT)

            chains = {k: Chain(dve, S[k.lower() + "_dve"]) for k in "ABC"}

            def norm(key, b, rows, normed):
                ch, k = chains[key], key.lower()
                for t in range(LT):
                    ch.link(V.bn_stats(stat[key][:, t, :], rows[:, t, :]))
                ch.settle()
                hold()
                for t in range(LT):
                    last = V.bn_aggr(mv[key][:, t, :], stat[key][:, t, :])
                last.then_inc(S[k + "_var"], 1)
                at(dve, k + "_rstd", b, 1, 1)
                for t in range(LT):
                    V.tensor_scalar(normed[:, t, :], rows[:, t, :], mv[key][:, t, 0:1], rstd[key][:, t:t + 1],
                                    ALU.subtract, ALU.mult).then_inc(S[k + "_ln"], 1)

            def a_conv(b, part):
                ch = chains["A"]
                if part == 0:
                    ch.begin(b)
                at(dve, "a_u", b, part + 1, 3)
                for q in range(2):
                    m = 4 - 2 * part + q
                    ch.link(V.scalar_tensor_tensor(out=uc[:, m, :], in0=u[:, m, 1:L + 1], scalar=sw[:, 1, m:m + 1],
                                                   in1=uc[:, m, :], op0=ALU.mult, op1=ALU.add))
                ch.settle()
                for q in range(2):
                    m = 4 - 2 * part + q
                    ins = V.scalar_tensor_tensor(out=uc[:, m, :], in0=u[:, m, 0:L], scalar=sw[:, 0, m:m + 1],
                                                 in1=uc[:, m, :], op0=ALU.mult, op1=ALU.add)
                    if q == 0:
                        ch.link(ins)
                ins.then_inc(S["a_conv"], 1)
                if part == 1:
                    ch.settle()
                    at(dve, "a_conv", b, 2, 3)
                    V.tensor_tensor(vT[:, :, :], uc[:, 4:6, :], uc[:, 2:4, :], ALU.mult).then_inc(S["a_vT"], 1)

            def a_Yr(b):
                ch = chains["A"]
                at(dve, "a_Vr", b, 1, 1)
                at(dve, "a_Vi", b, 1, 1)
                ago(dve, "a_full", b, 7, 9)
                for blk in range(2):
                    ch.link(V.tensor_tensor(pr[0][:, blk, :], Kr[:, blk, :], Vr[:, 0, :], ALU.mult))
                    ch.link(V.tensor_tensor(pr[1][:, blk, :], Ki[:, blk, :], Vi[:, 0, :], ALU.mult))
                ch.settle()
                ch.link(V.tensor_tensor(Yr[:, :, :], pr[0][:, :, :], pr[1][:, :, :], ALU.subtract))
                ch.settle()
                ch.link(V.tensor_tensor(pr[0][:, 0, :], Kr[:, 0, :], Vr[:, 1, :], ALU.mult))
                ch.link(V.tensor_tensor(pr[1][:, 0, :], Ki[:, 0, :], Vi[:, 1, :], ALU.mult))
                ch.settle()
                ch.link(V.tensor_tensor(Yr[:, 1, :], Yr[:, 1, :], pr[0][:, 0, :], ALU.add))
                ch.settle()
                V.tensor_tensor(Yr[:, 1, :], Yr[:, 1, :], pr[1][:, 0, :], ALU.subtract).then_inc(S["a_Yr"], 1)

            def a_yx(b):
                at(dve, "a_full", b, 7, 9)
                at(dve, "a_conv", b, 3, 3)
                V.tensor_tensor(yx[:, :, :], halves(bank[0]), uc[:, 0:2, :], ALU.mult).then_inc(S["a_yx"], 1)

            def a_ln(b):
                ch = chains["A"]
                at(dve, "a_full", b, 8, 9)
                ago(dve, "a_full", b, 9, 9)
                ago(dve, "a_kept", b, 1, 1)
                V.tensor_tensor(lnA_in[:, :, :], halves(bank[0]), xtok[:, tiles(b), :],
                                ALU.add).then_inc(S["a_free"], 1)
                at(dve, "a_free", b, 1, 1)
                norm("A", b, lnA_in, lnA)

            def b_h(b, h):
                ch = chains["B"]
                if h == 0:
                    ch.begin(b)
                    ago(dve, "b_full", b, 9, 10)
                at(dve, "b_th", b, h + 1, 8)
                o = halves(bank[1 + h % 2])
                V.scalar_tensor_tensor(out=hT[:, h, :], in0=th[:, h % 2, :], scalar=1.0, in1=o[:, 0, :],
                                       op0=ALU.add, op1=ALU.mult).then_inc(S["b_g"], 1)
                at(dve, "b_g", b, h + 1, 8)
                V.tensor_tensor(hT[:, h, :], hT[:, h, :], o[:, 1, :], ALU.mult).then_inc(S["b_h"], 1)

            def b_ln(b):
                at(dve, "b_full", b, 9, 10)
                ago(dve, "b_full", b, 10, 10)
                ago(dve, "b_kept", b, 1, 1)
                at(dve, "a_kept", b, 1, 1)
                V.tensor_tensor(lnB_in[:, :, :], halves(bank[1]), xtok[:, tiles(b), :], ALU.add)\
                    .then_inc(S["b_free"], 1)
                at(dve, "b_free", b, 1, 1)
                norm("B", b, lnB_in, lnB)

            def c_q(b):
                ch = chains["C"]
                ch.begin(b)
                at(dve, "c_sq", b, 1, 1)
                ago(dve, "c_rs", b, 1, 1)
                V.tensor_reduce(ms[:, :, :], sq[:, :, :].rearrange("p t (h d) -> p t h d", d=DH), AX_X, ALU.add)\
                    .then_inc(S["c_ms"], 1)
                at(dve, "c_rs", b, 1, 1)
                at(dve, "c_v", b, 1, 1)
                ago(dve, "c_qt", b, 1, 1)
                for t in range(LT):
                    q = bank[3 + t][:, 0:HQ * DH].rearrange("p (h g d) -> p h g d", h=HKV, g=G)
                    r = rs[:, t, 0:HQ].rearrange("p (h g) -> p h g", h=HKV).unsqueeze(3).broadcast_to([P, HKV, G, DH])
                    V.tensor_tensor(qpad[:, t, :, :, 0:DH].rearrange("p g h d -> p h g d"), q, r, ALU.mult)
                    k = bank[3 + t][:, HQ * DH:QV].rearrange("p (h d) -> p h d", h=HKV)
                    last = V.tensor_tensor(kpad[:, t, :, 0:DH], k,
                                           rs[:, t, HQ:HQ + HKV].unsqueeze(2).broadcast_to([P, HKV, DH]), ALU.mult)
                last.then_inc(S["c_q"], 1)

            def c_y(b, p):
                at(dve, "c_pv", b, 2 * p + 2, 4)
                if p == 0:
                    ago(dve, "c_wo", b, 1, 1)
                V.tensor_copy(yT[:, 2 * p:2 * p + 2, :], halves(bank[7])).then_inc(S["c_y"], 1)

            def c_yn(b):
                ch = chains["C"]
                at(dve, "c_den", b, 1, 1)
                for p in range(2):
                    ch.link(V.reciprocal(rsum[:, 2 * p:2 * p + 2, :], halves(bank[3 + p])))
                ch.settle()
                V.tensor_tensor(yT[:, :, :], yT[:, :, :], rsum[:, :, :], ALU.mult).then_inc(S["c_yn"], 1)

            def c_ln(b):
                ch = chains["C"]
                at(dve, "c_ss", b, 1, 1)
                ago(dve, "c_rms", b, 1, 1)
                V.tensor_reduce(ssq[:, :], sq[:, :, 0:D], AX_X, ALU.add).then_inc(S["c_ssum"], 1)
                at(dve, "c_rms", b, 1, 1)
                ago(dve, "c_tr", b, 1, 1)
                ago(dve, "c_kept", b, 1, 1)
                at(dve, "b_kept", b, 1, 1)
                for t in range(LT):
                    last = V.scalar_tensor_tensor(out=lnC_in[:, t, :], in0=halves(bank[5])[:, t, :],
                                                  scalar=rms[:, t:t + 1], in1=xtok[:, bass.ds(b * LT + t, 1), :].rearrange("p o d -> p (o d)"),
                                                  op0=ALU.mult, op1=ALU.add)
                    if t == 0:
                        ch.link(last)
                last.then_inc(S["c_wod"], 1)
                ch.settle()
                at(dve, "c_wod", b, 1, 1)
                norm("C", b, lnC_in, lnC)

            def c_route(b):
                ch = chains["C"]
                at(dve, "c_sc", b, 1, 1)
                ago(dve, "c_w", b, 1, 1)
                ch.link(V.tensor_scalar(sc[:, :, :], rep[:, :, :], 0.5, 0.5, ALU.mult, ALU.add))
                ch.settle()
                hold()
                for t in range(LT):
                    ch.link(V.max(top[:, t, :], sc[:, t, :]))
                ch.settle()
                ch.link(V.tensor_reduce(tsum[:, :], top[:, :, 0:TOPK], AX_X, ALU.add))
                ch.link(V.memset(top[:, :, TOPK:8], -1.0))
                ch.settle()
                hold()
                for t in range(LT):
                    ch.link(V.match_replace(rep[:, t, :], top[:, t, :], sc[:, t, :], -2.0))
                ch.settle()
                ago(dve, "c_before", b, 1, 1)
                ago(dve, "c_pos", b, 1, 1)
                V.tensor_tensor(picked[:, :, :], rep[:, :, :], sc[:, :, :], ALU.not_equal).then_inc(S["c_pick"], 1)
                ch.link(V.reciprocal(tsum[:, :], tsum[:, :]))
                at(dve, "c_pick", b, 1, 1)
                ch.link(V.tensor_tensor(sc[:, :, :], sc[:, :, :], picked[:, :, :], ALU.mult))
                ch.settle()

            def c_w(b):
                ch = chains["C"]
                at(dve, "c_pos", b, 1, 1)
                ago(dve, "c_wtr", b, 1, 1)
                pos = bank[4][:, 0:LT * E].rearrange("p (t e) -> p t e", t=LT)
                V_last = V.scalar_tensor_tensor(out=wtok[:, :, 0:E], in0=pos, scalar=float(CAP), in1=sc[:, :, :],
                                                op0=ALU.is_lt, op1=ALU.mult)
                ch.link(V_last)
                ch.settle()
                for t in range(LT):
                    last = V.tensor_scalar(wtok[:, t, 0:E], wtok[:, t, 0:E], tsum[:, t:t + 1], 0.5, ALU.mult, ALU.mult)
                    if t == 0:
                        ch.link(last)
                last.then_inc(S["c_w"], 1)

            layers(dve, {
                "A": [lambda b: a_conv(b, 0), lambda b: a_conv(b, 1), lambda b: a_conv(b, 2), None, None,
                      a_Yr, a_yx, a_ln, None],
                "B": [lambda b, h=h: b_h(b, h) for h in range(HT)] + [b_ln, None],
                "C": [c_q, None, None, None, lambda b: c_y(b, 0), None, lambda b: c_y(b, 1), c_yn, c_ln, None,
                      c_route, c_w, None]})

            at(dve, "c_kept", NB - 1, 1, 1)
            def d_hidden(b):
                for j in range(ET + 1):
                    at(dve, "d_th", b, j + 1, ET + 1)
                    n = P if j < ET else HS
                    o = halves(bank[2 * (j % 2)])
                    h = hT2[:, j, :] if j < ET else hs[:, :]
                    if j == 0:
                        ago(dve, "d_acc", b, 1, 1)
                    V.scalar_tensor_tensor(out=h, in0=th[0:n, j % 2, :], scalar=1.0, in1=o[0:n, 0, :],
                                           op0=ALU.add, op1=ALU.mult).then_inc(S["d_g"], 1)
                    at(dve, "d_g", b, j + 1, ET + 1)
                    if j < ET:
                        V.tensor_tensor(h, h, o[:, 1, :], ALU.mult).then_inc(S["d_dve"], 1)
                        at(dve, "d_dve", b, j + 1, ET + LT)
                        V.tensor_tensor(h, h, bank[1 + 2 * (j % 2)][:, 0:L], ALU.mult).then_inc(S["d_h"], 1)
                    else:
                        V.scalar_tensor_tensor(out=h, in0=h, scalar=0.5, in1=o[0:HS, 1, :],
                                               op0=ALU.mult, op1=ALU.mult).then_inc(S["d_h"], 1)
                at(dve, "d_acc", b, 1, 1)
                for t in range(LT):
                    last = V.tensor_tensor(lnC_in[:, t, :], bank[4 + t][:, 0:D],
                                           xtok[:, bass.ds(b * LT + t, 1), :].rearrange("p o d -> p (o d)"), ALU.add)
                last.then_inc(S["d_accd"], 1)
                at(dve, "d_accd", b, 1, 1)
                for t in range(LT):
                    V.bn_stats(stat["D"][:, t, :], lnC_in[:, t, :]).then_inc(S["d_dve"], 1)
                at(dve, "d_dve", b, ET + LT, ET + LT)
                hold()
                for t in range(LT):
                    last = V.bn_aggr(mv["D"][:, t, :], stat["D"][:, t, :])
                last.then_inc(S["d_var"], 1)
                at(dve, "d_var", b, 1, 1)
                at(dve, "d_rstd", b, 1, 1)
                if not (isinstance(b, int) and b == 0):
                    dve.wait_ge(s_out, 16 * b)
                for t in range(LT):
                    V.tensor_scalar(lnD[:, t, :], lnC_in[:, t, :], mv["D"][:, t, 0:1], rstd["D"][:, t:t + 1],
                                    ALU.subtract, ALU.mult).then_inc(S["d_ln"], 1)

            each_batch(dve, d_hidden)

        @block.gpsimd
        def _(pool):
            Gp = nc.gpsimd
            pool.wait_ge(s_mat, 16 * len(MATS))
            Gp.tensor_copy(onesb[:, :], mat["ones"][:, :])
            Gp.tensor_copy(trib[:, :], mat["tri"][:, :])
            Gp.memset(before[:, :], 0.0)
            Gp.memset(mhalf[:, :], -0.5)
            Gp.memset(rms_eps[:, :], RMS_EPS)
            Gp.memset(ln_eps[:, :], LN_EPS)
            Gp.memset(wtok[:, :, :], 0.0)
            Gp.memset(qpad[:, :, :, :, :], 0.0)
            Gp.memset(kpad[:, :, :, :], 0.0)
            Gp.memset(vaug[:, :, :, :], 0.0).then_inc(i_pool, 1)
            pool.wait_ge(i_pool, 1)
            Gp.memset(vaug[:, :, :, DH:DH + 1], 1.0).then_inc(i_pads, 1)
            pool.wait_ge(i_pads, 1)
            pool.wait_ge(s_w2l, 16)
            src, dst = w2_sb, w2_tmp
            for n, step in enumerate((1, 2, 4)):
                s = src[:, :, :].rearrange("p (o two i) d -> p o two i d", two=2, i=step)
                d = dst[:, :, :].rearrange("p (o two i) d -> p o two i d", two=2, i=step)
                for o in range(HT // (2 * step)):
                    Gp.tensor_tensor(out=d[:, o, 0], in0=s[:, o, 0], in1=s[:, o, 1], op=ALU.add)
                    last = Gp.tensor_tensor(out=d[:, o, 1], in0=s[:, o, 0], in1=s[:, o, 1], op=ALU.subtract)
                last.then_inc(i_w2, 2)
                pool.wait_ge(i_w2, 2 * n + 2)
                src, dst = dst, src
            pool.wait_ge(s_wa, 16 * 6)
            pool.wait_ge(s_x, 16)
            for t in range(NB * LT):
                Gp.tensor_tensor(out=xtok[:, t, :], in0=xtok[:, t, :], in1=bout[:, :], op=ALU.add).then_inc(i_bout, 1)
            pool.wait_ge(i_bout, NB * LT)

            def rstd_of(key, b):
                k = key.lower()
                at(pool, k + "_var", b, 1, 1)
                ago(pool, k + "_ln", b, 2, 2)
                Gp.tensor_tensor(out=rstd[key][:, :], in0=mv[key][:, :, 1], in1=ln_eps[:, :], op=ALU.add)\
                    .then_inc(S[k + "_pool"], 1)
                per = 3 if key == "C" else 1
                at(pool, k + "_pool", b, per, per)
                Gp.tensor_tensor(out=rstd[key][:, :], in0=rstd[key][:, :], in1=mhalf[:, 0:LT], op=ALU.pow)\
                    .then_inc(S[k + "_rstd"], 1)

            def keep(key, b, src):
                k = key.lower()
                at(pool, k + "_ln", b, 2, 2)
                Gp.tensor_copy(xtok[:, tiles(b), :], src[:, :, :]).then_inc(S[k + "_kept"], 1)

            def a_Yi(b):
                at(pool, "a_Vi", b, 1, 1)
                ago(pool, "a_full", b, 7, 9)
                for blk in range(2):
                    Gp.tensor_tensor(out=pr[2][:, blk, :], in0=Kr[:, blk, :], in1=Vi[:, 0, :], op=ALU.mult)
                    last = Gp.tensor_tensor(out=pr[3][:, blk, :], in0=Ki[:, blk, :], in1=Vr[:, 0, :], op=ALU.mult)
                last.then_inc(S["a_pool2"], 1)
                at(pool, "a_pool2", b, 1, 4)
                Gp.tensor_tensor(out=Yi[:, :, :], in0=pr[2][:, :, :], in1=pr[3][:, :, :], op=ALU.add)\
                    .then_inc(S["a_pool2"], 1)
                at(pool, "a_pool2", b, 2, 4)
                Gp.tensor_tensor(out=pr[2][:, 0, :], in0=Kr[:, 0, :], in1=Vi[:, 1, :], op=ALU.mult)
                Gp.tensor_tensor(out=pr[3][:, 0, :], in0=Ki[:, 0, :], in1=Vr[:, 1, :], op=ALU.mult)\
                    .then_inc(S["a_pool2"], 1)
                at(pool, "a_pool2", b, 3, 4)
                Gp.tensor_tensor(out=Yi[:, 1, :], in0=Yi[:, 1, :], in1=pr[2][:, 0, :], op=ALU.add)\
                    .then_inc(S["a_pool2"], 1)
                at(pool, "a_pool2", b, 4, 4)
                Gp.tensor_tensor(out=Yi[:, 1, :], in0=Yi[:, 1, :], in1=pr[3][:, 0, :], op=ALU.add)\
                    .then_inc(S["a_Yi"], 1)

            def a_rows(b):
                rstd_of("A", b)
                keep("A", b, lnA)

            def b_rows(b):
                rstd_of("B", b)
                keep("B", b, lnB)

            def c_rs(b):
                at(pool, "c_ms", b, 1, 1)
                ago(pool, "c_q", b, 1, 1)
                for t in range(LT):
                    last = Gp.tensor_tensor(out=rs[:, t, :], in0=ms[:, t, :], in1=rms_eps[:, :], op=ALU.add)
                last.then_inc(S["c_pool"], 1)
                at(pool, "c_pool", b, 1, 3)
                for t in range(LT):
                    last = Gp.tensor_tensor(out=rs[:, t, :], in0=rs[:, t, :], in1=mhalf[:, :], op=ALU.pow)
                last.then_inc(S["c_rs"], 1)

            def c_rows(b):
                at(pool, "c_ssum", b, 1, 1)
                ago(pool, "c_wod", b, 1, 1)
                Gp.tensor_tensor(out=rms[:, :], in0=ssq[:, :], in1=rms_eps[:, 0:LT], op=ALU.add)\
                    .then_inc(S["c_pool"], 1)
                at(pool, "c_pool", b, 2, 3)
                Gp.tensor_tensor(out=rms[:, :], in0=rms[:, :], in1=mhalf[:, 0:LT], op=ALU.pow).then_inc(S["c_rms"], 1)
                rstd_of("C", b)
                keep("C", b, lnC)

            def c_before(b):
                at(pool, "c_pos", b, 1, 1)
                Gp.tensor_tensor(out=before[:, :], in0=before[:, :], in1=picked[:, 0, :], op=ALU.add)\
                    .then_inc(S["c_cnt"], 1)
                at(pool, "c_cnt", b, 1, 1)
                Gp.tensor_tensor(out=before[:, :], in0=before[:, :], in1=picked[:, 1, :], op=ALU.add)\
                    .then_inc(S["c_before"], 1)

            layers(pool, {
                "A": [None, None, None, None, None, a_Yi, None, a_rows, None],
                "B": [None] * 8 + [b_rows, None],
                "C": [c_rs] + [None] * 7 + [c_rows, None, None, c_before, None]})

            def d_power(b):
                at(pool, "d_var", b, 1, 1)
                ago(pool, "d_ln", b, 2, 2)
                Gp.tensor_tensor(out=rstd["D"][:, :], in0=mv["D"][:, :, 1], in1=ln_eps[:, :], op=ALU.add)\
                    .then_inc(S["d_pool"], 1)
                at(pool, "d_pool", b, 1, 1)
                Gp.tensor_tensor(out=rstd["D"][:, :], in0=rstd["D"][:, :], in1=mhalf[:, 0:LT], op=ALU.pow)\
                    .then_inc(S["d_rstd"], 1)

            each_batch(pool, d_power)


def kernel(**inputs):
    import math
    import numpy as np
    import concourse.bacc as bacc
    from concourse.bass_utils import run_bass_kernel_spmd

    nc = bacc.Bacc("TRN2", target_bir_lowering=False, num_devices=1)
    v = {n: np.asarray(a) for n, a in inputs.items()}

    def rows(a):
        return a.reshape(-1, P, a.shape[-1]).transpose(1, 0, 2)

    wo = v["L1_attn_Wo"].reshape(HKV, G, DH, D)
    wo_pad = np.zeros((HKV, 32, G, D), wo.dtype)
    wo_pad[:, :DH] = wo.transpose(0, 2, 1, 3)
    up = v["L1_ffn_w_up"].transpose(1, 0, 2)
    x = v["L0_attn_x"].reshape(TOK, D)
    laid = {
        "x": rows(x), "xT": rows(x.T),
        "w_in": rows(v["L0_attn_in_proj_w"].T), "b_in": v["L0_attn_in_proj_b"].reshape(CH, P).T,
        "short_w": v["L0_attn_short_w"].reshape(CH, P, 3).transpose(1, 2, 0),
        "short_b": v["L0_attn_short_b"].reshape(CH, P).T,
        "mlp_w0": v["L0_attn_mlp_w0"].T, "mlp_b0": v["L0_attn_mlp_b0"][:, None], "freq": v["L0_attn_sin_freq"].T,
        "mlp_w1": v["L0_attn_mlp_w1"].T, "mlp_b1": v["L0_attn_mlp_b1"][:, None],
        "mlp_w2": v["L0_attn_mlp_w2"].T, "mlp_b2": v["L0_attn_mlp_b2"][:, None],
        "mlp_w3": v["L0_attn_mlp_w3"].T, "filter_bias": v["L0_attn_filter_bias"][None, :],
        "w_out": rows(v["L0_attn_out_proj_w"].T), "b_out": np.broadcast_to(v["L0_attn_out_proj_b"], (P, D)),
        "w1": rows(v["L0_ffn_W1"].T), "w3": rows(v["L0_ffn_W3"].T), "w2": rows(v["L0_ffn_W2"].T),
        "wqv": rows(np.concatenate([v["L1_attn_Wq"], v["L1_attn_Wv"]], axis=1)),
        "wo": wo_pad.reshape(P, G, D), "wgate": rows(v["L1_ffn_w_gate"]),
        "ws_up": rows(v["L1_ffn_w_shared_up"]), "ws_down": v["L1_ffn_w_shared_down"],
        "we_gate": rows(up[:, :, :EH].reshape(D, E * EH)), "we_val": rows(up[:, :, EH:].reshape(D, E * EH)),
        "we_down": rows(v["L1_ffn_w_down"].reshape(E * EH, D)),
    }

    t, k = np.arange(P, dtype=np.float64), np.arange(P, dtype=np.float64) + 0.5
    angle = 2 * np.pi / L * t[:, None] * k[None, :]
    wide = 2 * np.pi / L * (t[:, None] - P) * k[None, :]
    n = np.arange(P)
    had = np.ones((1, 1))
    while had.shape[0] < P:
        had = np.block([[had, had], [had, -had]])
    square = {
        "ident": np.eye(P), "cos_t": np.cos(angle), "msin_t": -np.sin(angle), "cos_w": np.cos(wide),
        "msin_w": -np.sin(wide), "icos": np.cos(angle).T / P, "imsin": -np.sin(angle).T / P,
        "sumsel": (n[:, None] % 32 == DH) & (n[:, None] // 32 == n[None, :] // 32),
        "tri": n[:, None] < n[None, :], "ones": np.ones((P, P)),
        "had": had / (2 * math.sqrt(HID)),
    }
    pos = np.linspace(0.0, 1.0, L, dtype=np.float32)
    ang = np.float32(0.0001) * (np.float32(2 * math.pi) * np.linspace(0.0, L - 1.0, L, dtype=np.float32) / L)
    deltas = np.abs(np.linspace(math.log(0.01) / 1.5, math.log(0.01) / 0.3, D, dtype=np.float32))
    laid["mats"] = np.stack([square[m] for m in MATS]).astype(np.float32)
    laid["pos_emb"] = np.stack([pos, np.cos(ang), -np.sin(ang)]).astype(np.float32)
    laid["decay"] = rows(np.exp(-pos[:, None] * deltas[None, :]).astype(np.float32))
    e = np.arange(E)[:, None, None]
    laid["expert_sel"] = (e == EPT * np.arange(ET)[None, :, None] + n[None, None, :] // EH).astype(np.float32)

    order = ["x", "xT", "w_in", "b_in", "short_w", "short_b", "mlp_w0", "mlp_b0", "freq", "mlp_w1", "mlp_b1",
             "mlp_w2", "mlp_b2", "mlp_w3", "filter_bias", "w_out", "b_out", "w1", "w3", "w2", "wqv", "wo", "wgate",
             "ws_up", "ws_down", "we_gate", "we_val", "we_down", "mats", "decay", "pos_emb", "expert_sel"]
    arrays, args = {}, []
    for name in order:
        a = np.ascontiguousarray(laid[name])
        arrays["in_" + name] = a
        args.append(nc.dram_tensor("in_" + name, a.shape, mybir.dt.from_np(a.dtype), kind="ExternalInput").ap())
    out = nc.dram_tensor("out_0", (TOK, D), F32, kind="ExternalOutput").ap()
    mixed_kernel(nc, *args, out.rearrange("(t p) d -> p t d", p=P))
    r = run_bass_kernel_spmd(nc, [arrays], core_ids=[0])
    return r.results[0]["out_0"].reshape(NB, L, D)
```

```python
from contextlib import ExitStack

import concourse.bass as bass
from concourse import mybir

F32 = mybir.dt.float32
F32R = mybir.dt.float32r
BF16 = mybir.dt.bfloat16
ALU = mybir.AluOpType
ACT = mybir.ActivationFunctionType
AX_X = mybir.AxisListType.X

P = 128
NB, L, D = 8, 256, 256
TOK = NB * L
LT = L // P
DT = D // P
CH = 3 * D // P
FO = 64
HID = 1024
HT = HID // P
HQ, HKV, DH = 16, 4, 16
G = HQ // HKV
QV = HQ * DH + HKV * DH
E, EH, HS = 64, 32, 64
TOPK, CAP = 6, 128
EPT = P // EH
ET = E // EPT
LN_EPS = 1e-5
RMS_EPS = 1.1920929e-07
TWO_PI = 6.283185307179586
TWO_PI_HI = 6.28125
TWO_PI_LO = TWO_PI - TWO_PI_HI
PI_SAFE = 3.1415925
ROUND = 12582912.0

EW = 3 * D + P
STAGES = 7
SLOTS = 5

MATS = ["ident", "cos_t", "msin_t", "cos_w", "msin_w", "icos", "imsin", "sumsel", "tri", "ones", "had"]


def mixed_kernel(nc, x, xT, w_in, b_in, short_w, short_b, mlp_w0, mlp_b0, freq, mlp_w1, mlp_b1, mlp_w2, mlp_b2,
                 mlp_w3, filter_bias, w_out, b_out, w1, w3, w2, wqv, wo, wgate,
                 mats, decay, pos_emb, wexp, out):
    with ExitStack() as ctx:
        layers_memory = ExitStack()

        def sb(name, shape, dt=F32):
            return layers_memory.enter_context(nc.sbuf_tensor(name, shape, dt))

        def keep_sb(name, shape, dt=F32):
            return ctx.enter_context(nc.sbuf_tensor(name, shape, dt))

        def sem(name):
            return ctx.enter_context(nc.semaphore(name))

        xtok = keep_sb("xtok", [P, NB * LT, D])
        xT0 = keep_sb("xT0", [P, DT, TOK])
        x3T = xT0
        gateT = keep_sb("gateT", [E, TOK])
        mhalf = keep_sb("mhalf", [P, HQ + HKV])
        ln_eps = keep_sb("ln_eps", [P, LT])
        scratch = keep_sb("scratch", [P, 1])
        stat = {k: keep_sb("stat" + k, [P, LT, 6]) for k in "ABRD"}
        mv = {k: keep_sb("mv" + k, [P, LT, 2]) for k in "ABRD"}
        rstd = {k: keep_sb("rstd" + k, [P, LT]) for k in "ABRD"}

        win = sb("win", [P, DT, 3 * D])
        u = sb("u", [P, CH, L + 2])
        uc = sb("uc", [P, CH, L])
        vT = sb("vT", [P, DT, L])
        vtok, Vr, Vi, Yr, Yi = (sb(n, [P, LT, D]) for n in ("vtok", "Vr", "Vi", "Yr", "Yi"))
        pr = [sb(f"pr{n}", [P, LT, D]) for n in range(4)]
        Kr = sb("Kr", [P, 2, D])
        Ki = sb("Ki", [P, 2, D])
        yx = sb("yx", [P, DT, L])
        lnA, lnA_in = sb("lnA", [P, LT, D]), sb("lnA_in", [P, LT, D])
        wout = sb("wout", [P, DT, D])

        mat = {n: sb("m_" + n, [P, P]) for n in MATS}
        pos_sb = sb("pos_sb", [3, L])
        bin_sb = sb("bin_sb", [P, CH])
        sw = sb("sw", [P, 3, CH])
        sbias = sb("sbias", [P, CH])
        bias2 = sb("bias2", [P, CH])
        m0 = sb("m0", [3, FO])
        m1 = sb("m1", [FO, FO])
        m2 = sb("m2", [FO, FO])
        m3 = sb("m3", [FO, D])
        mb = sb("mb", [FO, 4])
        fb = sb("fb", [1, D])
        bout = sb("bout", [P, D])
        wqv_sb = sb("wqv_sb", [P, DT, QV])
        wo_sb = sb("wo_sb", [P, G, D])
        wg_sb = sb("wg_sb", [P, DT, E])
        rms_eps = sb("rms_eps", [P, HQ + HKV])

        def views(store, *shapes):
            got, at_word = [], 0
            for shape in shapes:
                n = 1
                for d in shape:
                    n *= d
                piece = store[:, at_word:at_word + n]
                dims = " ".join("abc"[:len(shape)])
                if len(shape) > 1:
                    piece = piece.rearrange(f"p ({dims}) -> p {dims}", **dict(zip("abc", shape)))
                got.append(piece)
                at_word += n
            return got

        w1_sb, w3_sb, w2_sb = sb("w1_sb", [P, DT, HID]), sb("w3_sb", [P, DT, HID]), sb("w2_sb", [P, HT, D])
        store_c = sb("store_c", [P, 2 * HT * D])
        w2_tmp, _ = views(store_c, (HT, D), (HT, D))
        prob = views(store_c, (HKV, 2 * L), (HKV, 2 * L))

        arg = sb("arg", [FO, L])
        turns = sb("turns", [FO, L])
        hf = sb("hf", [FO, L])
        x1T = sb("x1T", [P, DT, L])

        th = sb("th", [P, 2, L])
        hT = sb("hT", [P, HT, L])
        lnB, lnB_in = sb("lnB", [P, LT, D]), sb("lnB_in", [P, LT, D])
        decay_sb, taps = lnB, lnB_in
        x2T = sb("x2T", [P, DT, L])

        ms = sb("ms", [P, LT, HQ + HKV])
        rs = sb("rs", [P, LT, HQ + HKV])
        kn = sb("kn", [P, LT, HKV * DH])
        kpad = sb("kpad", [P, LT, HKV, 4, DH])
        vaug = sb("vaug", [P, LT, HKV, 32])
        QT = sb("QT", [P, HKV, 2, L], F32R)
        KT = sb("KT", [P, HKV, L], F32R)
        store_q = sb("store_q", [P, LT * HQ * 4 * DH])
        qpad, = views(store_q, (LT, HQ, 4 * DH))
        yT, rsum = views(store_q, (G, L), (G, L))
        _, sq = views(store_q, (G, L), (LT, QV))
        lnC, lnC_in = sb("lnC", [P, LT, D]), sb("lnC_in", [P, LT, D])
        ssq = sb("ssq", [P, LT])
        rms = sb("rms", [P, LT])
        x3s = sb("x3s", [P, DT, L])
        sc = sb("sc", [P, LT, E])
        rep = sb("rep", [P, LT, E])
        top = sb("top", [P, LT, 8])
        tsum = sb("tsum", [P, LT])
        picked = sb("picked", [P, LT, E], BF16)
        before = sb("before", [P, E], BF16)
        onesb = sb("onesb", [P, P], BF16)
        trib = sb("trib", [P, P], BF16)
        wtok = sb("wtok", [P, LT, P])

        layers_memory.close()
        def d_sb(name, shape, dt=F32):
            return keep_sb("mix_" + name, shape, dt)

        stage = d_sb("stage", [P, STAGES, EW])
        whi = d_sb("whi", [P, ET + 1, EW], F32R)
        wlo = d_sb("wlo", [P, ET + 1, 3 * D], F32R)
        xhi = d_sb("xhi", [P, DT, L], F32R)
        xlo = d_sb("xlo", [P, DT, L], F32R)
        ghl = d_sb("ghl", [P, L], F32R)
        dth = d_sb("dth", [P, SLOTS, L])
        dh = d_sb("dh", [P, SLOTS, L])
        hhi = d_sb("hhi", [P, SLOTS, L], F32R)
        hlo = d_sb("hlo", [P, SLOTS, L], F32R)
        lnD, lnD_in = d_sb("lnD", [P, LT, D]), d_sb("lnD_in", [P, LT, D])

        ps = ctx.enter_context(nc.psum_tensor("ps", [P, 8, 512], F32))
        bank = [ps[:, n, :] for n in range(8)]

        s_mat, s_filt, s_wa, s_x, s_xT, s_wb, s_w2l, s_wc = (sem("s_" + n) for n in (
            "mat", "filt", "wa", "x", "xT", "wb", "w2l", "wc"))
        s_stage = [sem(f"s_stage{n}") for n in range(STAGES)]
        s_out = sem("s_out")
        i_dve, i_pool, i_pe, i_act = (sem("i_" + n) for n in ("dve", "pool", "pe", "act"))
        i_w2 = sem("i_w2")
        i_w2pe = sem("i_w2pe")
        i_w2done = sem("i_w2done")
        i_ready = sem("i_ready")
        i_bias2 = sem("i_bias2")
        i_pads = sem("i_pads")
        i_bout = sem("i_bout")
        names = """a_full a_free a_u a_conv a_vT a_vtok a_Vr a_Yr a_Yi a_yx a_ln a_x1T a_dve a_pool a_var a_rstd a_kept a_Vi a_pool2
                   b_full b_free b_th b_g b_h b_ln b_x2T b_dve b_pool b_var b_rstd b_kept
                   c_qv c_sq c_ms c_rs c_q c_v c_qt c_qtc c_s c_p c_pv c_y c_den c_ssum c_yn c_wo c_ss c_rms c_wod c_tr c_x3
                   c_dve c_pool r_pool r_var r_rstd r_kept r_ln c_lg c_sc c_pick c_pos c_posd c_w c_wtr c_gateT c_before c_cnt c_ql r_dve
                   d_full d_th d_g d_dve d_h d_hh d_hl d_down d_xh d_x d_wh d_w d_accd d_pool d_var d_rstd d_ln d_stat""".split()
        S = {n: sem(n) for n in names}

        class Chain:

            def __init__(self, eng, s, per=None):
                self.eng, self.s, self.per, self.n = eng, s, per, 0

            def begin(self, b):
                if self.n and self.per is None:
                    self.per = self.n
                self.b, self.n = b, 0

            def link(self, ins):
                self.n += 1
                ins.then_inc(self.s, 1)

            def settle(self):
                self.eng.wait_ge(self.s, self.n if self.per is None else self.b * self.per + self.n)

        def at(eng, name, b, k, per):
            eng.wait_ge(S[name], b * per + k)

        def ago(eng, name, b, k, per):
            if not (isinstance(b, int) and b == 0):
                eng.wait_ge(S[name], (b - 1) * per + k)

        def hold():
            nc.vector.memset(scratch[:, :], 0.0)

        def tiles(b):
            return bass.ds(b * LT, LT)

        def toks(b):
            return bass.ds(b * L, L)

        def halves(t):
            return t.rearrange("p (a n) -> p a n", a=2)

        ORDER = """B.up0 R.ln1 A.u0 C.qv R.ln2 B.up1 R.tr A.u1 B.up2 R.logit B.up3 C.q A.u2 B.up4 C.qt A.vT R.route
                   B.up5 A.real B.up6 A.imag B.up7 C.s0 B.down0 C.s1 A.back C.s2 A.out A.ln1 C.s3 C.s4 A.ln2 A.tr
                   C.den B.down1 B.ln1 R.pos C.out C.square B.ln2 B.tr R.weight""".split()

        def layers(eng, steps):
            def turn(a, b, c, r):
                for step in ORDER:
                    n = {"A": a, "B": b, "C": c, "R": r}[step[0]]
                    if n is not None and step in steps:
                        steps[step](n)

            turn(0, None, None, None)
            turn(1, 0, None, None)
            turn(2, 1, 0, None)
            turn(3, 2, 1, 0)
            with eng.Fori(4, NB) as i:
                turn(i, i - 1, i - 2, i - 3)
            turn(None, NB - 1, NB - 2, NB - 3)
            turn(None, None, NB - 1, NB - 2)
            turn(None, None, None, NB - 1)

        TILES = ET + 1

        def slot(j):
            return j % (SLOTS - 1) if j < ET else SLOTS - 1

        def layers_through(eng):
            at(eng, "c_gateT", NB - 1, 1, 1)
            at(eng, "c_w", NB - 1, 1, 1)
            at(eng, "r_kept", NB - 1, 1, 1)
            at(eng, "c_before", NB - 1, 1, 1)

        def each_batch(eng, step):
            step(0)
            with eng.Fori(1, NB) as b:
                step(b)

        def at_first(b):
            return isinstance(b, int) and b == 0

        def h_free(eng, b, j):
            if j == ET:
                ago(eng, "d_down", b, TILES, TILES)
            elif j < SLOTS - 1:
                ago(eng, "d_down", b, j + ET - SLOTS + 2, TILES)
            else:
                at(eng, "d_down", b, j - SLOTS + 2, TILES)

        block = ctx.enter_context(nc.Block())

        @block.sync
        def _(sp):
            for n, name in enumerate(MATS):
                sp.dma_start(mat[name][:, :], mats[n]).then_inc(s_mat, 16)
            for dst, src in ((pos_sb[:, :], pos_emb), (m0[:, :], mlp_w0), (m1[:, :], mlp_w1), (m2[:, :], mlp_w2),
                             (m3[:, :], mlp_w3), (mb[:, 0:1], mlp_b0), (mb[:, 1:2], mlp_b1), (mb[:, 2:3], mlp_b2),
                             (mb[:, 3:4], freq), (fb[:, :], filter_bias), (decay_sb[:, :, :], decay)):
                sp.dma_start(dst, src).then_inc(s_filt, 16)
            sp.dma_start(w2_sb[:, :, :], w2).then_inc(s_w2l, 16)
            for dst, src in ((w1_sb, w1), (w3_sb, w3)):
                sp.dma_start(dst[:, :, :], src).then_inc(s_wb, 16)
            for dst, src in ((wqv_sb[:, :, :], wqv), (wo_sb[:, :, :], wo), (wg_sb[:, :, :], wgate)):
                sp.dma_start(dst, src).then_inc(s_wc, 16)
            at(sp, "a_full", NB - 1, 9, 9)
            at(sp, "a_kept", NB - 1, 1, 1)
            for j in range(TILES):
                if j >= STAGES:
                    sp.wait_ge(S["d_w"], j - STAGES + 1)
                sp.dma_start(stage[:, j % STAGES, :], wexp[j]).then_inc(s_stage[j % STAGES], 16)
            with sp.Fori(0, NB) as b:
                at(sp, "d_ln", b, 2, 2)
                sp.dma_start(out[:, tiles(b), :], lnD[:, :, :]).then_inc(s_out, 16)
            sp.wait_ge(s_out, 16 * (NB + 1))

        @block.scalar
        def _(act):
            act.dma_start(xT0[:, :, :], xT).then_inc(s_xT, 16)
            for dst, src in ((win[:, :, :], w_in), (bin_sb[:, :], b_in), (sw[:, :, :], short_w),
                             (sbias[:, :], short_b), (wout[:, :, :], w_out), (bout[:, :], b_out)):
                act.dma_start(dst, src).then_inc(s_wa, 16)
            act.dma_start(xtok[:, :, :], x).then_inc(s_x, 16)
            for k in range(3):
                act.wait_ge(i_dve, 6 * (k + 1))
                nc.scalar.activation(hf[:, :], arg[:, :], ACT.Sin).then_inc(i_act, 1)
            act.wait_ge(i_bias2, 2)

            def a_u(b, part):
                at(act, "a_full", b, part + 1, 9)
                ago(act, "a_yx" if part == 2 else "a_vT", b, 1, 1)
                for q in range(2):
                    m = 4 - 2 * part + q
                    nc.scalar.activation(u[:, m, 2:L + 2], halves(bank[0])[:, q, :], ACT.Identity,
                                         bias=bin_sb[:, m:m + 1])
                    last = nc.scalar.activation(uc[:, m, :], halves(bank[0])[:, q, :], ACT.Identity,
                                                bias=bias2[:, m:m + 1], scale=sw[:, 2, m:m + 1])
                last.then_inc(S["a_u"], 1)

            def a_vtok(b):
                at(act, "a_full", b, 4, 9)
                nc.scalar.activation(vtok[:, :, :], halves(bank[0]), ACT.Copy).then_inc(S["a_vtok"], 1)

            def a_spec(b, k):
                at(act, "a_full", b, 5 + k, 9)
                ago(act, "a_Yr", b, 1, 1)
                ago(act, "a_Yi", b, 1, 1)
                nc.scalar.activation((Vr, Vi)[k][:, :, :], halves(bank[0]), ACT.Copy)\
                    .then_inc(S[("a_Vr", "a_Vi")[k]], 1)

            def a_x1T(b):
                at(act, "a_full", b, 9, 9)
                ago(act, "b_full", b, 8, 10)
                nc.scalar.activation(x1T[:, :, :], halves(bank[0]), ACT.Copy).then_inc(S["a_x1T"], 1)

            def b_th(b, h):
                at(act, "b_full", b, h + 1, 10)
                if h >= 2:
                    at(act, "b_g", b, h - 1, 8)
                else:
                    ago(act, "b_g", b, h + 7, 8)
                nc.scalar.activation(th[:, h % 2, :], bank[1 + h % 2][:, 0:L], ACT.Tanh, scale=0.5)\
                    .then_inc(S["b_th"], 1)

            def b_x2T(b):
                at(act, "b_full", b, 10, 10)
                ago(act, "c_qv", b, 1, 1)
                nc.scalar.activation(x2T[:, :, :], halves(bank[2]), ACT.Copy).then_inc(S["b_x2T"], 1)

            def c_sq(b):
                at(act, "c_qv", b, 1, 1)
                ago(act, "c_ssum", b, 1, 1)
                for t in range(LT):
                    last = nc.scalar.activation(sq[:, t, :], bank[3 + t][:, 0:QV], ACT.Square, scale=DH ** -0.5)
                last.then_inc(S["c_sq"], 1)
                ago(act, "c_pv", b, 4, 4)
                act.wait_ge(i_pads, 1)
                for t in range(LT):
                    last = nc.scalar.activation(vaug[:, t, :, 0:DH],
                                                bank[3 + t][:, HQ * DH:QV].rearrange("p (h d) -> p h d", h=HKV),
                                                ACT.Copy)
                last.then_inc(S["c_v"], 1)

            def c_qtc(b):
                at(act, "c_qt", b, 1, 1)
                ago(act, "c_s", b, 4, 4)
                for h in range(HKV):
                    nc.scalar.activation(QT[:, h, :, :], halves(bank[3 + h]), ACT.Copy)
                for odd in range(2):
                    for r in (slice(0, 64), slice(64, 128)):
                        last = nc.scalar.activation(KT[r, odd::2, :], halves(bank[7])[64 * odd:64 * odd + 64], ACT.Copy)
                last.then_inc(S["c_qtc"], 1)

            def c_exp(b, n):
                at(act, "c_s", b, n + 1, 4)
                if n >= 2:
                    at(act, "c_pv", b, n - 1, 4)
                else:
                    ago(act, "c_pv", b, n + 3, 4)
                for h in range(0, HKV, 2):
                    last = nc.scalar.activation(prob[n % 2][:, h:h + 2, :], ps[:, 3 + h:5 + h, :], ACT.Exp)
                last.then_inc(S["c_p"], 1)

            def c_ss(b):
                at(act, "c_wo", b, 1, 1)
                at(act, "c_ms", b, 1, 1)
                for t in range(LT):
                    last = nc.scalar.activation(sq[:, t, 0:D], halves(bank[5])[:, t, :], ACT.Square,
                                                scale=D ** -0.5)
                last.then_inc(S["c_ss"], 1)

            def c_x3(b):
                at(act, "c_tr", b, 1, 1)
                nc.scalar.activation(x3s[:, :, :], halves(bank[5]), ACT.Copy)
                nc.scalar.activation(x3T[:, :, toks(b)], halves(bank[5]), ACT.Copy).then_inc(S["c_x3"], 1)

            def c_sc(b):
                at(act, "c_lg", b, 1, 1)
                ago(act, "c_pick", b, 1, 1)
                nc.scalar.activation(rep[:, :, :], bank[6][:, 0:LT * E].rearrange("p (t e) -> p t e", t=LT),
                                     ACT.Tanh, scale=0.5).then_inc(S["c_sc"], 1)

            def c_gateT(b):
                at(act, "c_wtr", b, 1, 1)
                nc.scalar.activation(gateT[:, toks(b)], bank[7][0:E, 0:L], ACT.Copy).then_inc(S["c_gateT"], 1)

            layers(act, {"A.u0": lambda b: a_u(b, 0), "A.u1": lambda b: a_u(b, 1), "A.u2": lambda b: a_u(b, 2),
                         "A.vT": a_vtok, "A.real": lambda b: a_spec(b, 0), "A.imag": lambda b: a_spec(b, 1),
                         "A.tr": a_x1T, "B.tr": b_x2T, "C.qv": c_sq, "C.qt": c_qtc, "C.square": c_ss,
                         "R.tr": c_x3, "R.logit": c_sc, "R.weight": c_gateT,
                         **{f"B.up{h}": lambda b, h=h: b_th(b, h) for h in range(HT)},
                         **{f"C.s{n}": lambda b, n=n: c_exp(b, n) for n in range(4)}})

            layers_through(act)

            def d_split_w(j):
                act.wait_ge(s_stage[j % STAGES], 16 * (j // STAGES + 1))
                nc.scalar.activation(whi[:, j, :], stage[:, j % STAGES, :], ACT.Copy).then_inc(S["d_wh"], 1)

            def d_xhi(b):
                if not at_first(b):
                    at(act, "d_full", b - 1, TILES, TILES)
                nc.scalar.activation(ghl[0:E, :], gateT[:, toks(b)], ACT.Copy)
                nc.scalar.activation(xhi[:, :, :], x3T[:, :, toks(b)], ACT.Copy).then_inc(S["d_xh"], 1)

            def d_tanh(b, j):
                at(act, "d_full", b, j + 1, TILES)
                if j < SLOTS - 1 or j == ET:
                    ago(act, "d_g", b, j + ET - SLOTS + 2 if j < ET else TILES, TILES)
                else:
                    at(act, "d_g", b, j - SLOTS + 2, TILES)
                g = halves(bank[2 * (j % 2)] if j < ET else bank[7])[:, 0, :]
                nc.scalar.activation(dth[:, slot(j), :], g, ACT.Tanh, scale=0.5).then_inc(S["d_th"], 1)

            def d_hhi(b, j):
                at(act, "d_h", b, j + 1, TILES)
                h_free(act, b, j)
                nc.scalar.activation(hhi[:, slot(j), :], dh[:, slot(j), :], ACT.Copy).then_inc(S["d_hh"], 1)

            def d_act(b):
                if at_first(b):
                    d_split_w(0)
                d_xhi(b)
                if at_first(b):
                    d_split_w(1)
                    d_split_w(2)
                else:
                    d_tanh(b - 1, ET)
                    d_hhi(b - 1, ET - 1)
                for j in range(ET):
                    d_tanh(b, j)
                    if j:
                        d_hhi(b, j - 1)
                    elif not at_first(b):
                        d_hhi(b - 1, ET)
                    if at_first(b) and j + 3 < TILES:
                        d_split_w(j + 3)

            each_batch(act, d_act)
            d_tanh(NB - 1, ET)
            d_hhi(NB - 1, ET - 1)
            d_hhi(NB - 1, ET)

        @block.tensor
        def _(pe):
            mm, tr = nc.tensor.matmul, nc.tensor.transpose
            ident = mat["ident"]
            pe.wait_ge(s_mat, 16 * len(MATS))
            pe.wait_ge(s_filt, 16 * 11)
            mm(bank[0][0:FO, 0:L], m0[:, :], pos_sb[:, :], start=True, stop=True).then_inc(i_pe, 1)
            pe.wait_ge(i_act, 1)
            mm(bank[0][0:FO, 0:L], m1[:, :], hf[:, :], start=True, stop=True).then_inc(i_pe, 1)
            pe.wait_ge(i_act, 2)
            mm(bank[0][0:FO, 0:L], m2[:, :], hf[:, :], start=True, stop=True).then_inc(i_pe, 1)
            pe.wait_ge(i_act, 3)
            for t in range(LT):
                last = mm(halves(bank[0])[:, t, :], hf[:, t * P:(t + 1) * P], m3[:, :], start=True, stop=True)
            last.then_inc(i_pe, 1)
            pe.wait_ge(i_dve, 20)
            for k, (first, wide) in enumerate((("cos_t", "cos_w"), ("msin_t", "msin_w"))):
                view = halves(bank[1 + k])
                mm(view[:, 0, :], mat[first][:, :], taps[:, 0, :], start=True, stop=True)
                mm(view[:, 1, :], mat[first][:, :], taps[:, 1, :], start=True, stop=False)
                last = mm(view[:, 1, :], mat[wide][:, :], taps[:, 0, :], start=False, stop=True)
            last.then_inc(i_pe, 1)
            pe.wait_ge(i_w2, 6)
            for q in range(HT // 2):
                mm(bank[4 + q][:, :], mat["had"][:, :], w2_tmp[:, 2 * q:2 * q + 2, :].rearrange("p a d -> p (a d)"),
                   start=True, stop=True).then_inc(i_w2pe, 1)
            pe.wait_ge(s_xT, 16)
            pe.wait_ge(s_wa, 16 * 6)
            pe.wait_ge(i_ready, 1)

            def a_u(b, part):
                a_wait(b, part)
                for q in range(2):
                    m = 4 - 2 * part + q
                    for c in range(DT):
                        last = mm(halves(bank[0])[:, q, :], win[:, c, m * P:(m + 1) * P], xT0[:, c, toks(b)],
                                  start=c == 0, stop=c == DT - 1)
                last.then_inc(S["a_full"], 1)

            def a_wait(b, k):
                name, n, per = (("a_x1T", 1, 1), ("a_u", 1, 3), ("a_u", 2, 3), ("a_u", 3, 3), ("a_vtok", 1, 1),
                                ("a_Vr", 1, 1), ("a_Vi", 1, 1), ("a_yx", 1, 1), ("a_free", 1, 1))[k]
                (ago if k == 0 else at)(pe, name, b, n, per)

            def a_vT(b):
                a_wait(b, 3)
                at(pe, "a_vT", b, 1, 1)
                for t in range(LT):
                    for m in range(DT):
                        last = tr(halves(bank[0])[:, t, m * P:(m + 1) * P], vT[:, m, t * P:(t + 1) * P], ident[:, :])
                last.then_inc(S["a_full"], 1)

            def a_dft(b, k):
                a_wait(b, 4 + k)
                at(pe, "a_vtok", b, 1, 1)
                last = mm(bank[0][:, :], mat[("cos_t", "msin_t")[k]][:, :],
                          vtok[:, :, :].rearrange("p t d -> p (t d)"), start=True, stop=True)
                last.then_inc(S["a_full"], 1)

            def a_idft(b):
                a_wait(b, 6)
                at(pe, "a_Yr", b, 1, 1)
                at(pe, "a_Yi", b, 1, 1)
                for m in range(DT):
                    for t in range(LT):
                        o = halves(bank[0])[:, m, t * P:(t + 1) * P]
                        mm(o, Yr[:, t, m * P:(m + 1) * P], mat["icos"][:, :], start=True, stop=False)
                        last = mm(o, Yi[:, t, m * P:(m + 1) * P], mat["imsin"][:, :], start=False, stop=True)
                last.then_inc(S["a_full"], 1)

            def a_out(b):
                a_wait(b, 7)
                at(pe, "a_yx", b, 1, 1)
                for t in range(LT):
                    for m in range(DT):
                        last = mm(halves(bank[0])[:, t, :], yx[:, m, t * P:(t + 1) * P], wout[:, m, :],
                                  start=m == 0, stop=m == DT - 1)
                last.then_inc(S["a_full"], 1)

            def turn_rows(dst, src):
                for m in range(DT):
                    for t in range(LT):
                        last = tr(halves(dst)[:, m, t * P:(t + 1) * P], src[:, t, m * P:(m + 1) * P], ident[:, :])
                return last

            def a_tr(b):
                a_wait(b, 8)
                at(pe, "a_ln", b, 2, 2)
                turn_rows(bank[0], lnA).then_inc(S["a_full"], 1)

            def b_up(b, h):
                if h == 0:
                    at(pe, "a_x1T", b, 1, 1)
                if h >= 2:
                    at(pe, "b_h", b, h - 1, 8)
                elif h == 0:
                    ago(pe, "b_free", b, 1, 1)
                else:
                    ago(pe, "b_x2T", b, 1, 1)
                for q, w in enumerate((w1_sb, w3_sb)):
                    for c in range(DT):
                        last = mm(halves(bank[1 + h % 2])[:, q, :], w[:, c, h * P:(h + 1) * P], x1T[:, c, :],
                                  start=c == 0, stop=c == DT - 1)
                last.then_inc(S["b_full"], 1)

            def b_down(b, t):
                at(pe, "b_h", b, HT, 8)
                if t == 0 and isinstance(b, int) and b == 0:
                    pe.wait_ge(i_w2done, 1)
                for h in range(HT):
                    last = mm(halves(bank[1])[:, t, :], hT[:, h, t * P:(t + 1) * P], w2_sb[:, h, :],
                              start=h == 0, stop=h == HT - 1)
                if t == LT - 1:
                    last.then_inc(S["b_full"], 1)

            def b_tr(b):
                at(pe, "b_h", b, HT, 8)
                at(pe, "b_ln", b, 2, 2)
                turn_rows(bank[2], lnB).then_inc(S["b_full"], 1)

            def c_qv(b):
                at(pe, "b_x2T", b, 1, 1)
                ago(pe, "c_yn", b, 1, 1)
                for t in range(LT):
                    for c in range(DT):
                        last = mm(bank[3 + t][:, 0:QV], x2T[:, c, t * P:(t + 1) * P], wqv_sb[:, c, :],
                                  start=c == 0, stop=c == DT - 1)
                last.then_inc(S["c_qv"], 1)

            def c_qt(b):
                at(pe, "c_q", b, 1, 1)
                at(pe, "c_v", b, 1, 1)
                ago(pe, "c_sc", b, 1, 1)
                if not isinstance(b, int) or b >= 2:
                    at(pe, "c_gateT", b, -1, 1)
                for n in range(HQ // 2):
                    for t in range(LT):
                        tr(halves(bank[3 + n // 2])[:, n % 2, t * P:(t + 1) * P],
                           qpad[:, t, 2 * n:2 * n + 2, :].rearrange("p h s -> p (h s)"), ident[:, :])
                for p in range(2):
                    for t in range(LT):
                        last = tr(halves(bank[7])[:, p, t * P:(t + 1) * P],
                                  kpad[:, t, 2 * p:2 * p + 2, :, :].rearrange("p h s d -> p (h s d)"), ident[:, :])
                last.then_inc(S["c_qt"], 1)

            def c_s(b, n):
                if n == 0:
                    at(pe, "c_qtc", b, 1, 1)
                    at(pe, "c_ql", b, 1, 1)
                else:
                    at(pe, "c_p", b, n, 4)
                odd, t = n // 2, n % 2
                r = slice(64 * odd, 64 * odd + 64)
                for h in range(HKV):
                    last = mm(bank[3 + h][:, :], KT[r, h, t * P:(t + 1) * P],
                              QT[r, h, :, :].rearrange("p g n -> p (g n)"), start=True, stop=True)
                last.then_inc(S["c_s"], 1)

            def c_pv(b, n):
                at(pe, "c_p", b, n + 1, 4)
                if n == 2:
                    at(pe, "c_y", b, 1, 2)
                for h in range(HKV):
                    last = mm(bank[7][32 * h:32 * h + 32, :], vaug[:, n % 2, h, :], prob[n % 2][:, h, :],
                              start=n % 2 == 0, stop=n % 2 == 1, skip_group_check=True)
                last.then_inc(S["c_pv"], 1)

            def c_den(b):
                at(pe, "c_y", b, 2, 2)
                for p in range(2):
                    last = mm(bank[3 + p][:, :], mat["sumsel"][:, :],
                              yT[:, 2 * p:2 * p + 2, :].rearrange("p g n -> p (g n)"), start=True, stop=True)
                last.then_inc(S["c_den"], 1)

            def c_wo(b):
                at(pe, "c_yn", b, 1, 1)
                at(pe, "c_p", b, 4, 4)
                for t in range(LT):
                    for g in range(G):
                        last = mm(halves(bank[5])[:, t, :], yT[:, g, t * P:(t + 1) * P], wo_sb[:, g, :],
                                  start=g == 0, stop=g == G - 1)
                last.then_inc(S["c_wo"], 1)

            def c_tr(b):
                at(pe, "r_ln", b, 2, 2)
                at(pe, "c_wod", b, 1, 1)
                turn_rows(bank[5], lnC).then_inc(S["c_tr"], 1)

            def c_lg(b):
                at(pe, "c_x3", b, 1, 1)
                for t in range(LT):
                    for c in range(DT):
                        last = mm(bank[6][:, t * E:(t + 1) * E], x3s[:, c, t * P:(t + 1) * P], wg_sb[:, c, :],
                                  start=c == 0, stop=c == DT - 1)
                last.then_inc(S["c_lg"], 1)

            def c_pos(b):
                at(pe, "c_pick", b, 1, 1)
                at(pe, "c_y", b, 2, 2)
                ago(pe, "c_before", b, 1, 1)
                if isinstance(b, int) and b == 0:
                    pe.wait_ge(i_pads, 1)
                mm(bank[7][:, 0:E], trib[:, :], picked[:, 0, :], start=True, stop=False)
                mm(bank[7][:, 0:E], onesb[:, :], before[:, :], start=False, stop=True)
                mm(bank[7][:, E:2 * E], trib[:, :], picked[:, 1, :], start=True, stop=False)
                mm(bank[7][:, E:2 * E], onesb[:, :], picked[:, 0, :], start=False, stop=False)
                mm(bank[7][:, E:2 * E], onesb[:, :], before[:, :], start=False, stop=True).then_inc(S["c_pos"], 1)

            def c_wtr(b):
                at(pe, "c_w", b, 1, 1)
                for t in range(LT):
                    last = tr(bank[7][:, t * P:(t + 1) * P], wtok[:, t, :], ident[:, :])
                last.then_inc(S["c_wtr"], 1)

            pe.wait_ge(s_wb, 32)
            pe.wait_ge(s_wc, 48)

            def s_then_pv(n):
                def step(b):
                    if n < 4:
                        c_s(b, n)
                    if n:
                        c_pv(b, n - 1)
                return step

            layers(pe, {"A.u0": lambda b: a_u(b, 0), "A.u1": lambda b: a_u(b, 1), "A.u2": lambda b: a_u(b, 2),
                        "A.vT": a_vT, "A.real": lambda b: a_dft(b, 0), "A.imag": lambda b: a_dft(b, 1),
                        "A.back": a_idft, "A.out": a_out, "A.tr": a_tr,
                        "B.down0": lambda b: b_down(b, 0), "B.down1": lambda b: b_down(b, 1), "B.tr": b_tr,
                        "C.qv": c_qv, "C.qt": c_qt, "C.den": c_den, "C.out": c_wo,
                        "R.tr": c_tr, "R.logit": c_lg, "R.pos": c_pos, "R.weight": c_wtr,
                        **{f"B.up{h}": lambda b, h=h: b_up(b, h) for h in range(HT)},
                        **{f"C.s{n}": s_then_pv(n) for n in range(5)}})

            layers_through(pe)

            def up(b, j):
                if at_first(b):
                    pe.wait_ge(S["d_w"], j + 1)
                if j == 0:
                    at(pe, "d_x", b, 1, 1)
                if j == ET:
                    ago(pe, "d_h", b, TILES, TILES)
                elif j >= 2:
                    at(pe, "d_h", b, j - 1, TILES)
                else:
                    ago(pe, "d_h", b, ET - 1 + j, TILES)
                o = halves(bank[2 * (j % 2)] if j < ET else bank[7])
                for q in range(2):
                    for c in range(DT):
                        cols = slice(q * D + c * P, q * D + (c + 1) * P)
                        for n, (w, v) in enumerate(((wlo, xhi), (whi, xhi), (whi, xlo))):
                            last = mm(o[:, q, :], w[:, j, cols], v[:, c, :], start=c + n == 0,
                                      stop=c == DT - 1 and n == 2)
                if j < ET:
                    last = mm(bank[1 + 2 * (j % 2)][:, 0:L], whi[:, j, 3 * D:EW], ghl[:, :], start=True, stop=True)
                last.then_inc(S["d_full"], 1)

            def down(b, j):
                at(pe, "d_hh", b, j + 1, TILES)
                at(pe, "d_hl", b, j + 1, TILES)
                if j == 0:
                    ago(pe, "d_accd", b, 1, 1)
                for t in range(LT):
                    rows = slice(t * P, (t + 1) * P)
                    for n, (h, w) in enumerate(((hhi, whi), (hhi, wlo), (hlo, whi))):
                        last = mm(bank[4 + t][:, 0:D], h[:, slot(j), rows], w[:, j, 2 * D:3 * D],
                                  start=j + n == 0, stop=j == ET and n == 2)
                last.then_inc(S["d_down"], 1)

            def d_pe(b):
                if not at_first(b):
                    down(b - 1, ET - 3)
                    down(b - 1, ET - 2)
                for j in range(ET):
                    if j >= 3:
                        down(b, j - 3)
                    elif j and not at_first(b):
                        down(b - 1, ET - 2 + j)
                    up(b, j)
                up(b, ET)

            each_batch(pe, d_pe)
            for j in range(ET - 3, TILES):
                down(NB - 1, j)

        @block.vector
        def _(dve):
            V = nc.vector
            setup = Chain(dve, i_dve)
            setup.begin(0)
            dve.wait_ge(s_filt, 16 * 11)
            for k in range(3):
                dve.wait_ge(i_pe, k + 1)
                setup.link(V.tensor_scalar(arg[:, :], bank[0][0:FO, 0:L], mb[:, k:k + 1], mb[:, 3:4],
                                           ALU.add, ALU.mult))
                setup.settle()
                setup.link(V.tensor_scalar(turns[:, :], arg[:, :], 1.0 / TWO_PI, ROUND, ALU.mult, ALU.add))
                setup.settle()
                setup.link(V.tensor_scalar(turns[:, :], turns[:, :], ROUND, None, ALU.subtract))
                setup.settle()
                for part in (TWO_PI_HI, TWO_PI_LO):
                    setup.link(V.scalar_tensor_tensor(out=arg[:, :], in0=turns[:, :], scalar=-part,
                                                      in1=arg[:, :], op0=ALU.mult, op1=ALU.add))
                    setup.settle()
                setup.link(V.tensor_scalar(arg[:, :], arg[:, :], PI_SAFE, -PI_SAFE, ALU.min, ALU.max))
            dve.wait_ge(i_pe, 4)
            setup.link(V.tensor_tensor(taps[:, :, :], halves(bank[0]), decay_sb[:, :, :], ALU.mult))
            setup.settle()
            setup.link(V.tensor_tensor(taps[0:1, 0, :], taps[0:1, 0, :], fb[:, :], ALU.add))
            dve.wait_ge(i_pe, 5)
            setup.link(V.tensor_copy(Kr[:, :, :], halves(bank[1])))
            setup.link(V.tensor_copy(Ki[:, :, :], halves(bank[2])))
            setup.settle()
            dve.wait_ge(s_wa, 16 * 6)
            setup.link(V.tensor_tensor(bias2[:, :], bin_sb[:, :], sw[:, 2, :], ALU.mult))
            setup.settle()
            V.tensor_tensor(bias2[:, :], bias2[:, :], sbias[:, :], ALU.add).then_inc(i_bias2, 1)
            V.memset(u[:, :, 0:2], 0.0).then_inc(i_bias2, 1)
            dve.wait_ge(i_bias2, 2)
            for q in range(HT // 2):
                dve.wait_ge(i_w2pe, q + 1)
                last = V.tensor_copy(w2_sb[:, 2 * q:2 * q + 2, :], halves(bank[4 + q]))
            last.then_inc(i_w2done, 1)
            dve.wait_ge(i_w2done, 1)
            V.memset(scratch[:, :], 0.0).then_inc(i_ready, 1)
            dve.wait_ge(s_x, 16)
            dve.wait_ge(i_pads, 1)
            dve.wait_ge(i_bout, NB * LT)

            chains = {k: Chain(dve, S[k.lower() + "_dve"]) for k in "ABCR"}

            def stats(key, b, rows):
                ch, k = chains[key], key.lower()
                for t in range(LT):
                    ch.link(V.bn_stats(stat[key][:, t, :], rows[:, t, :]))
                ch.settle()
                hold()
                for t in range(LT):
                    last = V.bn_aggr(mv[key][:, t, :], stat[key][:, t, :])
                last.then_inc(S[k + "_var"], 1)

            def norm(key, b, rows, normed):
                k = key.lower()
                at(dve, k + "_rstd", b, 1, 1)
                for t in range(LT):
                    V.tensor_scalar(normed[:, t, :], rows[:, t, :], mv[key][:, t, 0:1], rstd[key][:, t:t + 1],
                                    ALU.subtract, ALU.mult).then_inc(S[k + "_ln"], 1)

            def a_conv(b, part):
                ch = chains["A"]
                if part == 0:
                    ch.begin(b)
                at(dve, "a_u", b, part + 1, 3)
                for q in range(2):
                    m = 4 - 2 * part + q
                    ch.link(V.scalar_tensor_tensor(out=uc[:, m, :], in0=u[:, m, 1:L + 1], scalar=sw[:, 1, m:m + 1],
                                                   in1=uc[:, m, :], op0=ALU.mult, op1=ALU.add))
                ch.settle()
                for q in range(2):
                    m = 4 - 2 * part + q
                    ins = V.scalar_tensor_tensor(out=uc[:, m, :], in0=u[:, m, 0:L], scalar=sw[:, 0, m:m + 1],
                                                 in1=uc[:, m, :], op0=ALU.mult, op1=ALU.add)
                    if q == 0:
                        ch.link(ins)
                ins.then_inc(S["a_conv"], 1)
                if part == 1:
                    ch.settle()
                    at(dve, "a_conv", b, 2, 3)
                    V.tensor_tensor(vT[:, :, :], uc[:, 4:6, :], uc[:, 2:4, :], ALU.mult).then_inc(S["a_vT"], 1)

            def a_Yr(b):
                ch = chains["A"]
                at(dve, "a_Vr", b, 1, 1)
                at(dve, "a_Vi", b, 1, 1)
                ago(dve, "a_full", b, 7, 9)
                for blk in range(2):
                    ch.link(V.tensor_tensor(pr[0][:, blk, :], Kr[:, blk, :], Vr[:, 0, :], ALU.mult))
                    ch.link(V.tensor_tensor(pr[1][:, blk, :], Ki[:, blk, :], Vi[:, 0, :], ALU.mult))
                ch.settle()
                ch.link(V.tensor_tensor(Yr[:, :, :], pr[0][:, :, :], pr[1][:, :, :], ALU.subtract))
                ch.settle()
                ch.link(V.tensor_tensor(pr[0][:, 0, :], Kr[:, 0, :], Vr[:, 1, :], ALU.mult))
                ch.link(V.tensor_tensor(pr[1][:, 0, :], Ki[:, 0, :], Vi[:, 1, :], ALU.mult))
                ch.settle()
                ch.link(V.tensor_tensor(Yr[:, 1, :], Yr[:, 1, :], pr[0][:, 0, :], ALU.add))
                ch.settle()
                V.tensor_tensor(Yr[:, 1, :], Yr[:, 1, :], pr[1][:, 0, :], ALU.subtract).then_inc(S["a_Yr"], 1)

            def a_yx(b):
                at(dve, "a_full", b, 7, 9)
                at(dve, "a_conv", b, 3, 3)
                V.tensor_tensor(yx[:, :, :], halves(bank[0]), uc[:, 0:2, :], ALU.mult).then_inc(S["a_yx"], 1)

            def a_ln(b):
                at(dve, "a_full", b, 8, 9)
                V.tensor_tensor(lnA_in[:, :, :], halves(bank[0]), xtok[:, tiles(b), :],
                                ALU.add).then_inc(S["a_free"], 1)
                at(dve, "a_free", b, 1, 1)
                stats("A", b, lnA_in)

            def a_ln2(b):
                ago(dve, "a_full", b, 9, 9)
                ago(dve, "a_kept", b, 1, 1)
                norm("A", b, lnA_in, lnA)

            def b_h(b, h):
                ch = chains["B"]
                if h == 0:
                    ch.begin(b)
                    ago(dve, "b_full", b, 9, 10)
                at(dve, "b_th", b, h + 1, 8)
                o = halves(bank[1 + h % 2])
                V.scalar_tensor_tensor(out=hT[:, h, :], in0=th[:, h % 2, :], scalar=1.0, in1=o[:, 0, :],
                                       op0=ALU.add, op1=ALU.mult).then_inc(S["b_g"], 1)
                at(dve, "b_g", b, h + 1, 8)
                V.tensor_tensor(hT[:, h, :], hT[:, h, :], o[:, 1, :], ALU.mult).then_inc(S["b_h"], 1)

            def b_ln(b):
                at(dve, "b_full", b, 9, 10)
                at(dve, "a_kept", b, 1, 1)
                V.tensor_tensor(lnB_in[:, :, :], halves(bank[1]), xtok[:, tiles(b), :], ALU.add)\
                    .then_inc(S["b_free"], 1)
                at(dve, "b_free", b, 1, 1)
                stats("B", b, lnB_in)

            def b_ln2(b):
                ago(dve, "b_full", b, 10, 10)
                ago(dve, "b_kept", b, 1, 1)
                norm("B", b, lnB_in, lnB)

            def c_q(b):
                ch = chains["C"]
                ch.begin(b)
                at(dve, "c_sq", b, 1, 1)
                ago(dve, "c_rs", b, 1, 1)
                V.tensor_reduce(ms[:, :, :], sq[:, :, :].rearrange("p t (h d) -> p t h d", d=DH), AX_X, ALU.add)\
                    .then_inc(S["c_ms"], 1)

            def c_split(b):
                ch = chains["C"]
                at(dve, "c_rs", b, 1, 1)
                at(dve, "c_v", b, 1, 1)
                ago(dve, "c_qt", b, 1, 1)
                for t in range(LT):
                    V.tensor_tensor(qpad[:, t, :, :].rearrange("p h (s d) -> p h s d", d=DH),
                                    bank[3 + t][:, 0:HQ * DH].rearrange("p (h d) -> p h d", d=DH).unsqueeze(2)
                                    .broadcast_to([P, HQ, 4, DH]),
                                    rs[:, t, 0:HQ].unsqueeze(2).unsqueeze(3).broadcast_to([P, HQ, 4, DH]), ALU.mult)
                    ch.link(V.tensor_tensor(kn[:, t, :].rearrange("p (h d) -> p h d", d=DH),
                                            bank[3 + t][:, HQ * DH:QV].rearrange("p (h d) -> p h d", d=DH),
                                            rs[:, t, HQ:HQ + HKV].unsqueeze(2).broadcast_to([P, HKV, DH]), ALU.mult))
                ch.settle()
                k = kn[:, :, :].rearrange("p t (h d) -> p (t h) d", d=DH)
                parts = kpad[:, :, :, :, :].rearrange("p t h s d -> p (t h) s d")
                for s in (0, 2):
                    ch.link(V.tensor_copy(parts[:, :, s, :].bitcast(F32R), k))
                ch.settle()
                V.tensor_tensor(parts[:, :, 1, :].bitcast(F32R), k, parts[:, :, 0, :], ALU.subtract)\
                    .then_inc(S["c_q"], 1)

            def c_ql(b):
                at(dve, "c_qtc", b, 1, 1)
                for k in range(2):
                    r = slice(64 * k + 32, 64 * k + 64)
                    last = V.tensor_tensor(QT[r, :, :, :].rearrange("p h g n -> p (h g n)"),
                                           ps[r, 3:7, :].rearrange("p h n -> p (h n)"),
                                           QT[r, :, :, :].bitcast(F32).rearrange("p h g n -> p (h g n)"),
                                           ALU.subtract)
                last.then_inc(S["c_ql"], 1)

            def c_y(b, p):
                at(dve, "c_pv", b, 2 * p + 2, 4)
                if p == 0:
                    ago(dve, "c_wo", b, 1, 1)
                V.tensor_copy(yT[:, 2 * p:2 * p + 2, :], halves(bank[7])).then_inc(S["c_y"], 1)

            def c_yn(b):
                ch = chains["C"]
                at(dve, "c_den", b, 1, 1)
                for p in range(2):
                    ch.link(V.reciprocal(rsum[:, 2 * p:2 * p + 2, :], halves(bank[3 + p])))
                ch.settle()
                V.tensor_tensor(yT[:, :, :], yT[:, :, :], rsum[:, :, :], ALU.mult).then_inc(S["c_yn"], 1)

            def c_ln(b):
                at(dve, "c_ss", b, 1, 1)
                ago(dve, "c_rms", b, 1, 1)
                V.tensor_reduce(ssq[:, :], sq[:, :, 0:D], AX_X, ALU.add).then_inc(S["c_ssum"], 1)

            def r_ln(b):
                ch = chains["R"]
                ch.begin(b)
                at(dve, "c_rms", b, 1, 1)
                at(dve, "b_kept", b, 1, 1)
                for t in range(LT):
                    last = V.scalar_tensor_tensor(out=lnC_in[:, t, :], in0=halves(bank[5])[:, t, :],
                                                  scalar=rms[:, t:t + 1], in1=xtok[:, bass.ds(b * LT + t, 1), :].rearrange("p o d -> p (o d)"),
                                                  op0=ALU.mult, op1=ALU.add)
                    if t == 0:
                        ch.link(last)
                last.then_inc(S["c_wod"], 1)
                ch.settle()
                at(dve, "c_wod", b, 1, 1)
                stats("R", b, lnC_in)

            def r_ln2(b):
                ago(dve, "c_tr", b, 1, 1)
                ago(dve, "r_kept", b, 1, 1)
                norm("R", b, lnC_in, lnC)

            def c_route(b):
                ch = chains["R"]
                at(dve, "c_sc", b, 1, 1)
                ago(dve, "c_w", b, 1, 1)
                ch.link(V.tensor_scalar(sc[:, :, :], rep[:, :, :], 0.5, 0.5, ALU.mult, ALU.add))
                ch.settle()
                hold()
                for t in range(LT):
                    ch.link(V.max(top[:, t, :], sc[:, t, :]))
                ch.settle()
                ch.link(V.tensor_reduce(tsum[:, :], top[:, :, 0:TOPK], AX_X, ALU.add))
                ch.link(V.memset(top[:, :, TOPK:8], -1.0))
                ch.settle()
                hold()
                for t in range(LT):
                    ch.link(V.match_replace(rep[:, t, :], top[:, t, :], sc[:, t, :], -2.0))
                ch.settle()
                ago(dve, "c_before", b, 1, 1)
                ago(dve, "c_pos", b, 1, 1)
                V.tensor_tensor(picked[:, :, :], rep[:, :, :], sc[:, :, :], ALU.not_equal).then_inc(S["c_pick"], 1)
                ch.link(V.reciprocal(tsum[:, :], tsum[:, :]))
                at(dve, "c_pick", b, 1, 1)
                ch.link(V.tensor_tensor(sc[:, :, :], sc[:, :, :], picked[:, :, :], ALU.mult))
                ch.settle()

            def c_w(b):
                ch = chains["R"]
                at(dve, "c_pos", b, 1, 1)
                ago(dve, "c_wtr", b, 1, 1)
                pos = bank[7][:, 0:LT * E].rearrange("p (t e) -> p t e", t=LT)
                V_last = V.scalar_tensor_tensor(out=wtok[:, :, 0:E], in0=pos, scalar=float(CAP), in1=sc[:, :, :],
                                                op0=ALU.is_lt, op1=ALU.mult)
                ch.link(V_last)
                ch.settle()
                for t in range(LT):
                    last = V.tensor_scalar(wtok[:, t, 0:E], wtok[:, t, 0:E], tsum[:, t:t + 1], 0.5, ALU.mult, ALU.mult)
                    if t == 0:
                        ch.link(last)
                last.then_inc(S["c_w"], 1)

            layers(dve, {"A.u0": lambda b: a_conv(b, 0), "A.u1": lambda b: a_conv(b, 1), "A.u2": lambda b: a_conv(b, 2),
                         "A.imag": a_Yr, "A.back": a_yx, "A.ln1": a_ln, "A.ln2": a_ln2, "B.ln1": b_ln, "B.ln2": b_ln2,
                         "C.qv": c_q, "C.q": c_split, "C.qt": c_ql, "C.s2": lambda b: c_y(b, 0),
                         "C.s4": lambda b: c_y(b, 1), "C.den": c_yn, "C.square": c_ln,
                         "R.ln1": r_ln, "R.ln2": r_ln2, "R.route": c_route, "R.pos": c_w,
                         **{f"B.up{h}": lambda b, h=h: b_h(b, h) for h in range(HT)}})

            layers_through(dve)
            V.memset(scratch[:, :], 0.0).then_inc(s_out, 16)

            def d_rest_w(j):
                dve.wait_ge(S["d_wh"], j + 1)
                V.tensor_tensor(wlo[:, j, :], stage[:, j % STAGES, 0:3 * D], whi[:, j, 0:3 * D].bitcast(F32),
                                ALU.subtract).then_inc(S["d_w"], 1)

            def d_xlo(b):
                at(dve, "d_xh", b, 1, 1)
                V.tensor_tensor(ghl[E:P, :], gateT[:, toks(b)], ghl[0:E, :].bitcast(F32), ALU.subtract)
                V.tensor_tensor(xlo[:, :, :], x3T[:, :, toks(b)], xhi[:, :, :].bitcast(F32), ALU.subtract)\
                    .then_inc(S["d_x"], 1)

            def d_hidden(b, j):
                at(dve, "d_th", b, j + 1, TILES)
                if j == ET:
                    ago(dve, "d_hl", b, TILES, TILES)
                    ago(dve, "d_hh", b, TILES, TILES)
                elif j < SLOTS - 1:
                    ago(dve, "d_hl", b, j + ET - SLOTS + 2, TILES)
                    ago(dve, "d_hh", b, j + ET - SLOTS + 2, TILES)
                else:
                    at(dve, "d_hl", b, j - SLOTS + 2, TILES)
                    at(dve, "d_hh", b, j - SLOTS + 2, TILES)
                o = halves(bank[2 * (j % 2)] if j < ET else bank[7])
                h = dh[:, slot(j), :]
                V.scalar_tensor_tensor(out=h, in0=dth[:, slot(j), :], scalar=1.0, in1=o[:, 0, :],
                                       op0=ALU.add, op1=ALU.mult).then_inc(S["d_g"], 1)
                at(dve, "d_g", b, j + 1, TILES)
                if j < ET:
                    V.tensor_tensor(h, h, o[:, 1, :], ALU.mult).then_inc(S["d_dve"], 1)
                    at(dve, "d_dve", b, j + 1, ET)
                    V.tensor_tensor(h, h, bank[1 + 2 * (j % 2)][:, 0:L], ALU.mult).then_inc(S["d_h"], 1)
                else:
                    V.scalar_tensor_tensor(out=h, in0=h, scalar=0.5, in1=o[:, 1, :],
                                           op0=ALU.mult, op1=ALU.mult).then_inc(S["d_h"], 1)

            def d_sum(b):
                at(dve, "d_down", b, TILES, TILES)
                for t in range(LT):
                    last = V.tensor_tensor(lnD_in[:, t, :], bank[4 + t][:, 0:D],
                                           xtok[:, bass.ds(b * LT + t, 1), :].rearrange("p o d -> p (o d)"), ALU.add)
                last.then_inc(S["d_accd"], 1)

            def d_stats(b):
                at(dve, "d_accd", b, 1, 1)
                for t in range(LT):
                    last = V.bn_stats(stat["D"][:, t, :], lnD_in[:, t, :])
                last.then_inc(S["d_stat"], 1)
                at(dve, "d_stat", b, 1, 1)
                hold()
                for t in range(LT):
                    last = V.bn_aggr(mv["D"][:, t, :], stat["D"][:, t, :])
                last.then_inc(S["d_var"], 1)

            def d_norm(b):
                at(dve, "d_var", b, 1, 1)
                at(dve, "d_rstd", b, 1, 1)
                dve.wait_ge(s_out, 16 * (b + 1))
                for t in range(LT):
                    V.tensor_scalar(lnD[:, t, :], lnD_in[:, t, :], mv["D"][:, t, 0:1], rstd["D"][:, t:t + 1],
                                    ALU.subtract, ALU.mult).then_inc(S["d_ln"], 1)

            def d_dve(b):
                if at_first(b):
                    d_rest_w(0)
                d_xlo(b)
                if at_first(b):
                    d_rest_w(1)
                    d_rest_w(2)
                else:
                    d_hidden(b - 1, ET)
                for j in range(ET):
                    d_hidden(b, j)
                    if at_first(b) and j + 3 < TILES:
                        d_rest_w(j + 3)
                    if not at_first(b):
                        if j == 1:
                            d_sum(b - 1)
                        elif j == 2:
                            d_stats(b - 1)
                        elif j == 4:
                            d_norm(b - 1)

            each_batch(dve, d_dve)
            d_hidden(NB - 1, ET)
            d_sum(NB - 1)
            d_stats(NB - 1)
            d_norm(NB - 1)

        @block.gpsimd
        def _(pool):
            Gp = nc.gpsimd
            pool.wait_ge(s_mat, 16 * len(MATS))
            Gp.tensor_copy(onesb[:, :], mat["ones"][:, :])
            Gp.tensor_copy(trib[:, :], mat["tri"][:, :])
            Gp.memset(before[:, :], 0.0)
            Gp.memset(mhalf[:, :], -0.5)
            Gp.memset(rms_eps[:, :], RMS_EPS)
            Gp.memset(ln_eps[:, :], LN_EPS)
            Gp.memset(wtok[:, :, :], 0.0)
            Gp.memset(kpad[:, :, :, :, :], 0.0)
            Gp.memset(vaug[:, :, :, :], 0.0).then_inc(i_pool, 1)
            pool.wait_ge(i_pool, 1)
            Gp.memset(vaug[:, :, :, DH:DH + 1], 1.0).then_inc(i_pads, 1)
            pool.wait_ge(i_pads, 1)
            pool.wait_ge(s_w2l, 16)
            src, dst = w2_sb, w2_tmp
            for n, step in enumerate((1, 2, 4)):
                s = src[:, :, :].rearrange("p (o two i) d -> p o two i d", two=2, i=step)
                d = dst[:, :, :].rearrange("p (o two i) d -> p o two i d", two=2, i=step)
                for o in range(HT // (2 * step)):
                    Gp.tensor_tensor(out=d[:, o, 0], in0=s[:, o, 0], in1=s[:, o, 1], op=ALU.add)
                    last = Gp.tensor_tensor(out=d[:, o, 1], in0=s[:, o, 0], in1=s[:, o, 1], op=ALU.subtract)
                last.then_inc(i_w2, 2)
                pool.wait_ge(i_w2, 2 * n + 2)
                src, dst = dst, src
            pool.wait_ge(s_wa, 16 * 6)
            pool.wait_ge(s_x, 16)
            for t in range(NB * LT):
                Gp.tensor_tensor(out=xtok[:, t, :], in0=xtok[:, t, :], in1=bout[:, :], op=ALU.add).then_inc(i_bout, 1)
            pool.wait_ge(i_bout, NB * LT)

            def rstd_of(key, b):
                k = key.lower()
                at(pool, k + "_var", b, 1, 1)
                ago(pool, k + "_ln", b, 2, 2)
                Gp.tensor_tensor(out=rstd[key][:, :], in0=mv[key][:, :, 1], in1=ln_eps[:, :], op=ALU.add)\
                    .then_inc(S[k + "_pool"], 1)
                at(pool, k + "_pool", b, 1, 1)
                Gp.tensor_tensor(out=rstd[key][:, :], in0=rstd[key][:, :], in1=mhalf[:, 0:LT], op=ALU.pow)\
                    .then_inc(S[k + "_rstd"], 1)

            def keep(key, b, src):
                k = key.lower()
                at(pool, k + "_ln", b, 2, 2)
                Gp.tensor_copy(xtok[:, tiles(b), :], src[:, :, :]).then_inc(S[k + "_kept"], 1)

            def a_Yi(b):
                at(pool, "a_Vi", b, 1, 1)
                ago(pool, "a_full", b, 7, 9)
                for blk in range(2):
                    Gp.tensor_tensor(out=pr[2][:, blk, :], in0=Kr[:, blk, :], in1=Vi[:, 0, :], op=ALU.mult)
                    last = Gp.tensor_tensor(out=pr[3][:, blk, :], in0=Ki[:, blk, :], in1=Vr[:, 0, :], op=ALU.mult)
                last.then_inc(S["a_pool2"], 1)
                at(pool, "a_pool2", b, 1, 4)
                Gp.tensor_tensor(out=Yi[:, :, :], in0=pr[2][:, :, :], in1=pr[3][:, :, :], op=ALU.add)\
                    .then_inc(S["a_pool2"], 1)
                at(pool, "a_pool2", b, 2, 4)
                Gp.tensor_tensor(out=pr[2][:, 0, :], in0=Kr[:, 0, :], in1=Vi[:, 1, :], op=ALU.mult)
                Gp.tensor_tensor(out=pr[3][:, 0, :], in0=Ki[:, 0, :], in1=Vr[:, 1, :], op=ALU.mult)\
                    .then_inc(S["a_pool2"], 1)
                at(pool, "a_pool2", b, 3, 4)
                Gp.tensor_tensor(out=Yi[:, 1, :], in0=Yi[:, 1, :], in1=pr[2][:, 0, :], op=ALU.add)\
                    .then_inc(S["a_pool2"], 1)
                at(pool, "a_pool2", b, 4, 4)
                Gp.tensor_tensor(out=Yi[:, 1, :], in0=Yi[:, 1, :], in1=pr[3][:, 0, :], op=ALU.add)\
                    .then_inc(S["a_Yi"], 1)

            def a_rows(b):
                keep("A", b, lnA)

            def b_rows(b):
                keep("B", b, lnB)

            def c_rs(b):
                at(pool, "c_ms", b, 1, 1)
                ago(pool, "c_q", b, 1, 1)
                for t in range(LT):
                    last = Gp.tensor_tensor(out=rs[:, t, :], in0=ms[:, t, :], in1=rms_eps[:, :], op=ALU.add)
                last.then_inc(S["c_pool"], 1)
                at(pool, "c_pool", b, 1, 2)
                for t in range(LT):
                    last = Gp.tensor_tensor(out=rs[:, t, :], in0=rs[:, t, :], in1=mhalf[:, :], op=ALU.pow)
                last.then_inc(S["c_rs"], 1)

            def c_rows(b):
                at(pool, "c_ssum", b, 1, 1)
                ago(pool, "c_wod", b, 1, 1)
                Gp.tensor_tensor(out=rms[:, :], in0=ssq[:, :], in1=rms_eps[:, 0:LT], op=ALU.add)\
                    .then_inc(S["c_pool"], 1)
                at(pool, "c_pool", b, 2, 2)
                Gp.tensor_tensor(out=rms[:, :], in0=rms[:, :], in1=mhalf[:, 0:LT], op=ALU.pow).then_inc(S["c_rms"], 1)

            def r_rows(b):
                keep("R", b, lnC)

            def c_before(b):
                at(pool, "c_pos", b, 1, 1)
                Gp.tensor_tensor(out=before[:, :], in0=before[:, :], in1=picked[:, 0, :], op=ALU.add)\
                    .then_inc(S["c_cnt"], 1)
                at(pool, "c_cnt", b, 1, 1)
                Gp.tensor_tensor(out=before[:, :], in0=before[:, :], in1=picked[:, 1, :], op=ALU.add)\
                    .then_inc(S["c_before"], 1)

            layers(pool, {"A.imag": a_Yi, "A.ln1": lambda b: rstd_of("A", b), "A.ln2": a_rows,
                          "B.ln1": lambda b: rstd_of("B", b), "B.ln2": b_rows, "C.qv": c_rs, "C.square": c_rows,
                          "R.ln1": lambda b: rstd_of("R", b), "R.ln2": r_rows, "R.pos": c_before})

            layers_through(pool)

            def d_hlo(b, j):
                at(pool, "d_hh", b, j + 1, TILES)
                Gp.tensor_tensor(out=hlo[:, slot(j), :], in0=dh[:, slot(j), :], in1=hhi[:, slot(j), :].bitcast(F32),
                                 op=ALU.subtract).then_inc(S["d_hl"], 1)

            def d_power(b):
                at(pool, "d_var", b, 1, 1)
                Gp.tensor_tensor(out=rstd["D"][:, :], in0=mv["D"][:, :, 1], in1=ln_eps[:, :], op=ALU.add)\
                    .then_inc(S["d_pool"], 1)
                at(pool, "d_pool", b, 1, 1)
                Gp.tensor_tensor(out=rstd["D"][:, :], in0=rstd["D"][:, :], in1=mhalf[:, 0:LT], op=ALU.pow)\
                    .then_inc(S["d_rstd"], 1)

            def d_pool(b):
                if not at_first(b):
                    d_hlo(b - 1, ET)
                for j in range(ET):
                    d_hlo(b, j)
                    if j == 2 and not at_first(b):
                        d_power(b - 1)

            each_batch(pool, d_pool)
            d_hlo(NB - 1, ET)
            d_power(NB - 1)


def kernel(**inputs):
    import math
    import numpy as np
    import concourse.bacc as bacc
    from concourse.bass_utils import run_bass_kernel_spmd

    nc = bacc.Bacc("TRN2", target_bir_lowering=False, num_devices=1)
    v = {n: np.asarray(a) for n, a in inputs.items()}

    def rows(a):
        return a.reshape(-1, P, a.shape[-1]).transpose(1, 0, 2)

    wo = v["L1_attn_Wo"].reshape(HKV, 2, 2, DH, D).transpose(0, 3, 2, 1, 4).reshape(HKV, DH, G, D)
    wo_pad = np.zeros((HKV, 32, G, D), wo.dtype)
    wo_pad[:, :DH] = wo
    up = v["L1_ffn_w_up"]
    n = np.arange(P)
    wexp = np.zeros((ET + 1, P, EW), up.dtype)
    for q, part in enumerate((up[:, :, :EH], up[:, :, EH:])):
        a = part.reshape(ET, EPT, DT, P, EH).transpose(0, 3, 2, 1, 4)
        wexp[:ET, :, q * D:(q + 1) * D] = a.reshape(ET, P, D)
    wexp[:ET, :, 2 * D:3 * D] = v["L1_ffn_w_down"].reshape(ET, P, D)
    wexp[:ET, :, 3 * D:] = n[None, :, None] % E == EPT * np.arange(ET)[:, None, None] + n[None, None, :] // EH
    shared = v["L1_ffn_w_shared_up"].reshape(DT, P, 2, HS)
    for q in range(2):
        for c in range(DT):
            wexp[ET, :, q * D + c * P:q * D + c * P + HS] = shared[c, :, 1 - q]
    wexp[ET, :HS, 2 * D:3 * D] = v["L1_ffn_w_shared_down"]
    x = v["L0_attn_x"].reshape(TOK, D)
    laid = {
        "x": rows(x), "xT": rows(x.T),
        "w_in": rows(v["L0_attn_in_proj_w"].T), "b_in": v["L0_attn_in_proj_b"].reshape(CH, P).T,
        "short_w": v["L0_attn_short_w"].reshape(CH, P, 3).transpose(1, 2, 0),
        "short_b": v["L0_attn_short_b"].reshape(CH, P).T,
        "mlp_w0": v["L0_attn_mlp_w0"].T, "mlp_b0": v["L0_attn_mlp_b0"][:, None], "freq": v["L0_attn_sin_freq"].T,
        "mlp_w1": v["L0_attn_mlp_w1"].T, "mlp_b1": v["L0_attn_mlp_b1"][:, None],
        "mlp_w2": v["L0_attn_mlp_w2"].T, "mlp_b2": v["L0_attn_mlp_b2"][:, None],
        "mlp_w3": v["L0_attn_mlp_w3"].T, "filter_bias": v["L0_attn_filter_bias"][None, :],
        "w_out": rows(v["L0_attn_out_proj_w"].T), "b_out": np.broadcast_to(v["L0_attn_out_proj_b"], (P, D)),
        "w1": rows(v["L0_ffn_W1"].T), "w3": rows(v["L0_ffn_W3"].T), "w2": rows(v["L0_ffn_W2"].T),
        "wqv": rows(np.concatenate([v["L1_attn_Wq"], v["L1_attn_Wv"]], axis=1)),
        "wo": wo_pad.reshape(P, G, D), "wgate": rows(v["L1_ffn_w_gate"]),
        "wexp": wexp,
    }

    t, k = np.arange(P, dtype=np.float64), np.arange(P, dtype=np.float64) + 0.5
    angle = 2 * np.pi / L * t[:, None] * k[None, :]
    wide = 2 * np.pi / L * (t[:, None] - P) * k[None, :]
    n = np.arange(P)
    had = np.ones((1, 1))
    while had.shape[0] < P:
        had = np.block([[had, had], [had, -had]])
    square = {
        "ident": np.eye(P), "cos_t": np.cos(angle), "msin_t": -np.sin(angle), "cos_w": np.cos(wide),
        "msin_w": -np.sin(wide), "icos": np.cos(angle).T / P, "imsin": -np.sin(angle).T / P,
        "sumsel": (n[:, None] % 32 == DH) & (n[:, None] // 32 == n[None, :] // 32),
        "tri": n[:, None] < n[None, :], "ones": np.ones((P, P)),
        "had": had / (2 * math.sqrt(HID)),
    }
    pos = np.linspace(0.0, 1.0, L, dtype=np.float32)
    ang = np.float32(0.0001) * (np.float32(2 * math.pi) * np.linspace(0.0, L - 1.0, L, dtype=np.float32) / L)
    deltas = np.abs(np.linspace(math.log(0.01) / 1.5, math.log(0.01) / 0.3, D, dtype=np.float32))
    laid["mats"] = np.stack([square[m] for m in MATS]).astype(np.float32)
    laid["pos_emb"] = np.stack([pos, np.cos(ang), -np.sin(ang)]).astype(np.float32)
    laid["decay"] = rows(np.exp(-pos[:, None] * deltas[None, :]).astype(np.float32))
    order = ["x", "xT", "w_in", "b_in", "short_w", "short_b", "mlp_w0", "mlp_b0", "freq", "mlp_w1", "mlp_b1",
             "mlp_w2", "mlp_b2", "mlp_w3", "filter_bias", "w_out", "b_out", "w1", "w3", "w2", "wqv", "wo", "wgate",
             "mats", "decay", "pos_emb", "wexp"]
    arrays, args = {}, []
    for name in order:
        a = np.ascontiguousarray(laid[name])
        arrays["in_" + name] = a
        args.append(nc.dram_tensor("in_" + name, a.shape, mybir.dt.from_np(a.dtype), kind="ExternalInput").ap())
    out = nc.dram_tensor("out_0", (TOK, D), F32, kind="ExternalOutput").ap()
    mixed_kernel(nc, *args, out.rearrange("(t p) d -> p t d", p=P))
    r = run_bass_kernel_spmd(nc, [arrays], core_ids=[0])
    return r.results[0]["out_0"].reshape(NB, L, D)
```

```python
from contextlib import ExitStack

import concourse.bass as bass
from concourse import mybir

F32 = mybir.dt.float32
F32R = mybir.dt.float32r
BF16 = mybir.dt.bfloat16
ALU = mybir.AluOpType
ACT = mybir.ActivationFunctionType
AX_X = mybir.AxisListType.X

P = 128
NB, L, D = 8, 256, 256
TOK = NB * L
LT = L // P
DT = D // P
CH = 3 * D // P
FO = 64
HID = 1024
HT = HID // P
HQ, HKV, DH = 16, 4, 16
G = HQ // HKV
QV = HQ * DH + HKV * DH
E, EH, HS = 64, 32, 64
TOPK, CAP = 6, 128
EPT = P // EH
ET = E // EPT
LN_EPS = 1e-5
RMS_EPS = 1.1920929e-07
TWO_PI = 6.283185307179586
TWO_PI_HI = 6.28125
TWO_PI_LO = TWO_PI - TWO_PI_HI
PI_SAFE = 3.1415925
ROUND = 12582912.0

MLP_COLS = (64, 128, 192, 448, 452, 708, 964)
EW = 3 * D + P
STAGES = 6
EARLY, EARLY_W = 4, 7
SLOTS = 5

MATS = ["cos_t", "msin_t", "cos_w", "msin_w", "icos", "imsin", "sumsel", "tri", "had"]


def mixed_kernel(nc, x, xT, w_in, conv, mlp, w_out, b_out, w1, w3, w2, wqv, wo, wgate, ident_in, mats, decay, wexp,
                 out):
    with ExitStack() as ctx:
        layers_memory = ExitStack()

        def sb(name, shape, dt=F32):
            return layers_memory.enter_context(nc.sbuf_tensor(name, shape, dt))

        def lent(name, shape, dt=F32):
            with nc.sbuf_tensor(name, shape, dt) as buffer:
                return buffer

        def keep_sb(name, shape, dt=F32):
            return ctx.enter_context(nc.sbuf_tensor(name, shape, dt))

        def sem(name):
            return ctx.enter_context(nc.semaphore(name))

        xtok = keep_sb("xtok", [P, NB * LT, D])
        xT0 = keep_sb("xT0", [P, DT, TOK])
        x3T = xT0
        gateT = keep_sb("gateT", [E, TOK])
        mhalf = keep_sb("mhalf", [P, HQ + HKV])
        ln_eps = keep_sb("ln_eps", [P, LT])
        scratch = keep_sb("scratch", [P, 1])
        stat = {k: keep_sb("stat" + k, [P, LT, 6]) for k in "ABRD"}
        mv = {k: keep_sb("mv" + k, [P, LT, 2]) for k in "ABRD"}
        rstd = {k: keep_sb("rstd" + k, [P, LT]) for k in "ABRD"}

        x3s = keep_sb("x3s", [P, DT, L])
        sc = keep_sb("sc", [P, LT, E])
        rep = keep_sb("rep", [P, LT, E])
        top = keep_sb("top", [P, LT, 8])
        tsum = keep_sb("tsum", [P, LT])
        picked = keep_sb("picked", [P, LT, E], BF16)
        before = keep_sb("before", [P, E], BF16)
        onesb = keep_sb("onesb", [P, P], BF16)
        trib = keep_sb("trib", [P, P], BF16)
        wtok = keep_sb("wtok", [P, LT, P])
        rms = keep_sb("rms", [P, LT])
        wg_sb = keep_sb("wg_sb", [P, DT, E])
        lnC, lnC_in = keep_sb("lnC", [P, LT, D]), keep_sb("lnC_in", [P, LT, D])
        ident_sb = keep_sb("ident_sb", [P, P])

        win = sb("win", [P, DT, 3 * D])
        u = sb("u", [P, CH, L + 2])
        uc = sb("uc", [P, CH, L])
        vT = sb("vT", [P, DT, L])
        vtok, Yr, Yi = (sb(n, [P, LT, D]) for n in ("vtok", "Yr", "Yi"))
        Vr, Vi = uc[:, 2:4, :], uc[:, 4:6, :]
        pr = [sb(f"pr{n}", [P, LT, D]) for n in range(4)]
        Kr = sb("Kr", [P, 2, D])
        Ki = sb("Ki", [P, 2, D])
        yx = pr[0]
        lnA, lnA_in = sb("lnA", [P, LT, D]), sb("lnA_in", [P, LT, D])
        wout = sb("wout", [P, DT, D])

        w2_sb = sb("w2_sb", [P, HT, D])
        w13hi = sb("w13hi", [P, 2, DT, HID], F32R)
        w13raw = lent("w13raw", [P, 2, DT, HID])
        w13lo = sb("w13lo", [P, 2, DT, HID], F32R)
        x1hi = sb("x1hi", [P, DT, L], F32R)
        x1lo = sb("x1lo", [P, DT, L], F32R)
        th = sb("th", [P, 2, L])
        hT = sb("hT", [P, HT, L])
        lnB, lnB_in = sb("lnB", [P, LT, D]), sb("lnB_in", [P, LT, D])
        decay_sb, taps = lnB, lnB_in

        mats_sb = sb("mats_sb", [P, len(MATS), P])
        mat = {name: mats_sb[:, n, :] for n, name in enumerate(MATS)}
        conv_sb = sb("conv_sb", [P, 5 * CH])
        bin_sb, sw, sbias = conv_sb[:, 0:CH], conv_sb[:, CH:4 * CH].rearrange("p (k c) -> p k c", k=3), \
            conv_sb[:, 4 * CH:5 * CH]
        bias2 = sb("bias2", [P, CH])
        store_c = lent("store_c", [P, 2 * HT * D])
        qpad = sb("qpad", [P, LT, HQ, 4, DH], F32R)
        sb("store_c_rest", [P, HT * D])
        mlp_sb = store_c[0:FO, HT * D:HT * D + MLP_COLS[-1]]
        m0, m1, m2, m3, mb, pos_sb, fb = (mlp_sb[0:n, a:b] for n, a, b in zip(
            (3, FO, FO, FO, FO, 3, 1), (0,) + MLP_COLS[:-1], MLP_COLS))
        bout = sb("bout", [P, D])
        wqv_sb = sb("wqv_sb", [P, DT, QV])
        wo_sb = sb("wo_sb", [P, G, D])
        rms_eps = sb("rms_eps", [P, HQ + HKV])

        def views(store, *shapes):
            got, at_word = [], 0
            for shape in shapes:
                n = 1
                for d in shape:
                    n *= d
                piece = store[:, at_word:at_word + n]
                dims = " ".join("abc"[:len(shape)])
                if len(shape) > 1:
                    piece = piece.rearrange(f"p ({dims}) -> p {dims}", **dict(zip("abc", shape)))
                got.append(piece)
                at_word += n
            return got

        w2_tmp, _ = views(store_c, (HT, D), (HT, D))
        prob = views(store_c, (HKV, 2 * L), (HKV, 2 * L))


        x2T = sb("x2T", [P, DT, L])

        ms = sb("ms", [P, LT, HQ + HKV])
        rs = sb("rs", [P, LT, HQ + HKV])
        kpad = sb("kpad", [P, LT, HKV, 4, DH], F32R)
        identr = sb("identr", [P, P], F32R)
        vaug = sb("vaug", [P, LT, HKV, 32])
        QT = sb("QT", [P, HKV, 2, L], F32R)
        KT = sb("KT", [P, HKV, L], F32R)
        yT = sb("yT", [P, G, L])
        rden = sb("rden", [P, LT, G, HKV])
        store_q = sb("store_q", [P, LT * G * P])
        sq, = views(store_q, (LT, QV))
        qn, kn = views(store_q, (LT, HQ * DH), (LT, HKV * DH))
        rspread = store_q[:, :].rearrange("p (t g h s) -> p t g h s", t=LT, g=G, h=HKV)
        arg, turns, hf = lnC[0:FO, 0, :], lnC[0:FO, 1, :], lnC_in[0:FO, 0, :]
        ssq = sb("ssq", [P, LT])

        layers_memory.close()
        def d_sb(name, shape, dt=F32):
            return keep_sb("mix_" + name, shape, dt)

        stage = d_sb("stage", [P, STAGES, EW])
        xhi = d_sb("xhi", [P, DT, L], F32R)
        xlo = d_sb("xlo", [P, DT, L], F32R)
        ghl = d_sb("ghl", [P, L], F32R)
        dh = d_sb("dh", [P, SLOTS, L])
        vshared = d_sb("vshared", [HS, L])
        hhi = d_sb("hhi", [P, SLOTS, L], F32R)
        hlo = d_sb("hlo", [P, SLOTS, L], F32R)
        wsplit = d_sb("wsplit", [P, ET + 1, EW + 3 * D], F32R)
        whi, wlo = wsplit[:, :, 0:EW], wsplit[:, :, EW:]
        lnD, lnD_in = d_sb("lnD", [P, LT, D]), d_sb("lnD_in", [P, LT, D])

        ps = ctx.enter_context(nc.psum_tensor("ps", [P, 8, 512], F32))
        bank = [ps[:, n, :] for n in range(8)]

        s_mat, s_filt, s_conv, s_u, s_wout, s_x, s_xT, s_w2l, s_wc = (sem("s_" + n) for n in (
            "mat", "filt", "conv", "u", "wout", "x", "xT", "w2l", "wc"))
        s_wb = [sem("s_w1"), sem("s_w3")]
        s_stage = [sem(f"s_stage{n}") for n in range(STAGES)]
        s_out = sem("s_out")
        i_dve, i_pool, i_pe, i_act = (sem("i_" + n) for n in ("dve", "pool", "pe", "act"))
        i_w13hi, i_w13 = sem("i_w13hi"), sem("i_w13")
        i_w2 = sem("i_w2")
        i_w2pe = sem("i_w2pe")
        i_w2done = sem("i_w2done")
        i_bias2 = sem("i_bias2")
        i_pads = sem("i_pads")
        i_bout = sem("i_bout")
        names = """a_full a_free a_u a_conv a_vT a_vtok a_Vr a_Yr a_Yi a_yx a_ln a_x1hi a_x1T a_dve a_pool a_var
                   a_rstd a_kept a_Vi a_pool2 b_full b_free b_th b_g b_h b_ln b_x2T b_dve b_pool b_var b_rstd
                   b_kept c_qv c_sq c_ms c_rs c_q c_v c_qt c_qtc c_ktc c_s c_p c_pv c_y c_den c_ssum c_yn c_wo c_ss
                   c_rms c_wod c_tr c_x3 c_dve c_pool r_pool r_var r_rstd r_kept r_ln c_lg c_sc c_pick c_pos c_w
                   c_wtr c_gateT c_before c_cnt r_dve c_rden c_spr c_sprt d_full d_th d_g d_dve d_h d_hh d_hl
                   d_down d_xh d_x d_wh d_w d_accd d_pool d_var d_rstd d_ln d_stat""".split()
        S = {n: sem(n) for n in names}

        class Chain:

            def __init__(self, eng, s, per=None):
                self.eng, self.s, self.per, self.n = eng, s, per, 0

            def begin(self, b):
                if self.n and self.per is None:
                    self.per = self.n
                self.b, self.n = b, 0

            def link(self, ins):
                self.n += 1
                ins.then_inc(self.s, 1)

            def settle(self):
                self.eng.wait_ge(self.s, self.n if self.per is None else self.b * self.per + self.n)

        def at(eng, name, b, k, per):
            eng.wait_ge(S[name], b * per + k)

        def ago(eng, name, b, k, per):
            if not (isinstance(b, int) and b == 0):
                eng.wait_ge(S[name], (b - 1) * per + k)

        def hold():
            nc.vector.memset(scratch[:, :], 0.0)

        def tiles(b):
            return bass.ds(b * LT, LT)

        def toks(b):
            return bass.ds(b * L, L)

        def halves(t):
            return t.rearrange("p (a n) -> p a n", a=2)

        ORDER = """R.ln1 R.ln2 A.u0 B.up0 C.qv A.u1 R.tr B.up1 A.u2 R.logit B.up2 B.up3 C.q A.vT B.up4
                   B.up5 A.real C.qt A.imag B.up6 C.s0 B.up7 C.s1 C.p0 C.s2 R.route B.down0 B.down1
                   A.back C.p1 A.out C.s3 C.p2 C.p3 A.ln1 A.ln2 B.down2 C.den B.down3 B.ln1 C.spread
                   B.ln2 A.tr R.pos C.out0 C.out1 C.square R.weight B.tr""".split()

        FIRST = """F.0 A.u0 F.1 F.2 A.u1 F.3 A.u2 A.vT F.4 A.real F.5 F.6 A.imag A.back A.out A.ln1
                   A.ln2 A.tr F.7""".split()
        LAST_BUT_ONE = """R.ln1 B.up0 C.qv B.up1 B.up2 B.up3 R.ln2 R.tr R.logit C.q B.up4 C.qt B.up5
                          B.up6 C.s0 C.s1 C.p0 C.s2 R.route B.up7 B.down0 B.down1 C.p1 C.s3 C.p2 C.p3
                          C.den B.down2 B.down3 C.spread B.ln1 R.pos C.out0 C.out1 B.ln2 C.square
                          R.weight B.tr""".split()
        LAST = """R.ln1 C.qv R.ln2 R.tr W.x R.logit C.q R.route W.0 C.qt W.1 C.s0 D.0 D.1 C.s1 C.p0 W.2
                  C.s2 C.p1 W.3 C.s3 C.p2 C.p3 D.2 C.den C.spread W.4 R.pos W.5 C.out0 C.out1 W.6
                  C.square D.3 R.weight""".split()

        def layers(eng, steps, after_first=None):
            def turn(a, b, c, r, order=ORDER):
                for step in order:
                    n = {"F": 0, "W": 0, "D": 0, "A": a, "B": b, "C": c, "R": r}[step[0]]
                    if n is not None and step in steps:
                        steps[step](n)

            turn(0, None, None, None, FIRST)
            if after_first:
                after_first()
            turn(1, 0, None, None)
            turn(2, 1, 0, None)
            turn(3, 2, 1, 0)
            with eng.Fori(4, NB) as i:
                turn(i, i - 1, i - 2, i - 3)
            turn(None, NB - 1, NB - 2, NB - 3, LAST_BUT_ONE)
            turn(None, None, NB - 1, NB - 2, LAST)

        TILES = ET + 1

        def slot(j):
            return j % (SLOTS - 1) if j < ET else SLOTS - 1

        def layers_through(eng):
            at(eng, "c_gateT", NB - 2, 1, 1)
            at(eng, "c_w", NB - 2, 1, 1)
            at(eng, "r_kept", NB - 2, 1, 1)
            at(eng, "c_before", NB - 2, 1, 1)
            at(eng, "b_kept", NB - 1, 1, 1)
            at(eng, "c_wo", NB - 1, 1, 1)
            at(eng, "c_rms", NB - 1, 1, 1)

        ROUTING = {0: "R.ln1", 4: "R.ln2", 5: "R.tr", 7: "R.logit", 9: "R.route", 11: "R.pos", 13: "R.weight"}

        def first_two_through(eng):
            at(eng, "a_kept", NB - 1, 1, 1)
            at(eng, "b_kept", NB - 1, 1, 1)
            at(eng, "b_x2T", NB - 1, 1, 1)

        def early(b, j):
            return at_first(b) and j < EARLY

        def units(j):
            return P if j < ET else HS

        def weights_bank(b, j):
            return bank[1] if early(b, j) else bank[1 + 2 * (j % 2)]

        def split_ahead(eng, split, b, j):
            if at_first(b) and EARLY_W <= j + 3 < TILES:
                if j + 3 == EARLY_W:
                    layers_through(eng)
                split(j + 3)

        def routing(steps, b, j):
            if at_first(b) and ROUTING.get(j) in steps:
                steps[ROUTING[j]](NB - 1)

        def each_batch(eng, step):
            step(0)
            at(eng, "c_gateT", NB - 1, 1, 1)
            at(eng, "c_x3", NB - 1, 2, 2)
            at(eng, "r_kept", NB - 1, 1, 1)
            with eng.Fori(1, NB) as b:
                step(b)

        def at_first(b):
            return isinstance(b, int) and b == 0

        def h_free(eng, b, j):
            if j == ET:
                ago(eng, "d_down", b, TILES, TILES)
            elif j < SLOTS - 1:
                ago(eng, "d_down", b, j + ET - SLOTS + 2, TILES)
            else:
                at(eng, "d_down", b, j - SLOTS + 2, TILES)

        block = ctx.enter_context(nc.Block())

        @block.sync
        def _(sp):
            sp.dma_start(mlp_sb, mlp).then_inc(s_filt, 16)
            sp.dma_start(decay_sb[:, :, :], decay).then_inc(s_filt, 16)
            sp.dma_start(ident_sb[:, :], ident_in).then_inc(s_mat, 16)
            sp.dma_start(mats_sb[:, :, :], mats).then_inc(s_mat, 16)
            sp.dma_start(w2_sb[:, :, :], w2).then_inc(s_w2l, 16)
            sp.dma_start(bout[:, :], b_out).then_inc(s_x, 16)
            sp.dma_start(xtok[:, :, :], x).then_inc(s_x, 16)
            for q, src in enumerate((w1, w3)):
                sp.dma_start(w13raw[:, q, :, :], src).then_inc(s_wb[q], 16)
            for dst, src in ((wqv_sb[:, :, :], wqv), (wo_sb[:, :, :], wo), (wg_sb[:, :, :], wgate)):
                sp.dma_start(dst, src).then_inc(s_wc, 16)
            at(sp, "a_full", NB - 1, 9, 9)
            at(sp, "a_kept", NB - 1, 1, 1)
            for j in range(TILES):
                if j >= STAGES:
                    sp.wait_ge(S["d_w"], j - STAGES + 1)
                sp.dma_start(stage[:, j % STAGES, :], wexp[j]).then_inc(s_stage[j % STAGES], 16)
            with sp.Fori(0, NB) as b:
                at(sp, "d_ln", b, 2, 2)
                sp.dma_start(out[:, tiles(b), :], lnD[:, :, :]).then_inc(s_out, 16)
            sp.wait_ge(s_out, 16 * (NB + 1))

        @block.scalar
        def _(act):
            act.dma_start(conv_sb[:, :], conv).then_inc(s_conv, 16)
            act.dma_start(xT0[:, :, 0:L], xT[:, :, 0:L]).then_inc(s_u, 16)
            act.dma_start(win[:, :, :], w_in).then_inc(s_u, 16)
            act.dma_start(wout[:, :, :], w_out).then_inc(s_wout, 16)
            act.dma_start(xT0[:, :, L:TOK], xT[:, :, L:TOK]).then_inc(s_xT, 16)

            def f_sine(k):
                act.wait_ge(i_dve, 6 * (k + 1))
                nc.scalar.activation(hf, arg, ACT.Sin).then_inc(i_act, 1)

            def w13_upper(q):
                act.wait_ge(s_wb[q], 16)
                nc.scalar.activation(w13hi[:, q, :, :], w13raw[:, q, :, :], ACT.Copy).then_inc(i_w13hi, 1)

            act.wait_ge(i_bias2, 3)

            def a_u(b, part):
                at(act, "a_full", b, part + 1, 9)
                ago(act, "a_yx" if part == 2 else "a_vT", b, 1, 1)
                for q in range(2):
                    m = 4 - 2 * part + q
                    nc.scalar.activation(u[:, m, 2:L + 2], halves(bank[0])[:, q, :], ACT.Identity,
                                         bias=bin_sb[:, m:m + 1])
                    last = nc.scalar.activation(uc[:, m, :], halves(bank[0])[:, q, :], ACT.Identity,
                                                bias=bias2[:, m:m + 1], scale=sw[:, 2, m:m + 1])
                last.then_inc(S["a_u"], 1)

            def a_vtok(b):
                at(act, "a_full", b, 4, 9)
                nc.scalar.activation(vtok[:, :, :], halves(bank[0]), ACT.Copy).then_inc(S["a_vtok"], 1)

            def a_spec(b, k):
                at(act, "a_full", b, 5 + k, 9)
                ago(act, "a_Yr", b, 1, 1)
                ago(act, "a_Yi", b, 1, 1)
                nc.scalar.activation((Vr, Vi)[k][:, :, :], halves(bank[0]), ACT.Copy)\
                    .then_inc(S[("a_Vr", "a_Vi")[k]], 1)

            def a_x1T(b):
                at(act, "a_full", b, 9, 9)
                ago(act, "b_full", b, 8, 10)
                nc.scalar.activation(x1hi[:, :, :], halves(bank[0]), ACT.Copy).then_inc(S["a_x1hi"], 1)

            def b_th(b, h):
                at(act, "b_full", b, h + 1, 10)
                if h >= 2:
                    at(act, "b_g", b, h - 1, 8)
                else:
                    ago(act, "b_g", b, h + 7, 8)
                nc.scalar.activation(th[:, h % 2, :], bank[1 + h % 2][:, 0:L], ACT.Tanh, scale=0.5)\
                    .then_inc(S["b_th"], 1)

            def b_x2T(b):
                at(act, "b_full", b, 10, 10)
                ago(act, "c_qv", b, 1, 1)
                nc.scalar.activation(x2T[:, :, :], halves(bank[2]), ACT.Copy).then_inc(S["b_x2T"], 1)

            def c_sq(b):
                at(act, "c_qv", b, 1, 1)
                ago(act, "c_ssum", b, 1, 1)
                for t in range(LT):
                    last = nc.scalar.activation(sq[:, t, :], bank[3 + t][:, 0:QV], ACT.Square, scale=DH ** -0.5)
                last.then_inc(S["c_sq"], 1)
                ago(act, "c_pv", b, 4, 4)
                act.wait_ge(i_pads, 1)
                for t in range(LT):
                    last = nc.scalar.activation(vaug[:, t, :, 0:DH],
                                                bank[3 + t][:, HQ * DH:QV].rearrange("p (h d) -> p h d", h=HKV),
                                                ACT.Copy)
                last.then_inc(S["c_v"], 1)

            def c_qtc(b):
                at(act, "c_qt", b, 1, 1)
                ago(act, "c_s", b, 8, 8)
                for h in range(HKV):
                    last = nc.scalar.activation(QT[:, h, :, :], halves(bank[3 + h]), ACT.Copy)
                    if h % 2:
                        last.then_inc(S["c_qtc"], 1)

            def c_exp(b, n):
                if n >= 2:
                    at(act, "c_pv", b, n - 1, 4)
                else:
                    ago(act, "c_pv", b, n + 3, 4)
                for p in range(2):
                    at(act, "c_s", b, 2 * n + p + 1, 8)
                    nc.scalar.activation(prob[n % 2][:, 2 * p:2 * p + 2, :], ps[:, 3 + 2 * p:5 + 2 * p, :], ACT.Exp)\
                        .then_inc(S["c_p"], 1)

            def c_ss(b):
                at(act, "c_wo", b, 1, 1)
                at(act, "c_ms", b, 1, 1)
                for t in range(LT):
                    last = nc.scalar.activation(sq[:, t, 0:D], halves(bank[5])[:, t, :], ACT.Square,
                                                scale=D ** -0.5)
                last.then_inc(S["c_ss"], 1)

            def c_spread(b):
                at(act, "c_rden", b, 1, 1)
                for g in (slice(0, 2), slice(2, 4)):
                    for t in range(LT):
                        last = nc.scalar.activation(rspread[:, t, g, :, :], rden[:, t, g, :].unsqueeze(3)
                                                    .broadcast_to([P, 2, HKV, 32]), ACT.Copy)
                    last.then_inc(S["c_spr"], 1)

            def c_x3(b):
                at(act, "c_tr", b, 1, 1)
                nc.scalar.activation(x3s[:, :, :], halves(bank[5]), ACT.Copy).then_inc(S["c_x3"], 1)
                at(act, "c_x3", b, 1, 2)
                nc.scalar.activation(x3T[:, :, toks(b)], x3s[:, :, :], ACT.Copy).then_inc(S["c_x3"], 1)

            def c_sc(b):
                at(act, "c_lg", b, 1, 1)
                ago(act, "c_pick", b, 1, 1)
                nc.scalar.activation(rep[:, :, :], bank[5][:, 0:LT * E].rearrange("p (t e) -> p t e", t=LT),
                                     ACT.Tanh, scale=0.5).then_inc(S["c_sc"], 1)

            def c_gateT(b):
                at(act, "c_wtr", b, 1, 1)
                nc.scalar.activation(gateT[:, toks(b)], bank[7][0:E, 0:L], ACT.Copy).then_inc(S["c_gateT"], 1)

            def d_split_w(j):
                act.wait_ge(s_stage[j % STAGES], 16 * (j // STAGES + 1))
                nc.scalar.activation(whi[:, j, :], stage[:, j % STAGES, :], ACT.Copy).then_inc(S["d_wh"], 1)

            def d_xhi(b):
                if not at_first(b):
                    at(act, "d_full", b - 1, TILES, TILES)
                nc.scalar.activation(xhi[:, :, :], x3T[:, :, toks(b)], ACT.Copy).then_inc(S["d_xh"], 1)
                nc.scalar.activation(ghl[0:E, :], gateT[:, toks(b)], ACT.Copy).then_inc(S["d_xh"], 1)

            def d_tanh(b, j):
                at(act, "d_full", b, j + 1, TILES)
                for split in ("d_hh", "d_hl"):
                    if j < SLOTS - 1 or j == ET:
                        ago(act, split, b, j + ET - SLOTS + 2 if j < ET else TILES, TILES)
                    else:
                        at(act, split, b, j - SLOTS + 2, TILES)
                n = units(j)
                if j == ET:
                    nc.scalar.activation(vshared[:, :], bank[7][HS:2 * HS, 0:L], ACT.Copy)
                nc.scalar.activation(dh[0:n, slot(j), :], (bank[2 * (j % 2)] if j < ET else bank[7])[0:n, 0:L],
                                     ACT.Tanh, scale=0.5).then_inc(S["d_th"], 1)

            def d_hhi(b, j):
                at(act, "d_h", b, j + 1, TILES)
                h_free(act, b, j)
                n = units(j)
                nc.scalar.activation(hhi[0:n, slot(j), :], dh[0:n, slot(j), :], ACT.Copy).then_inc(S["d_hh"], 1)

            steps = {**{f"F.{k}": lambda _, k=k: f_sine(k) for k in range(3)}, "A.u0": lambda b: a_u(b, 0),
                     "A.u1": lambda b: a_u(b, 1), "A.u2": lambda b: a_u(b, 2), "A.vT": a_vtok,
                     "A.real": lambda b: a_spec(b, 0), "A.imag": lambda b: a_spec(b, 1), "A.tr": a_x1T,
                     "B.tr": b_x2T, "C.qv": c_sq, "C.qt": c_qtc, "C.den": c_spread, "C.square": c_ss, "R.tr": c_x3,
                     "R.logit": c_sc, "R.weight": c_gateT,
                     **{f"B.up{h}": lambda b, h=h: b_th(b, h) for h in range(HT)},
                     **{f"C.s{n}": lambda b, n=n: c_exp(b, n) for n in range(4)}}
            steps.update({**{f"W.{j}": lambda _, j=j: d_split_w(j) for j in range(EARLY_W)},
                          "W.x": lambda _: (first_two_through(act), d_xhi(0)),
                          **{f"D.{j}": lambda _, j=j: (d_tanh(0, j), d_hhi(0, j)) for j in range(EARLY)}})
            steps.update({f"F.{6 + q}": lambda _, q=q: w13_upper(q) for q in range(2)})
            layers(act, steps)

            def d_act(b):
                if not at_first(b):
                    d_xhi(b)
                    d_tanh(b - 1, ET)
                    d_hhi(b - 1, ET - 1)
                for j in range(ET):
                    if not early(b, j):
                        d_tanh(b, j)
                    routing(steps, b, j)
                    if j and not early(b, j - 1):
                        d_hhi(b, j - 1)
                    elif j == 0 and not at_first(b):
                        d_hhi(b - 1, ET)
                    split_ahead(act, d_split_w, b, j)

            each_batch(act, d_act)
            d_tanh(NB - 1, ET)
            d_hhi(NB - 1, ET - 1)
            d_hhi(NB - 1, ET)

        @block.tensor
        def _(pe):
            mm, tr = nc.tensor.matmul, nc.tensor.transpose
            ident = ident_sb[:, :]
            def f_pe(k):
                if k == 0:
                    pe.wait_ge(s_filt, 32)
                    mm(bank[3][0:FO, 0:L], m0, pos_sb, start=True, stop=True).then_inc(i_pe, 1)
                elif k < 3:
                    pe.wait_ge(i_act, k)
                    mm(bank[3][0:FO, 0:L], (m1, m2)[k - 1], hf, start=True, stop=True).then_inc(i_pe, 1)
                elif k == 3:
                    pe.wait_ge(i_act, 3)
                    for t in range(LT):
                        last = mm(halves(bank[3])[:, t, :], hf[:, t * P:(t + 1) * P], m3, start=True, stop=True)
                    last.then_inc(i_pe, 1)
                else:
                    pe.wait_ge(i_dve, 20)
                    pe.wait_ge(s_mat, 32)
                    for q, (first, wide) in enumerate((("cos_t", "cos_w"), ("msin_t", "msin_w"))):
                        view = halves(bank[1 + q])
                        mm(view[:, 0, :], mat[first], taps[:, 0, :], start=True, stop=True)
                        mm(view[:, 1, :], mat[first], taps[:, 1, :], start=True, stop=False)
                        last = mm(view[:, 1, :], mat[wide], taps[:, 0, :], start=False, stop=True)
                    last.then_inc(i_pe, 1)

            def hadamard():
                pe.wait_ge(i_w2, 6)
                for q in range(HT // 2):
                    mm(bank[4 + q][:, :], mat["had"], w2_tmp[:, 2 * q:2 * q + 2, :].rearrange("p a d -> p (a d)"),
                       start=True, stop=True).then_inc(i_w2pe, 1)
                pe.wait_ge(i_w13, 2)
                pe.wait_ge(s_wc, 48)
                pe.wait_ge(s_xT, 16)

            def a_u(b, part):
                a_wait(b, part)
                if at_first(b) and part == 0:
                    pe.wait_ge(s_u, 32)
                for q in range(2):
                    m = 4 - 2 * part + q
                    for c in range(DT):
                        last = mm(halves(bank[0])[:, q, :], win[:, c, m * P:(m + 1) * P], xT0[:, c, toks(b)],
                                  start=c == 0, stop=c == DT - 1)
                last.then_inc(S["a_full"], 1)

            def a_wait(b, k):
                name, n, per = (("a_x1T", 1, 1), ("a_u", 1, 3), ("a_u", 2, 3), ("a_u", 3, 3), ("a_vtok", 1, 1),
                                ("a_Vr", 1, 1), ("a_Vi", 1, 1), ("a_yx", 1, 1), ("a_free", 1, 1))[k]
                (ago if k == 0 else at)(pe, name, b, n, per)

            def a_vT(b):
                a_wait(b, 3)
                at(pe, "a_vT", b, 1, 1)
                if at_first(b):
                    pe.wait_ge(s_mat, 32)
                for t in range(LT):
                    for m in range(DT):
                        last = tr(halves(bank[0])[:, t, m * P:(m + 1) * P], vT[:, m, t * P:(t + 1) * P], ident)
                last.then_inc(S["a_full"], 1)

            def a_dft(b, k):
                a_wait(b, 4 + k)
                at(pe, "a_vtok", b, 1, 1)
                last = mm(bank[0][:, :], mat[("cos_t", "msin_t")[k]],
                          vtok[:, :, :].rearrange("p t d -> p (t d)"), start=True, stop=True)
                last.then_inc(S["a_full"], 1)

            def a_idft(b):
                a_wait(b, 6)
                at(pe, "a_Yr", b, 1, 1)
                at(pe, "a_Yi", b, 1, 1)
                for m in range(DT):
                    for t in range(LT):
                        o = halves(bank[0])[:, m, t * P:(t + 1) * P]
                        mm(o, Yr[:, t, m * P:(m + 1) * P], mat["icos"], start=True, stop=False)
                        last = mm(o, Yi[:, t, m * P:(m + 1) * P], mat["imsin"], start=False, stop=True)
                last.then_inc(S["a_full"], 1)

            def a_out(b):
                a_wait(b, 7)
                at(pe, "a_yx", b, 1, 1)
                if at_first(b):
                    pe.wait_ge(s_wout, 16)
                for t in range(LT):
                    for m in range(DT):
                        last = mm(halves(bank[0])[:, t, :], yx[:, m, t * P:(t + 1) * P], wout[:, m, :],
                                  start=m == 0, stop=m == DT - 1)
                last.then_inc(S["a_full"], 1)

            def turn_rows(dst, src, b, normed):
                for t in range(LT):
                    at(pe, normed, b, t + 1, 2)
                    for m in range(DT):
                        last = tr(halves(dst)[:, m, t * P:(t + 1) * P], src[:, t, m * P:(m + 1) * P], ident)
                return last

            def a_tr(b):
                a_wait(b, 8)
                turn_rows(bank[0], lnA, b, "a_ln").then_inc(S["a_full"], 1)

            def b_up(b, h):
                if h == 0:
                    at(pe, "a_x1T", b, 1, 1)
                if h >= 2:
                    at(pe, "b_h", b, h - 1, 8)
                elif h == 0:
                    ago(pe, "b_free", b, 1, 1)
                else:
                    ago(pe, "b_x2T", b, 1, 1)
                for q in range(2):
                    for n, (w, v) in enumerate(((w13hi, x1hi), (w13hi, x1lo), (w13lo, x1hi))):
                        for c in range(DT):
                            last = mm(halves(bank[1 + h % 2])[:, q, :], w[:, q, c, h * P:(h + 1) * P], v[:, c, :],
                                      start=c + n == 0, stop=c == DT - 1 and n == 2)
                last.then_inc(S["b_full"], 1)

            def b_down(b, part):
                t, hidden = part // 2, range(part % 2 * HT // 2, (part % 2 + 1) * HT // 2)
                at(pe, "b_h", b, HT - 1 if part == 0 else HT, 8)
                if part == 0 and at_first(b):
                    pe.wait_ge(i_w2done, 1)
                for h in hidden:
                    last = mm(halves(bank[1])[:, t, :], hT[:, h, t * P:(t + 1) * P], w2_sb[:, h, :],
                              start=h == 0, stop=h == HT - 1)
                if part == 2 * LT - 1:
                    last.then_inc(S["b_full"], 1)

            def b_tr(b):
                at(pe, "b_h", b, HT, 8)
                turn_rows(bank[2], lnB, b, "b_ln").then_inc(S["b_full"], 1)

            def c_qv(b):
                at(pe, "b_x2T", b, 1, 1)
                ago(pe, "c_yn", b, 1, 2)
                for t in range(LT):
                    for c in range(DT):
                        last = mm(bank[3 + t][:, 0:QV], x2T[:, c, t * P:(t + 1) * P], wqv_sb[:, c, :],
                                  start=c == 0, stop=c == DT - 1)
                last.then_inc(S["c_qv"], 1)

            def c_qt(b):
                at(pe, "c_v", b, 1, 1)
                ago(pe, "c_sc", b, 1, 1)
                if not isinstance(b, int) or b >= 2:
                    at(pe, "c_gateT", b, -1, 1)

                def turn_heads(n, t):
                    mm(halves(bank[3 + n // 2])[:, n % 2, t * P:(t + 1) * P],
                       qpad[:, t, 2 * n:2 * n + 2, :, :].rearrange("p h s d -> p (h s d)"), identr[:, :],
                       start=True, stop=True)

                at(pe, "c_q", b, 1, 2)
                for n in (0, 1, 4, 5, 6, 7):
                    turn_heads(n, 0)
                at(pe, "c_q", b, 2, 2)
                for n in (2, 3):
                    turn_heads(n, 0)
                for n in range(HQ // 2):
                    turn_heads(n, 1)
                for p in range(2):
                    for t in range(LT):
                        last = mm(halves(bank[7])[:, p, t * P:(t + 1) * P],
                                  kpad[:, t, 2 * p:2 * p + 2, :, :].rearrange("p h s d -> p (h s d)"), identr[:, :],
                                  start=True, stop=True)
                last.then_inc(S["c_qt"], 1)

            def c_s(b, n):
                if n == 0:
                    at(pe, "c_ktc", b, 1, 1)
                odd, t = n // 2, n % 2
                r = slice(64 * odd, 64 * odd + 64)
                for h in range(HKV):
                    if n == 0 and h % 2 == 0:
                        at(pe, "c_qtc", b, 1 + h // 2, 2)
                    elif h % 2 == 0:
                        at(pe, "c_p", b, 2 * n - 1 + h // 2, 8)
                    last = mm(bank[3 + h][:, :], KT[r, h, t * P:(t + 1) * P],
                              QT[r, h, :, :].rearrange("p g n -> p (g n)"), start=True, stop=True)
                    if h % 2:
                        last.then_inc(S["c_s"], 1)

            def c_pv(b, n):
                if n == 2:
                    at(pe, "c_y", b, 1, 2)
                for h in range(HKV):
                    if h % 2 == 0:
                        at(pe, "c_p", b, 2 * n + 1 + h // 2, 8)
                    last = mm(bank[7][32 * h:32 * h + 32, :], vaug[:, n % 2, h, :], prob[n % 2][:, h, :],
                              start=n % 2 == 0, stop=n % 2 == 1, skip_group_check=True)
                last.then_inc(S["c_pv"], 1)

            def c_den(b):
                at(pe, "c_y", b, 2, 2)
                at(pe, "c_p", b, 8, 8)
                for t in range(LT):
                    for g in range(G):
                        n = (t * G + g) * HKV
                        last = mm(bank[3][:, n:n + HKV], yT[:, g, t * P:(t + 1) * P], mat["sumsel"][:, 0:HKV],
                                  start=True, stop=True)
                last.then_inc(S["c_den"], 1)

            def c_back(b):
                for p in range(2):
                    at(pe, "c_spr", b, p + 1, 2)
                    for g in range(2):
                        for t in range(LT):
                            last = tr(halves(bank[4 + 2 * p])[:, g, t * P:(t + 1) * P],
                                      rspread[:, t, 2 * p + g, :, :].rearrange("p h s -> p (h s)"), ident)
                    last.then_inc(S["c_sprt"], 1)

            def c_wo(b, t):
                for g in range(G):
                    if t == 0 and g % 2 == 0:
                        at(pe, "c_yn", b, g // 2 + 1, 2)
                    last = mm(halves(bank[5])[:, t, :], yT[:, g, t * P:(t + 1) * P], wo_sb[:, g, :],
                              start=g == 0, stop=g == G - 1)
                if t == LT - 1:
                    last.then_inc(S["c_wo"], 1)

            def c_tr(b):
                at(pe, "c_wod", b, 1, 1)
                turn_rows(bank[5], lnC, b, "r_ln").then_inc(S["c_tr"], 1)

            def c_lg(b):
                at(pe, "c_x3", b, 1, 2)
                for t in range(LT):
                    for c in range(DT):
                        last = mm(bank[5][:, t * E:(t + 1) * E], x3s[:, c, t * P:(t + 1) * P], wg_sb[:, c, :],
                                  start=c == 0, stop=c == DT - 1)
                last.then_inc(S["c_lg"], 1)

            def c_pos(b):
                at(pe, "c_pick", b, 1, 1)
                at(pe, "c_y", b, 2, 2)
                ago(pe, "c_before", b, 1, 1)
                if isinstance(b, int) and b == 0:
                    pe.wait_ge(i_pads, 1)
                mm(bank[7][:, 0:E], trib[:, :], picked[:, 0, :], start=True, stop=False)
                mm(bank[7][:, 0:E], onesb[:, :], before[:, :], start=False, stop=True)
                mm(bank[7][:, E:2 * E], trib[:, :], picked[:, 1, :], start=True, stop=False)
                mm(bank[7][:, E:2 * E], onesb[:, :], picked[:, 0, :], start=False, stop=False)
                mm(bank[7][:, E:2 * E], onesb[:, :], before[:, :], start=False, stop=True).then_inc(S["c_pos"], 1)

            def c_wtr(b):
                at(pe, "c_w", b, 1, 1)
                for t in range(LT):
                    last = tr(bank[7][:, t * P:(t + 1) * P], wtok[:, t, :], ident)
                last.then_inc(S["c_wtr"], 1)

            def up(b, j):
                if at_first(b):
                    pe.wait_ge(S["d_w"], j + 1)
                if j == 0:
                    at(pe, "d_xh", b, 1, 2)
                if j == ET:
                    ago(pe, "d_h", b, TILES, TILES)
                    if at_first(b):
                        at(pe, "c_gateT", NB - 1, 1, 1)
                elif j >= 2:
                    at(pe, "d_h", b, j - 1, TILES)
                else:
                    ago(pe, "d_h", b, ET - 1 + j, TILES)
                o = halves(bank[2 * (j % 2)] if j < ET else bank[7])
                for q in range(2 if j < ET else 1):
                    for n, (w, v) in enumerate(((wlo, xhi), (whi, xhi), (whi, xlo))):
                        if j == 0 and q == 0 and n == 2:
                            at(pe, "d_x", b, 1, 2)
                        for c in range(DT):
                            cols = slice(q * D + c * P, q * D + (c + 1) * P)
                            last = mm(o[:, q, :], w[:, j, cols], v[:, c, :], start=c + n == 0,
                                      stop=c == DT - 1 and n == 2)
                if j == 0:
                    at(pe, "d_x", b, 2, 2)
                if at_first(b) and 1 <= j <= EARLY:
                    at(pe, "d_h", 0, j, TILES)
                if j < ET:
                    last = mm(weights_bank(b, j)[:, 0:L], whi[:, j, 3 * D:EW], ghl[:, :], start=True, stop=True)
                last.then_inc(S["d_full"], 1)

            def down(b, j):
                at(pe, "d_hh", b, j + 1, TILES)
                at(pe, "d_hl", b, j + 1, TILES)
                if j == 0:
                    ago(pe, "d_accd", b, 1, 1)
                k = units(j)
                for t in range(LT):
                    rows = slice(t * P, (t + 1) * P)
                    for n, (h, w) in enumerate(((hhi, whi), (hhi, wlo), (hlo, whi))):
                        last = mm(bank[4 + 2 * t][:, 0:D], h[0:k, slot(j), rows], w[0:k, j, 2 * D:3 * D],
                                  start=j + n == 0, stop=j == ET and n == 2)
                last.then_inc(S["d_down"], 1)

            steps = {**{f"F.{k}": lambda _, k=k: f_pe(k) for k in range(5)}, "A.u0": lambda b: a_u(b, 0),
                     "A.u1": lambda b: a_u(b, 1), "A.u2": lambda b: a_u(b, 2), "A.vT": a_vT,
                     "A.real": lambda b: a_dft(b, 0), "A.imag": lambda b: a_dft(b, 1), "A.back": a_idft,
                     "A.out": a_out, "A.tr": a_tr, "B.tr": b_tr,
                     **{f"B.down{k}": lambda b, k=k: b_down(b, k) for k in range(2 * LT)}, "C.qv": c_qv,
                     "C.qt": c_qt, "C.den": c_den, "C.spread": c_back,
                     **{f"C.out{t}": lambda b, t=t: c_wo(b, t) for t in range(LT)}, "R.tr": c_tr, "R.logit": c_lg,
                     "R.pos": c_pos, "R.weight": c_wtr,
                     **{f"B.up{h}": lambda b, h=h: b_up(b, h) for h in range(HT)},
                     **{f"C.s{n}": lambda b, n=n: c_s(b, n) for n in range(4)},
                     **{f"C.p{n}": lambda b, n=n: c_pv(b, n) for n in range(4)}}
            steps.update({f"D.{j}": lambda _, j=j: up(0, j) for j in range(EARLY)})
            layers(pe, steps, hadamard)

            def d_pe(b):
                if not at_first(b):
                    down(b - 1, ET - 3)
                    down(b - 1, ET - 2)
                for j in range(ET):
                    if j >= 4:
                        if j == 4:
                            down(b, 0)
                        down(b, j - 3)
                    elif j in (1, 2) and not at_first(b):
                        down(b - 1, ET - 2 + j)
                    if not early(b, j):
                        up(b, j)
                    routing(steps, b, j)
                up(b, ET)

            each_batch(pe, d_pe)
            for j in range(ET - 3, TILES):
                down(NB - 1, j)

        @block.vector
        def _(dve):
            V = nc.vector
            setup = Chain(dve, i_dve)
            setup.begin(0)
            dve.wait_ge(s_conv, 16)
            V.memset(u[:, :, 0:2], 0.0).then_inc(i_bias2, 1)
            V.tensor_tensor(bias2[:, :], bin_sb, sw[:, 2, :], ALU.mult).then_inc(i_bias2, 1)
            dve.wait_ge(i_bias2, 2)
            V.tensor_tensor(bias2[:, :], bias2[:, :], sbias, ALU.add).then_inc(i_bias2, 1)
            dve.wait_ge(s_filt, 32)
            def f_argument(k):
                dve.wait_ge(i_pe, k + 1)
                setup.link(V.tensor_scalar(arg, bank[3][0:FO, 0:L], mb[:, k:k + 1], mb[:, 3:4], ALU.add, ALU.mult))
                setup.settle()
                setup.link(V.tensor_scalar(turns, arg, 1.0 / TWO_PI, ROUND, ALU.mult, ALU.add))
                setup.settle()
                setup.link(V.tensor_scalar(turns, turns, ROUND, None, ALU.subtract))
                setup.settle()
                for part in (TWO_PI_HI, TWO_PI_LO):
                    setup.link(V.scalar_tensor_tensor(out=arg, in0=turns, scalar=-part, in1=arg,
                                                      op0=ALU.mult, op1=ALU.add))
                    setup.settle()
                setup.link(V.tensor_scalar(arg, arg, PI_SAFE, -PI_SAFE, ALU.min, ALU.max))

            def f_taps():
                dve.wait_ge(i_pe, 4)
                setup.link(V.tensor_tensor(taps[:, :, :], halves(bank[3]), decay_sb[:, :, :], ALU.mult))
                setup.settle()
                setup.link(V.tensor_tensor(taps[0:1, 0, :], taps[0:1, 0, :], fb, ALU.add))

            def f_spectra():
                dve.wait_ge(i_pe, 5)
                setup.link(V.tensor_copy(Kr[:, :, :], halves(bank[1])))
                setup.link(V.tensor_copy(Ki[:, :, :], halves(bank[2])))
                setup.settle()

            f_steps = {"F.0": lambda _: f_argument(0), "F.1": lambda _: f_argument(1), "F.2": lambda _: f_argument(2),
                       "F.3": lambda _: f_taps(), "F.4": lambda _: f_spectra()}

            def w13_rest(q):
                dve.wait_ge(i_w13hi, q + 1)
                V.tensor_tensor(w13lo[:, q, :, :], w13raw[:, q, :, :], w13hi[:, q, :, :].bitcast(F32), ALU.subtract)\
                    .then_inc(i_w13, 1)

            def w2_back():
                for q in range(HT // 2):
                    dve.wait_ge(i_w2pe, q + 1)
                    last = V.tensor_copy(w2_sb[:, 2 * q:2 * q + 2, :], halves(bank[4 + q]))
                last.then_inc(i_w2done, 1)

            chains = {k: Chain(dve, S[k.lower() + "_dve"]) for k in "ABCR"}

            def stats(key, b, rows):
                ch, k = chains[key], key.lower()
                for t in range(LT):
                    ch.link(V.bn_stats(stat[key][:, t, :], rows[:, t, :]))
                ch.settle()
                hold()
                for t in range(LT):
                    last = V.bn_aggr(mv[key][:, t, :], stat[key][:, t, :])
                last.then_inc(S[k + "_var"], 1)

            def norm(key, b, rows, normed):
                k = key.lower()
                at(dve, k + "_rstd", b, 1, 1)
                for t in range(LT):
                    V.tensor_scalar(normed[:, t, :], rows[:, t, :], mv[key][:, t, 0:1], rstd[key][:, t:t + 1],
                                    ALU.subtract, ALU.mult).then_inc(S[k + "_ln"], 1)

            def a_conv(b, part):
                ch = chains["A"]
                if part == 0:
                    ch.begin(b)
                at(dve, "a_u", b, part + 1, 3)
                for q in range(2):
                    m = 4 - 2 * part + q
                    ch.link(V.scalar_tensor_tensor(out=uc[:, m, :], in0=u[:, m, 1:L + 1], scalar=sw[:, 1, m:m + 1],
                                                   in1=uc[:, m, :], op0=ALU.mult, op1=ALU.add))
                ch.settle()
                for q in range(2):
                    m = 4 - 2 * part + q
                    ins = V.scalar_tensor_tensor(out=uc[:, m, :], in0=u[:, m, 0:L], scalar=sw[:, 0, m:m + 1],
                                                 in1=uc[:, m, :], op0=ALU.mult, op1=ALU.add)
                    if q == 0:
                        ch.link(ins)
                ins.then_inc(S["a_conv"], 1)
                if part == 1:
                    ch.settle()
                    at(dve, "a_conv", b, 2, 3)
                    V.tensor_tensor(vT[:, :, :], uc[:, 4:6, :], uc[:, 2:4, :], ALU.mult).then_inc(S["a_vT"], 1)

            def a_Yr(b):
                ch = chains["A"]
                at(dve, "a_Vr", b, 1, 1)
                at(dve, "a_Vi", b, 1, 1)
                ago(dve, "a_full", b, 7, 9)
                for blk in range(2):
                    ch.link(V.tensor_tensor(pr[0][:, blk, :], Kr[:, blk, :], Vr[:, 0, :], ALU.mult))
                    ch.link(V.tensor_tensor(pr[1][:, blk, :], Ki[:, blk, :], Vi[:, 0, :], ALU.mult))
                ch.settle()
                ch.link(V.tensor_tensor(Yr[:, :, :], pr[0][:, :, :], pr[1][:, :, :], ALU.subtract))
                ch.settle()
                ch.link(V.tensor_tensor(pr[0][:, 0, :], Kr[:, 0, :], Vr[:, 1, :], ALU.mult))
                ch.link(V.tensor_tensor(pr[1][:, 0, :], Ki[:, 0, :], Vi[:, 1, :], ALU.mult))
                ch.settle()
                ch.link(V.tensor_tensor(Yr[:, 1, :], Yr[:, 1, :], pr[0][:, 0, :], ALU.add))
                ch.settle()
                V.tensor_tensor(Yr[:, 1, :], Yr[:, 1, :], pr[1][:, 0, :], ALU.subtract).then_inc(S["a_Yr"], 1)

            def a_yx(b):
                at(dve, "a_full", b, 7, 9)
                at(dve, "a_conv", b, 3, 3)
                V.tensor_tensor(yx[:, :, :], halves(bank[0]), uc[:, 0:2, :], ALU.mult).then_inc(S["a_yx"], 1)

            def a_ln(b):
                at(dve, "a_full", b, 8, 9)
                if isinstance(b, int) and b < 2:
                    dve.wait_ge(i_bout, b + 1)
                V.tensor_tensor(lnA_in[:, :, :], halves(bank[0]), xtok[:, tiles(b), :],
                                ALU.add).then_inc(S["a_free"], 1)
                at(dve, "a_free", b, 1, 1)
                stats("A", b, lnA_in)

            def a_ln2(b):
                ago(dve, "a_full", b, 9, 9)
                ago(dve, "a_kept", b, 1, 1)
                norm("A", b, lnA_in, lnA)

            def a_x1lo(b):
                at(dve, "a_x1hi", b, 1, 1)
                V.tensor_tensor(x1lo[:, :, :], halves(bank[0]), x1hi[:, :, :].bitcast(F32), ALU.subtract)\
                    .then_inc(S["a_x1T"], 1)

            def b_h(b, h):
                ch = chains["B"]
                if h == 0:
                    ch.begin(b)
                    ago(dve, "b_full", b, 9, 10)
                at(dve, "b_th", b, h + 1, 8)
                o = halves(bank[1 + h % 2])
                V.scalar_tensor_tensor(out=hT[:, h, :], in0=th[:, h % 2, :], scalar=1.0, in1=o[:, 0, :],
                                       op0=ALU.add, op1=ALU.mult).then_inc(S["b_g"], 1)
                at(dve, "b_g", b, h + 1, 8)
                V.tensor_tensor(hT[:, h, :], hT[:, h, :], o[:, 1, :], ALU.mult).then_inc(S["b_h"], 1)

            def b_ln(b):
                at(dve, "b_full", b, 9, 10)
                at(dve, "a_kept", b, 1, 1)
                V.tensor_tensor(lnB_in[:, :, :], halves(bank[1]), xtok[:, tiles(b), :], ALU.add)\
                    .then_inc(S["b_free"], 1)
                at(dve, "b_free", b, 1, 1)
                stats("B", b, lnB_in)

            def b_ln2(b):
                ago(dve, "b_full", b, 10, 10)
                ago(dve, "b_kept", b, 1, 1)
                norm("B", b, lnB_in, lnB)

            def c_q(b):
                ch = chains["C"]
                ch.begin(b)
                at(dve, "c_sq", b, 1, 1)
                if at_first(b):
                    dve.wait_ge(i_pads, 1)
                ago(dve, "c_rs", b, 2, 2)
                V.tensor_reduce(ms[:, :, :], sq[:, :, :].rearrange("p t (h d) -> p t h d", d=DH), AX_X, ALU.add)\
                    .then_inc(S["c_ms"], 1)

            def c_split(b):
                ch = chains["C"]
                at(dve, "c_v", b, 1, 1)
                ago(dve, "c_qt", b, 1, 1)
                for t in range(LT):
                    at(dve, "c_rs", b, t + 1, 2)
                    for n, dst, lo in ((HQ, qn[:, t, :], 0), (HKV, kn[:, t, :], HQ)):
                        heads = bank[3 + t][:, lo * DH:(lo + n) * DH].rearrange("p (h d) -> p h d", d=DH)
                        ch.link(V.tensor_tensor(dst.rearrange("p (h d) -> p h d", d=DH), heads,
                                                rs[:, t, lo:lo + n].unsqueeze(2).broadcast_to([P, n, DH]), ALU.mult))
                    ch.settle()
                    q = qn[:, t, :].rearrange("p (h d) -> p h d", d=DH)
                    k = kn[:, t, :].rearrange("p (h d) -> p h d", d=DH)
                    for s in (0, 2):
                        ch.link(V.tensor_copy(kpad[:, t, :, s, :], k))
                    ch.link(V.tensor_copy(qpad[:, t, :, 0:2, :], q.unsqueeze(2).broadcast_to([P, HQ, 2, DH])))
                    ch.settle()
                    V.tensor_tensor(kpad[:, t, :, 1, :], k, kpad[:, t, :, 0, :].bitcast(F32), ALU.subtract)
                    V.tensor_tensor(qpad[:, t, :, 2:4, :], q.unsqueeze(2).broadcast_to([P, HQ, 2, DH]),
                                    qpad[:, t, :, 0:2, :].bitcast(F32), ALU.subtract).then_inc(S["c_q"], 1)

            def c_ktc(b):
                at(dve, "c_qt", b, 1, 1)
                ago(dve, "c_s", b, 8, 8)
                for odd in range(2):
                    for r in (slice(0, 64), slice(64, 128)):
                        last = V.tensor_copy(KT[r, odd::2, :], halves(bank[7])[64 * odd:64 * odd + 64])
                last.then_inc(S["c_ktc"], 1)

            def c_y(b, p):
                at(dve, "c_pv", b, 2 * p + 2, 4)
                if p == 0:
                    ago(dve, "c_wo", b, 1, 1)
                V.tensor_copy(yT[:, 2 * p:2 * p + 2, :], halves(bank[7])).then_inc(S["c_y"], 1)

            def c_rden(b):
                at(dve, "c_den", b, 1, 1)
                sums = bank[3][:, 0:LT * G * HKV].rearrange("p (t g h) -> p t g h", t=LT, g=G)
                V.reciprocal(rden[:, :, :, :], sums).then_inc(S["c_rden"], 1)

            def c_yn(b):
                for p in range(2):
                    at(dve, "c_sprt", b, p + 1, 2)
                    V.tensor_tensor(yT[:, 2 * p:2 * p + 2, :], yT[:, 2 * p:2 * p + 2, :], halves(bank[4 + 2 * p]),
                                    ALU.mult).then_inc(S["c_yn"], 1)

            def c_ln(b):
                at(dve, "c_ss", b, 1, 1)
                ago(dve, "c_rms", b, 1, 1)
                V.tensor_reduce(ssq[:, :], sq[:, :, 0:D], AX_X, ALU.add).then_inc(S["c_ssum"], 1)

            def r_ln(b):
                ch = chains["R"]
                ch.begin(b)
                at(dve, "c_rms", b, 1, 1)
                at(dve, "b_kept", b, 1, 1)
                for t in range(LT):
                    row = xtok[:, bass.ds(b * LT + t, 1), :].rearrange("p o d -> p (o d)")
                    last = V.scalar_tensor_tensor(out=lnC_in[:, t, :], in0=halves(bank[5])[:, t, :],
                                                  scalar=rms[:, t:t + 1], in1=row,
                                                  op0=ALU.mult, op1=ALU.add)
                    if t == 0:
                        ch.link(last)
                last.then_inc(S["c_wod"], 1)
                ch.settle()
                at(dve, "c_wod", b, 1, 1)
                stats("R", b, lnC_in)

            def r_ln2(b):
                ago(dve, "c_tr", b, 1, 1)
                ago(dve, "r_kept", b, 1, 1)
                norm("R", b, lnC_in, lnC)

            def c_route(b):
                ch = chains["R"]
                at(dve, "c_sc", b, 1, 1)
                ago(dve, "c_w", b, 1, 1)
                ch.link(V.tensor_scalar(sc[:, :, :], rep[:, :, :], 0.5, 0.5, ALU.mult, ALU.add))
                ch.settle()
                hold()
                for t in range(LT):
                    ch.link(V.max(top[:, t, :], sc[:, t, :]))
                ch.settle()
                ch.link(V.tensor_reduce(tsum[:, :], top[:, :, 0:TOPK], AX_X, ALU.add))
                ch.link(V.memset(top[:, :, TOPK:8], -1.0))
                ch.settle()
                hold()
                for t in range(LT):
                    ch.link(V.match_replace(rep[:, t, :], top[:, t, :], sc[:, t, :], -2.0))
                ch.settle()
                ago(dve, "c_before", b, 1, 1)
                ago(dve, "c_pos", b, 1, 1)
                V.tensor_tensor(picked[:, :, :], rep[:, :, :], sc[:, :, :], ALU.not_equal).then_inc(S["c_pick"], 1)
                ch.link(V.reciprocal(tsum[:, :], tsum[:, :]))
                at(dve, "c_pick", b, 1, 1)
                ch.link(V.tensor_tensor(sc[:, :, :], sc[:, :, :], picked[:, :, :], ALU.mult))
                ch.settle()

            def c_w(b):
                ch = chains["R"]
                at(dve, "c_pos", b, 1, 1)
                ago(dve, "c_wtr", b, 1, 1)
                pos = bank[7][:, 0:LT * E].rearrange("p (t e) -> p t e", t=LT)
                V_last = V.scalar_tensor_tensor(out=wtok[:, :, 0:E], in0=pos, scalar=float(CAP), in1=sc[:, :, :],
                                                op0=ALU.is_lt, op1=ALU.mult)
                ch.link(V_last)
                ch.settle()
                for t in range(LT):
                    last = V.tensor_scalar(wtok[:, t, 0:E], wtok[:, t, 0:E], tsum[:, t:t + 1], 0.5,
                                           ALU.mult, ALU.mult)
                    if t == 0:
                        ch.link(last)
                last.then_inc(S["c_w"], 1)

            def d_rest_w(j):
                dve.wait_ge(S["d_wh"], j + 1)
                V.tensor_tensor(wlo[:, j, :], stage[:, j % STAGES, 0:3 * D], whi[:, j, 0:3 * D].bitcast(F32),
                                ALU.subtract).then_inc(S["d_w"], 1)

            def d_xlo(b):
                at(dve, "d_xh", b, 1, 2)
                V.tensor_tensor(xlo[:, :, :], x3T[:, :, toks(b)], xhi[:, :, :].bitcast(F32), ALU.subtract)\
                    .then_inc(S["d_x"], 1)
                at(dve, "d_xh", b, 2, 2)
                V.tensor_tensor(ghl[E:P, :], gateT[:, toks(b)], ghl[0:E, :].bitcast(F32), ALU.subtract)\
                    .then_inc(S["d_x"], 1)

            def d_hidden(b, j):
                at(dve, "d_th", b, j + 1, TILES)
                o = halves(bank[2 * (j % 2)] if j < ET else bank[7])
                h = dh[0:units(j), slot(j), :]
                V.scalar_tensor_tensor(out=h, in0=h, scalar=1.0, in1=o[0:units(j), 0, :],
                                       op0=ALU.add, op1=ALU.mult).then_inc(S["d_g"], 1)
                at(dve, "d_g", b, j + 1, TILES)
                if j < ET:
                    V.tensor_tensor(h, h, o[:, 1, :], ALU.mult).then_inc(S["d_dve"], 1)
                    at(dve, "d_dve", b, j + 1, ET)
                    V.tensor_tensor(h, h, weights_bank(b, j)[:, 0:L], ALU.mult).then_inc(S["d_h"], 1)
                else:
                    V.scalar_tensor_tensor(out=h, in0=h, scalar=0.5, in1=vshared[:, :],
                                           op0=ALU.mult, op1=ALU.mult).then_inc(S["d_h"], 1)

            steps = {**f_steps, "A.u0": lambda b: a_conv(b, 0), "A.u1": lambda b: a_conv(b, 1),
                     "A.u2": lambda b: a_conv(b, 2), "A.imag": a_Yr, "A.back": a_yx, "A.ln1": a_ln, "A.ln2": a_ln2,
                     "A.tr": a_x1lo, "B.ln1": b_ln, "B.ln2": b_ln2, "C.qv": c_q, "C.q": c_split, "C.qt": c_ktc,
                     "C.p1": lambda b: c_y(b, 0), "C.p3": lambda b: c_y(b, 1), "C.den": c_rden, "C.spread": c_yn,
                     "C.square": c_ln, "R.ln1": r_ln, "R.ln2": r_ln2, "R.route": c_route, "R.pos": c_w,
                     **{f"B.up{h}": lambda b, h=h: b_h(b, h) for h in range(HT)}}
            steps.update({**{f"W.{j}": lambda _, j=j: d_rest_w(j) for j in range(EARLY_W)},
                          "W.x": lambda _: (first_two_through(dve), d_xlo(0)),
                          **{f"D.{j}": lambda _, j=j: d_hidden(0, j) for j in range(EARLY)}})
            steps.update({f"F.{6 + q}": lambda _, q=q: w13_rest(q) for q in range(2)})
            layers(dve, steps, w2_back)

            V.memset(scratch[:, :], 0.0).then_inc(s_out, 16)

            def d_sum(b):
                at(dve, "d_down", b, TILES, TILES)
                for t in range(LT):
                    last = V.tensor_tensor(lnD_in[:, t, :], bank[4 + 2 * t][:, 0:D],
                                           xtok[:, bass.ds(b * LT + t, 1), :].rearrange("p o d -> p (o d)"), ALU.add)
                last.then_inc(S["d_accd"], 1)

            def d_stats(b):
                at(dve, "d_accd", b, 1, 1)
                for t in range(LT):
                    last = V.bn_stats(stat["D"][:, t, :], lnD_in[:, t, :])
                last.then_inc(S["d_stat"], 1)
                at(dve, "d_stat", b, 1, 1)
                hold()
                for t in range(LT):
                    last = V.bn_aggr(mv["D"][:, t, :], stat["D"][:, t, :])
                last.then_inc(S["d_var"], 1)

            def d_norm(b):
                at(dve, "d_var", b, 1, 1)
                at(dve, "d_rstd", b, 1, 1)
                dve.wait_ge(s_out, 16 * (b + 1))
                for t in range(LT):
                    V.tensor_scalar(lnD[:, t, :], lnD_in[:, t, :], mv["D"][:, t, 0:1], rstd["D"][:, t:t + 1],
                                    ALU.subtract, ALU.mult).then_inc(S["d_ln"], 1)

            def d_dve(b):
                if not at_first(b):
                    d_xlo(b)
                    d_hidden(b - 1, ET)
                for j in range(ET):
                    if not early(b, j):
                        d_hidden(b, j)
                    routing(steps, b, j)
                    split_ahead(dve, d_rest_w, b, j)
                    if not at_first(b):
                        if j == 1:
                            d_sum(b - 1)
                        elif j == 2:
                            d_stats(b - 1)
                        elif j == 4:
                            d_norm(b - 1)

            each_batch(dve, d_dve)
            d_hidden(NB - 1, ET)
            d_sum(NB - 1)
            d_stats(NB - 1)
            d_norm(NB - 1)

        @block.gpsimd
        def _(pool):
            Gp = nc.gpsimd
            Gp.memset(onesb[:, :], 1.0)
            Gp.memset(before[:, :], 0.0)
            Gp.memset(mhalf[:, :], -0.5)
            Gp.memset(rms_eps[:, :], RMS_EPS)
            Gp.memset(ln_eps[:, :], LN_EPS)
            Gp.memset(wtok[:, :, :], 0.0)
            Gp.memset(kpad[:, :, :, :, :].bitcast(F32), 0.0)
            Gp.memset(vaug[:, :, :, :], 0.0).then_inc(i_pool, 1)
            pool.wait_ge(i_pool, 1)
            Gp.memset(vaug[:, :, :, DH:DH + 1], 1.0)
            pool.wait_ge(s_mat, 32)
            Gp.tensor_copy(identr[:, :], ident_sb[:, :])
            Gp.tensor_copy(trib[:, :], mat["tri"]).then_inc(i_pads, 1)
            def with_bias(some):
                pool.wait_ge(s_x, 32)
                for t in some:
                    last = Gp.tensor_tensor(out=xtok[:, t, :], in0=xtok[:, t, :], in1=bout[:, :], op=ALU.add)
                last.then_inc(i_bout, 1)

            def w2_across():
                pool.wait_ge(s_w2l, 16)
                src, dst = w2_sb, w2_tmp
                for n, step in enumerate((1, 2, 4)):
                    s = src[:, :, :].rearrange("p (o two i) d -> p o two i d", two=2, i=step)
                    d = dst[:, :, :].rearrange("p (o two i) d -> p o two i d", two=2, i=step)
                    for o in range(HT // (2 * step)):
                        Gp.tensor_tensor(out=d[:, o, 0], in0=s[:, o, 0], in1=s[:, o, 1], op=ALU.add)
                        last = Gp.tensor_tensor(out=d[:, o, 1], in0=s[:, o, 0], in1=s[:, o, 1], op=ALU.subtract)
                    last.then_inc(i_w2, 2)
                    pool.wait_ge(i_w2, 2 * n + 2)
                    src, dst = dst, src

            w2_across()
            def rstd_of(key, b):
                k = key.lower()
                at(pool, k + "_var", b, 1, 1)
                ago(pool, k + "_ln", b, 2, 2)
                Gp.tensor_tensor(out=rstd[key][:, :], in0=mv[key][:, :, 1], in1=ln_eps[:, :], op=ALU.add)\
                    .then_inc(S[k + "_pool"], 1)
                at(pool, k + "_pool", b, 1, 1)
                Gp.tensor_tensor(out=rstd[key][:, :], in0=rstd[key][:, :], in1=mhalf[:, 0:LT], op=ALU.pow)\
                    .then_inc(S[k + "_rstd"], 1)

            def keep(key, b, src):
                k = key.lower()
                at(pool, k + "_ln", b, 2, 2)
                Gp.tensor_copy(xtok[:, tiles(b), :], src[:, :, :]).then_inc(S[k + "_kept"], 1)

            def a_Yi(b):
                at(pool, "a_Vi", b, 1, 1)
                if at_first(b):
                    pool.wait_ge(i_dve, 22)
                ago(pool, "a_full", b, 7, 9)
                for blk in range(2):
                    Gp.tensor_tensor(out=pr[2][:, blk, :], in0=Kr[:, blk, :], in1=Vi[:, 0, :], op=ALU.mult)
                    last = Gp.tensor_tensor(out=pr[3][:, blk, :], in0=Ki[:, blk, :], in1=Vr[:, 0, :], op=ALU.mult)
                last.then_inc(S["a_pool2"], 1)
                at(pool, "a_pool2", b, 1, 4)
                Gp.tensor_tensor(out=Yi[:, :, :], in0=pr[2][:, :, :], in1=pr[3][:, :, :], op=ALU.add)\
                    .then_inc(S["a_pool2"], 1)
                at(pool, "a_pool2", b, 2, 4)
                Gp.tensor_tensor(out=pr[2][:, 0, :], in0=Kr[:, 0, :], in1=Vi[:, 1, :], op=ALU.mult)
                Gp.tensor_tensor(out=pr[3][:, 0, :], in0=Ki[:, 0, :], in1=Vr[:, 1, :], op=ALU.mult)\
                    .then_inc(S["a_pool2"], 1)
                at(pool, "a_pool2", b, 3, 4)
                Gp.tensor_tensor(out=Yi[:, 1, :], in0=Yi[:, 1, :], in1=pr[2][:, 0, :], op=ALU.add)\
                    .then_inc(S["a_pool2"], 1)
                at(pool, "a_pool2", b, 4, 4)
                Gp.tensor_tensor(out=Yi[:, 1, :], in0=Yi[:, 1, :], in1=pr[3][:, 0, :], op=ALU.add)\
                    .then_inc(S["a_Yi"], 1)

            def a_rows(b):
                keep("A", b, lnA)

            def b_rows(b):
                keep("B", b, lnB)

            def c_rs(b):
                at(pool, "c_ms", b, 1, 1)
                ago(pool, "c_q", b, 2, 2)
                for t in range(LT):
                    last = Gp.tensor_tensor(out=rs[:, t, :], in0=ms[:, t, :], in1=rms_eps[:, :], op=ALU.add)
                last.then_inc(S["c_pool"], 1)
                at(pool, "c_pool", b, 1, 2)
                for t in range(LT):
                    Gp.tensor_tensor(out=rs[:, t, :], in0=rs[:, t, :], in1=mhalf[:, :], op=ALU.pow)\
                        .then_inc(S["c_rs"], 1)

            def c_rows(b):
                at(pool, "c_ssum", b, 1, 1)
                ago(pool, "c_wod", b, 1, 1)
                Gp.tensor_tensor(out=rms[:, :], in0=ssq[:, :], in1=rms_eps[:, 0:LT], op=ALU.add)\
                    .then_inc(S["c_pool"], 1)
                at(pool, "c_pool", b, 2, 2)
                Gp.tensor_tensor(out=rms[:, :], in0=rms[:, :], in1=mhalf[:, 0:LT], op=ALU.pow).then_inc(S["c_rms"], 1)

            def r_rows(b):
                keep("R", b, lnC)

            def c_before(b):
                at(pool, "c_pos", b, 1, 1)
                Gp.tensor_tensor(out=before[:, :], in0=before[:, :], in1=picked[:, 0, :], op=ALU.add)\
                    .then_inc(S["c_cnt"], 1)
                at(pool, "c_cnt", b, 1, 1)
                Gp.tensor_tensor(out=before[:, :], in0=before[:, :], in1=picked[:, 1, :], op=ALU.add)\
                    .then_inc(S["c_before"], 1)

            def d_hlo(b, j):
                at(pool, "d_hh", b, j + 1, TILES)
                n = units(j)
                Gp.tensor_tensor(out=hlo[0:n, slot(j), :], in0=dh[0:n, slot(j), :],
                                 in1=hhi[0:n, slot(j), :].bitcast(F32), op=ALU.subtract).then_inc(S["d_hl"], 1)

            steps = {"A.imag": a_Yi, "A.ln1": lambda b: rstd_of("A", b), "A.ln2": a_rows,
                     "B.ln1": lambda b: rstd_of("B", b), "B.ln2": b_rows, "C.qv": c_rs, "C.square": c_rows,
                     "R.ln1": lambda b: rstd_of("R", b), "R.ln2": r_rows, "R.pos": c_before}
            steps.update({f"D.{j}": lambda _, j=j: d_hlo(0, j) for j in range(EARLY)})
            steps["F.5"] = lambda _: with_bias(range(LT))
            layers(pool, steps, lambda: with_bias(range(LT, NB * LT)))

            def d_power(b):
                at(pool, "d_var", b, 1, 1)
                Gp.tensor_tensor(out=rstd["D"][:, :], in0=mv["D"][:, :, 1], in1=ln_eps[:, :], op=ALU.add)\
                    .then_inc(S["d_pool"], 1)
                at(pool, "d_pool", b, 1, 1)
                Gp.tensor_tensor(out=rstd["D"][:, :], in0=rstd["D"][:, :], in1=mhalf[:, 0:LT], op=ALU.pow)\
                    .then_inc(S["d_rstd"], 1)

            def d_pool(b):
                if not at_first(b):
                    d_hlo(b - 1, ET)
                for j in range(ET):
                    if not early(b, j):
                        d_hlo(b, j)
                    routing(steps, b, j)
                    if j == 2 and not at_first(b):
                        d_power(b - 1)

            each_batch(pool, d_pool)
            d_hlo(NB - 1, ET)
            d_power(NB - 1)


def kernel(**inputs):
    import math
    import numpy as np
    import concourse.bacc as bacc
    from concourse.bass_utils import run_bass_kernel_spmd

    nc = bacc.Bacc("TRN2", target_bir_lowering=False, num_devices=1)
    v = {n: np.asarray(a) for n, a in inputs.items()}

    def rows(a):
        return a.reshape(-1, P, a.shape[-1]).transpose(1, 0, 2)

    wo = v["L1_attn_Wo"].reshape(HKV, 2, 2, DH, D).transpose(0, 3, 2, 1, 4).reshape(HKV, DH, G, D)
    wo_pad = np.zeros((HKV, 32, G, D), wo.dtype)
    wo_pad[:, :DH] = wo
    up = v["L1_ffn_w_up"]
    n = np.arange(P)
    wexp = np.zeros((ET + 1, P, EW), up.dtype)
    for q, part in enumerate((up[:, :, :EH], up[:, :, EH:])):
        a = part.reshape(ET, EPT, DT, P, EH).transpose(0, 3, 2, 1, 4)
        wexp[:ET, :, q * D:(q + 1) * D] = a.reshape(ET, P, D)
    wexp[:ET, :, 2 * D:3 * D] = v["L1_ffn_w_down"].reshape(ET, P, D)
    wexp[:ET, :, 3 * D:] = n[None, :, None] % E == EPT * np.arange(ET)[:, None, None] + n[None, None, :] // EH
    shared = v["L1_ffn_w_shared_up"].reshape(DT, P, 2, HS)
    for c in range(DT):
        for q in range(2):
            wexp[ET, :, c * P + q * HS:c * P + (q + 1) * HS] = shared[c, :, 1 - q]
    wexp[ET, :HS, 2 * D:3 * D] = v["L1_ffn_w_shared_down"]
    x = v["L0_attn_x"].reshape(TOK, D)
    laid = {
        "x": rows(x), "xT": rows(x.T),
        "w_in": rows(v["L0_attn_in_proj_w"].T),
        "conv": np.concatenate([v["L0_attn_in_proj_b"].reshape(CH, P).T] +
                               [v["L0_attn_short_w"].reshape(CH, P, 3)[:, :, k].T for k in range(3)] +
                               [v["L0_attn_short_b"].reshape(CH, P).T], axis=1),
        "w_out": rows(v["L0_attn_out_proj_w"].T), "b_out": np.broadcast_to(v["L0_attn_out_proj_b"], (P, D)),
        "w1": rows(v["L0_ffn_W1"].T), "w3": rows(v["L0_ffn_W3"].T), "w2": rows(v["L0_ffn_W2"].T),
        "wqv": rows(np.concatenate([v["L1_attn_Wq"], v["L1_attn_Wv"]], axis=1)),
        "wo": wo_pad.reshape(P, G, D), "wgate": rows(v["L1_ffn_w_gate"]),
        "wexp": wexp,
    }

    t, k = np.arange(P, dtype=np.float64), np.arange(P, dtype=np.float64) + 0.5
    angle = 2 * np.pi / L * t[:, None] * k[None, :]
    wide = 2 * np.pi / L * (t[:, None] - P) * k[None, :]
    n = np.arange(P)
    had = np.ones((1, 1))
    while had.shape[0] < P:
        had = np.block([[had, had], [had, -had]])
    square = {
        "cos_t": np.cos(angle), "msin_t": -np.sin(angle), "cos_w": np.cos(wide),
        "msin_w": -np.sin(wide), "icos": np.cos(angle).T / P, "imsin": -np.sin(angle).T / P,
        "sumsel": (n[:, None] % 32 == DH) & (n[:, None] // 32 == n[None, :]),
        "tri": n[:, None] < n[None, :],
        "had": had / (2 * math.sqrt(HID)),
    }
    pos = np.linspace(0.0, 1.0, L, dtype=np.float32)
    ang = np.float32(0.0001) * (np.float32(2 * math.pi) * np.linspace(0.0, L - 1.0, L, dtype=np.float32) / L)
    deltas = np.abs(np.linspace(math.log(0.01) / 1.5, math.log(0.01) / 0.3, D, dtype=np.float32))
    laid["ident_in"] = np.eye(P, dtype=np.float32)
    laid["mats"] = np.stack([square[m] for m in MATS], axis=1).astype(np.float32)
    mlp = np.zeros((FO, MLP_COLS[-1]), np.float32)
    starts = (0,) + MLP_COLS[:-1]
    for a, part in zip(starts, (v["L0_attn_mlp_w0"].T, v["L0_attn_mlp_w1"].T, v["L0_attn_mlp_w2"].T,
                                v["L0_attn_mlp_w3"].T)):
        mlp[:part.shape[0], a:a + part.shape[1]] = part
    for c, name in enumerate(("mlp_b0", "mlp_b1", "mlp_b2")):
        mlp[:, starts[4] + c] = v["L0_attn_" + name]
    mlp[:, starts[4] + 3] = v["L0_attn_sin_freq"].reshape(-1)
    mlp[0:3, starts[5]:MLP_COLS[5]] = np.stack([pos, np.cos(ang), -np.sin(ang)])
    mlp[0, starts[6]:] = v["L0_attn_filter_bias"]
    laid["mlp"] = mlp
    laid["decay"] = rows(np.exp(-pos[:, None] * deltas[None, :]).astype(np.float32))
    order = ["x", "xT", "w_in", "conv", "mlp", "w_out", "b_out", "w1", "w3", "w2", "wqv", "wo", "wgate", "ident_in",
             "mats", "decay", "wexp"]
    arrays, args = {}, []
    for name in order:
        a = np.ascontiguousarray(laid[name])
        arrays["in_" + name] = a
        args.append(nc.dram_tensor("in_" + name, a.shape, mybir.dt.from_np(a.dtype), kind="ExternalInput").ap())
    out = nc.dram_tensor("out_0", (TOK, D), F32, kind="ExternalOutput").ap()
    mixed_kernel(nc, *args, out.rearrange("(t p) d -> p t d", p=P))
    r = run_bass_kernel_spmd(nc, [arrays], core_ids=[0])
    return r.results[0]["out_0"].reshape(NB, L, D)
```
